# Optimizing a Trainium2 kernel written in Bass

```python
import numpy as np
import jax
import jax.numpy as jnp

def _softmax(x, axis=-1):
    return jax.nn.softmax(x, axis=axis)

def _gelu(x):
    return jax.nn.gelu(x, approximate=True)

def _silu(x):
    return jax.nn.silu(x)

def _sigmoid(x):
    return jax.nn.sigmoid(x)

def _layernorm(x, axis=-1, eps=1e-05):
    m = jnp.mean(x, axis=axis, keepdims=True)
    v = jnp.var(x, axis=axis, keepdims=True)
    return (x - m) / jnp.sqrt(v + eps)

def _scatter_add(tgt, idx, src, axis=0):
    return tgt.at[idx].add(src)

def _segment_sum(src, seg, n):
    return jax.ops.segment_sum(src, seg, n)
kernel_name = 'mk_flamingo_gated_d4_seqx_r4_91f632'

def setup_inputs(seed: int=0):
    np.random.seed(seed)
    _w = jnp.asarray

    def _rec_inputs():
        import jax
        import jax.numpy as jnp
        _rk = jax.random.key(seed)
        x = 7.22e-05 + 1 * jax.random.normal(jax.random.fold_in(_rk, 1), (8, 256, 256), jnp.float32)
        _lenS = 256 - jax.random.randint(jax.random.fold_in(_rk, 7), (8,), 0, max(1, 256 // 4) + 1, jnp.int32)
        _lenS2 = 77 - jax.random.randint(jax.random.fold_in(_rk, 8), (8,), 0, max(1, 77 // 4) + 1, jnp.int32)
        _ctx_768P = jax.random.normal(jax.random.fold_in(_rk, 11), (8, 16, 192), jnp.float32)
        _ctx_768c = jax.random.dirichlet(jax.random.fold_in(_rk, 511), 0.3 * jnp.ones((16,), jnp.float32), (8, 77))
        _ctx_768t = jnp.einsum('bsk,bkd->bsd', _ctx_768c, _ctx_768P)
        _ctx_768t = _ctx_768t * jax.lax.rsqrt(jnp.mean(jnp.square(_ctx_768t)) + 1e-12) * 0.953939
        ctx_768 = 3.88148e-05 + 0.999967 * (_ctx_768t + 0.3 * jax.random.normal(jax.random.fold_in(_rk, 611), (8, 77, 192), jnp.float32))
        _validS = jnp.arange(256)[None, :] < _lenS[:, None]
        _validS2 = jnp.arange(77)[None, :] < _lenS2[:, None]
        _causal = jnp.tril(jnp.ones((256, 256), dtype=bool))
        mask_BxS_bf1 = jnp.ones((8, 256), dtype=bool)
        mask_BxS2_bf1 = jnp.ones((8, 77), dtype=bool)
        mask_BxS_bk0 = jnp.logical_not(jnp.broadcast_to(_validS[:, :], (8, 256)))
        _g = jax.random.normal(jax.random.fold_in(_rk, 9001), (2, 4), jnp.float32)
        _g = jnp.sign(_g) * jnp.maximum(jnp.abs(_g), 1.0) + (_g == 0) * 1.0
        g_xattn = _g[0]
        g_ffn = _g[1]
        return (x, ctx_768, mask_BxS_bf1, mask_BxS2_bf1, mask_BxS_bk0, g_xattn, g_ffn)
    x, ctx_768, mask_BxS_bf1, mask_BxS2_bf1, mask_BxS_bk0, g_xattn, g_ffn = _rec_inputs()

    def _L0_xattn_setup():
        import jax, jax.numpy as jnp
        import numpy as np
        B, T, DT, G, DV = (16, 128, 256, 144, 192)
        H, DH = (4, 32)
        INNER = H * DH
        HID = 4 * DT
        N_STATE = 64
        K_TOP = 32

        def layernorm(x, g, b, eps=1e-05):
            m = x.mean(-1, keepdims=True)
            v = x.var(-1, keepdims=True)
            return (x - m) * jax.lax.rsqrt(v + eps) * g + b

        def s4d(x, log_dt, A_re, A_im, C_re, C_im, D_skip):
            Bb, L, D = x.shape
            dt = jnp.exp(log_dt)
            A = A_re + 1j * A_im
            C = C_re + 1j * C_im
            dtA = dt[:, None] * A
            dC = C * (jnp.exp(dtA) - 1.0) / A
            powers = jnp.exp(dtA[:, :, None] * jnp.arange(L))
            K = 2.0 * jnp.einsum('dn,dnl->dl', dC, powers).real
            n = 2 * L
            Kf = jnp.fft.rfft(K, n=n, axis=-1)
            xf = jnp.fft.rfft(x, n=n, axis=1)
            y = jnp.fft.irfft(xf * Kf.T[None], n=n, axis=1)[:, :L]
            return y + x * D_skip
        key = jax.random.key(seed)
        ks = jax.random.split(key, 16)
        s = 0.02
        inp = {'x_text': jax.random.normal(ks[0], (B, T, DT), jnp.float32), 'x_vision': jax.random.normal(ks[1], (B, G, DV), jnp.float32), 'text_mask': jnp.ones((B, T), bool), 'vision_mask': jnp.ones((B, G), bool), 'Wq': jax.random.normal(ks[2], (DT, INNER), jnp.float32) * s, 'Wk': jax.random.normal(ks[3], (DV, INNER), jnp.float32) * s, 'Wv': jax.random.normal(ks[4], (DV, DT), jnp.float32) * s, 'W_film_in': jax.random.normal(ks[5], (DT, 2 * DT), jnp.float32) * s, 'b_film_in': jnp.zeros((2 * DT,), jnp.float32), 'W_film_out': jax.random.normal(ks[6], (DT, 2 * DT), jnp.float32) * s, 'b_film_out': jnp.zeros((2 * DT,), jnp.float32), 'g_norm_in': jnp.ones((DT,), jnp.float32), 'b_norm_in': jnp.zeros((DT,), jnp.float32), 'g_norm_out': jnp.ones((DT,), jnp.float32), 'b_norm_out': jnp.zeros((DT,), jnp.float32), 'g_ffn': jnp.ones((DT,), jnp.float32), 'b_ffn': jnp.zeros((DT,), jnp.float32), 'W1': jax.random.normal(ks[7], (DT, HID), jnp.float32) * s, 'b1': jnp.zeros((HID,), jnp.float32), 'W2': jax.random.normal(ks[8], (HID, DT), jnp.float32) * s, 'b2': jnp.zeros((DT,), jnp.float32), 'log_dt': jnp.log(0.001) + jax.random.uniform(ks[9], (DT,), jnp.float32) * (jnp.log(0.1) - jnp.log(0.001)), 'A_re': -0.5 * jnp.ones((DT, N_STATE), jnp.float32), 'A_im': jnp.tile(jnp.pi * jnp.arange(N_STATE, dtype=jnp.float32), (DT, 1)), 'C_re': jax.random.normal(ks[10], (DT, N_STATE), jnp.float32) * 0.5 ** 0.5, 'C_im': jax.random.normal(ks[11], (DT, N_STATE), jnp.float32) * 0.5 ** 0.5, 'D_skip': jax.random.normal(ks[12], (DT,), jnp.float32), 'mod_gate': jnp.array(0.5, jnp.float32)}
        return inp
    _L0_xattn_all = _L0_xattn_setup()
    _L0_xattn_in = {k: v for k, v in _L0_xattn_all.items() if k in ('Wq', 'Wk', 'Wv', 'W_film_in', 'b_film_in', 'W_film_out', 'b_film_out', 'g_norm_in', 'b_norm_in', 'g_norm_out', 'b_norm_out', 'g_ffn', 'b_ffn', 'W1', 'b1', 'W2', 'b2', 'log_dt', 'A_re', 'A_im', 'C_re', 'C_im', 'D_skip', 'mod_gate')}
    del _L0_xattn_all

    def _L0_ffn_setup():
        import jax, jax.numpy as jnp
        import numpy as np
        HIDDEN = 256
        NUM_EXPERTS = 8
        TOP_K = 2
        B, S = (2, 512)
        key = jax.random.key(seed)
        k1, k2, k3, k4, k5 = jax.random.split(key, 5)
        d, dff, E = (HIDDEN, 4 * HIDDEN, NUM_EXPERTS)
        x = jax.random.normal(k1, (B, S, d), dtype=jnp.float32)
        W1 = jax.random.normal(k2, (E, d, dff), dtype=jnp.float32) * (1.0 / np.sqrt(d))
        b1 = jax.random.normal(k3, (E, dff), dtype=jnp.float32) * 0.01
        W2 = jax.random.normal(k4, (E, dff, d), dtype=jnp.float32) * (1.0 / np.sqrt(dff))
        b2 = jax.random.normal(k5, (E, d), dtype=jnp.float32) * 0.01
        return {'x': x, 'W1': W1, 'b1': b1, 'W2': W2, 'b2': b2}
    _L0_ffn_all = _L0_ffn_setup()
    _L0_ffn_in = {k: v for k, v in _L0_ffn_all.items() if k in ('W1', 'b1', 'W2', 'b2')}
    del _L0_ffn_all

    def _L1_xattn_setup():
        import jax, jax.numpy as jnp
        import numpy as np
        NUM_HEADS = 8
        DIM_HEAD = 128
        SCALE = DIM_HEAD ** (-0.25)
        key = jax.random.key(seed)
        ks = jax.random.split(key, 7)
        B, Tq, Dq = (8, 1024, 256)
        Tk, Dc = (256, 192)
        inner = NUM_HEADS * DIM_HEAD
        s = lambda d: 1.0 / np.sqrt(d)
        return {'x': jax.random.normal(ks[0], (B, Tq, Dq), jnp.float32), 'context': jax.random.normal(ks[1], (B, Tk, Dc), jnp.float32), 'Wq': jax.random.normal(ks[2], (Dq, inner), jnp.float32) * s(Dq), 'Wk': jax.random.normal(ks[3], (Dc, inner), jnp.float32) * s(Dc), 'Wv': jax.random.normal(ks[4], (Dc, inner), jnp.float32) * s(Dc), 'Wo': jax.random.normal(ks[5], (inner, Dq), jnp.float32) * s(inner), 'bo': jnp.zeros((Dq,), jnp.float32)}
    _L1_xattn_all = _L1_xattn_setup()
    _L1_xattn_in = {k: v for k, v in _L1_xattn_all.items() if k in ('Wq', 'Wk', 'Wv', 'Wo', 'bo')}
    del _L1_xattn_all

    def _L1_ffn_setup():
        import jax, jax.numpy as jnp
        import numpy as np
        EPS = 1e-05
        LN_EPS = 1e-05
        NUM_EXPERTS = 8
        TOP_K = 2
        HIDDEN = 256
        INTER = 512

        def _swiglu(x, wg, wu, wd):
            return jax.nn.silu(x @ wg) * (x @ wu) @ wd
        key = jax.random.key(seed)
        ks = jax.random.split(key, 10)
        B, S, H, I, E = (8, 1024, HIDDEN, INTER, NUM_EXPERTS)
        std_h = 1.0 / np.sqrt(H)
        std_i = 1.0 / np.sqrt(I)
        return {'x': jax.random.normal(ks[0], (B, S, H), dtype=jnp.float32), 'ln_scale': jnp.ones((H,), dtype=jnp.float32), 'ln_bias': jnp.zeros((H,), dtype=jnp.float32), 'gate_w': jax.random.normal(ks[1], (E, H), dtype=jnp.float32) * 0.01, 'Wg': jax.random.normal(ks[2], (E, H, I), dtype=jnp.float32) * std_h, 'Wu': jax.random.normal(ks[3], (E, H, I), dtype=jnp.float32) * std_h, 'Wd': jax.random.normal(ks[4], (E, I, H), dtype=jnp.float32) * std_i, 'sWg': jax.random.normal(ks[5], (H, I), dtype=jnp.float32) * std_h, 'sWu': jax.random.normal(ks[6], (H, I), dtype=jnp.float32) * std_h, 'sWd': jax.random.normal(ks[7], (I, H), dtype=jnp.float32) * std_i}
    _L1_ffn_all = _L1_ffn_setup()
    _L1_ffn_in = {k: v for k, v in _L1_ffn_all.items() if k in ('ln_scale', 'ln_bias', 'gate_w', 'Wg', 'Wu', 'Wd', 'sWg', 'sWu', 'sWd')}
    del _L1_ffn_all

    def _L2_xattn_setup():
        import jax, jax.numpy as jnp
        import numpy as np
        NUM_HEADS = 16
        CLAMP = 10000.0
        key = jax.random.key(seed)
        ks = jax.random.split(key, 8)
        B, Nq, Nkv, Cq, Ckv = (4, 512, 512, 256, 192)
        s_q = 1.0 / np.sqrt(Cq)
        s_kv = 1.0 / np.sqrt(Ckv)
        return {'query': jax.random.normal(ks[0], (B, Nq, Cq), jnp.float32), 'key_value': jax.random.normal(ks[1], (B, Nkv, Ckv), jnp.float32), 'Wq': jax.random.normal(ks[2], (Cq, Cq), jnp.float32) * s_q, 'bq': jnp.zeros((Cq,), jnp.float32), 'Wk': jax.random.normal(ks[3], (Ckv, Cq), jnp.float32) * s_kv, 'bk': jnp.zeros((Cq,), jnp.float32), 'Wv': jax.random.normal(ks[4], (Ckv, Cq), jnp.float32) * s_kv, 'bv': jnp.zeros((Cq,), jnp.float32), 'Wo': jax.random.normal(ks[5], (Cq, Cq), jnp.float32) * s_q, 'bo': jnp.zeros((Cq,), jnp.float32)}
    _L2_xattn_all = _L2_xattn_setup()
    _L2_xattn_in = {k: v for k, v in _L2_xattn_all.items() if k in ('Wq', 'bq', 'Wk', 'bk', 'Wv', 'bv', 'Wo', 'bo')}
    del _L2_xattn_all

    def _L2_ffn_setup():
        import jax, jax.numpy as jnp
        import numpy as np
        E = 8
        D = 256
        DO = 256
        R = 64
        H = 64
        B, T = (8, 512)
        key = jax.random.key(seed)
        ks = jax.random.split(key, 12)
        s = lambda k, shape, fan: jax.random.normal(k, shape, jnp.float32) / np.sqrt(fan)
        return {'x': jax.random.normal(ks[0], (B, T, D), jnp.float32), 'W_base': s(ks[1], (D, DO), D), 'b_base': jnp.zeros((DO,), jnp.float32), 'Wd1': s(ks[2], (E, D, H), D), 'bd1': jnp.zeros((E, H), jnp.float32), 'Wd2': s(ks[3], (E, H, D), H), 'bd2': jnp.zeros((E, D), jnp.float32), 'Wa_down': s(ks[4], (E, D, R), D), 'ba_down': jnp.zeros((E, R), jnp.float32), 'Wa_up': s(ks[5], (E, R, DO), R), 'ba_up': jnp.zeros((E, DO), jnp.float32)}
    _L2_ffn_all = _L2_ffn_setup()
    _L2_ffn_in = {k: v for k, v in _L2_ffn_all.items() if k in ('W_base', 'b_base', 'Wd1', 'bd1', 'Wd2', 'bd2', 'Wa_down', 'ba_down', 'Wa_up', 'ba_up')}
    del _L2_ffn_all

    def _L3_xattn_setup():
        import jax, jax.numpy as jnp
        import numpy as np
        NUM_HEADS = 16
        key = jax.random.key(seed)
        k1, k2, k3, k4, k5 = jax.random.split(key, 5)
        B, N, C = (4, 512, 256)
        N2, Cy = (256, 192)
        x = jax.random.normal(k1, (B, N, C), dtype=jnp.float32)
        y = jax.random.normal(k2, (B, N2, Cy), dtype=jnp.float32)
        pad_mask = jax.random.randint(k3, (B, N), 0, 2).astype(jnp.bool_)
        Wq = jax.random.normal(k4, (C, C), dtype=jnp.float32) * C ** (-0.5)
        Wkv = jax.random.normal(k5, (2 * C, Cy), dtype=jnp.float32) * Cy ** (-0.5)
        return {'x': x, 'y': y, 'pad_mask': pad_mask, 'Wq': Wq, 'Wkv': Wkv}
    _L3_xattn_all = _L3_xattn_setup()
    _L3_xattn_in = {k: v for k, v in _L3_xattn_all.items() if k in ('Wq', 'Wkv')}
    del _L3_xattn_all

    def _L3_ffn_setup():
        import jax, jax.numpy as jnp
        import numpy as np
        B, S, D = (2, 512, 256)
        E, K, F = (16, 2, 128)
        FS = 256
        key = jax.random.key(seed)
        ks = jax.random.split(key, 8)

        def w(k, shape, fan_in):
            return jax.random.normal(k, shape, jnp.float32) / np.sqrt(fan_in).astype(np.float32)
        return {'x': jax.random.normal(ks[0], (B, S, D), jnp.float32), 'Wr': w(ks[1], (D, E), D), 'Wg': w(ks[2], (E, D, F), D), 'Wu': w(ks[3], (E, D, F), D), 'Wd': w(ks[4], (E, F, D), F), 'Sg': w(ks[5], (D, FS), D), 'Su': w(ks[6], (D, FS), D), 'Sd': w(ks[7], (FS, D), FS)}
    _L3_ffn_all = _L3_ffn_setup()
    _L3_ffn_in = {k: v for k, v in _L3_ffn_all.items() if k in ('Wr', 'Wg', 'Wu', 'Wd', 'Sg', 'Su', 'Sd')}
    del _L3_ffn_all
    return {'x': x, 'ctx_768': ctx_768, 'mask_BxS_bf1': mask_BxS_bf1, 'mask_BxS2_bf1': mask_BxS2_bf1, 'mask_BxS_bk0': mask_BxS_bk0, 'g_xattn': g_xattn, 'g_ffn': g_ffn, 'L0_xattn_Wq': _L0_xattn_in['Wq'], 'L0_xattn_Wk': _L0_xattn_in['Wk'], 'L0_xattn_Wv': _L0_xattn_in['Wv'], 'L0_xattn_W_film_in': _L0_xattn_in['W_film_in'], 'L0_xattn_b_film_in': _L0_xattn_in['b_film_in'], 'L0_xattn_W_film_out': _L0_xattn_in['W_film_out'], 'L0_xattn_b_film_out': _L0_xattn_in['b_film_out'], 'L0_xattn_g_norm_in': _L0_xattn_in['g_norm_in'], 'L0_xattn_b_norm_in': _L0_xattn_in['b_norm_in'], 'L0_xattn_g_norm_out': _L0_xattn_in['g_norm_out'], 'L0_xattn_b_norm_out': _L0_xattn_in['b_norm_out'], 'L0_xattn_g_ffn': _L0_xattn_in['g_ffn'], 'L0_xattn_b_ffn': _L0_xattn_in['b_ffn'], 'L0_xattn_W1': _L0_xattn_in['W1'], 'L0_xattn_b1': _L0_xattn_in['b1'], 'L0_xattn_W2': _L0_xattn_in['W2'], 'L0_xattn_b2': _L0_xattn_in['b2'], 'L0_xattn_log_dt': _L0_xattn_in['log_dt'], 'L0_xattn_A_re': _L0_xattn_in['A_re'], 'L0_xattn_A_im': _L0_xattn_in['A_im'], 'L0_xattn_C_re': _L0_xattn_in['C_re'], 'L0_xattn_C_im': _L0_xattn_in['C_im'], 'L0_xattn_D_skip': _L0_xattn_in['D_skip'], 'L0_xattn_mod_gate': _L0_xattn_in['mod_gate'], 'L0_ffn_W1': _L0_ffn_in['W1'], 'L0_ffn_b1': _L0_ffn_in['b1'], 'L0_ffn_W2': _L0_ffn_in['W2'], 'L0_ffn_b2': _L0_ffn_in['b2'], 'L1_xattn_Wq': _L1_xattn_in['Wq'], 'L1_xattn_Wk': _L1_xattn_in['Wk'], 'L1_xattn_Wv': _L1_xattn_in['Wv'], 'L1_xattn_Wo': _L1_xattn_in['Wo'], 'L1_xattn_bo': _L1_xattn_in['bo'], 'L1_ffn_ln_scale': _L1_ffn_in['ln_scale'], 'L1_ffn_ln_bias': _L1_ffn_in['ln_bias'], 'L1_ffn_gate_w': _L1_ffn_in['gate_w'], 'L1_ffn_Wg': _L1_ffn_in['Wg'], 'L1_ffn_Wu': _L1_ffn_in['Wu'], 'L1_ffn_Wd': _L1_ffn_in['Wd'], 'L1_ffn_sWg': _L1_ffn_in['sWg'], 'L1_ffn_sWu': _L1_ffn_in['sWu'], 'L1_ffn_sWd': _L1_ffn_in['sWd'], 'L2_xattn_Wq': _L2_xattn_in['Wq'], 'L2_xattn_bq': _L2_xattn_in['bq'], 'L2_xattn_Wk': _L2_xattn_in['Wk'], 'L2_xattn_bk': _L2_xattn_in['bk'], 'L2_xattn_Wv': _L2_xattn_in['Wv'], 'L2_xattn_bv': _L2_xattn_in['bv'], 'L2_xattn_Wo': _L2_xattn_in['Wo'], 'L2_xattn_bo': _L2_xattn_in['bo'], 'L2_ffn_W_base': _L2_ffn_in['W_base'], 'L2_ffn_b_base': _L2_ffn_in['b_base'], 'L2_ffn_Wd1': _L2_ffn_in['Wd1'], 'L2_ffn_bd1': _L2_ffn_in['bd1'], 'L2_ffn_Wd2': _L2_ffn_in['Wd2'], 'L2_ffn_bd2': _L2_ffn_in['bd2'], 'L2_ffn_Wa_down': _L2_ffn_in['Wa_down'], 'L2_ffn_ba_down': _L2_ffn_in['ba_down'], 'L2_ffn_Wa_up': _L2_ffn_in['Wa_up'], 'L2_ffn_ba_up': _L2_ffn_in['ba_up'], 'L3_xattn_Wq': _L3_xattn_in['Wq'], 'L3_xattn_Wkv': _L3_xattn_in['Wkv'], 'L3_ffn_Wr': _L3_ffn_in['Wr'], 'L3_ffn_Wg': _L3_ffn_in['Wg'], 'L3_ffn_Wu': _L3_ffn_in['Wu'], 'L3_ffn_Wd': _L3_ffn_in['Wd'], 'L3_ffn_Sg': _L3_ffn_in['Sg'], 'L3_ffn_Su': _L3_ffn_in['Su'], 'L3_ffn_Sd': _L3_ffn_in['Sd']}

def reference(x, ctx_768, mask_BxS_bf1, mask_BxS2_bf1, mask_BxS_bk0, g_xattn, g_ffn, L0_xattn_Wq, L0_xattn_Wk, L0_xattn_Wv, L0_xattn_W_film_in, L0_xattn_b_film_in, L0_xattn_W_film_out, L0_xattn_b_film_out, L0_xattn_g_norm_in, L0_xattn_b_norm_in, L0_xattn_g_norm_out, L0_xattn_b_norm_out, L0_xattn_g_ffn, L0_xattn_b_ffn, L0_xattn_W1, L0_xattn_b1, L0_xattn_W2, L0_xattn_b2, L0_xattn_log_dt, L0_xattn_A_re, L0_xattn_A_im, L0_xattn_C_re, L0_xattn_C_im, L0_xattn_D_skip, L0_xattn_mod_gate, L0_ffn_W1, L0_ffn_b1, L0_ffn_W2, L0_ffn_b2, L1_xattn_Wq, L1_xattn_Wk, L1_xattn_Wv, L1_xattn_Wo, L1_xattn_bo, L1_ffn_ln_scale, L1_ffn_ln_bias, L1_ffn_gate_w, L1_ffn_Wg, L1_ffn_Wu, L1_ffn_Wd, L1_ffn_sWg, L1_ffn_sWu, L1_ffn_sWd, L2_xattn_Wq, L2_xattn_bq, L2_xattn_Wk, L2_xattn_bk, L2_xattn_Wv, L2_xattn_bv, L2_xattn_Wo, L2_xattn_bo, L2_ffn_W_base, L2_ffn_b_base, L2_ffn_Wd1, L2_ffn_bd1, L2_ffn_Wd2, L2_ffn_bd2, L2_ffn_Wa_down, L2_ffn_ba_down, L2_ffn_Wa_up, L2_ffn_ba_up, L3_xattn_Wq, L3_xattn_Wkv, L3_ffn_Wr, L3_ffn_Wg, L3_ffn_Wu, L3_ffn_Wd, L3_ffn_Sg, L3_ffn_Su, L3_ffn_Sd):
    import jax
    import jax.numpy as jnp

    def _L0_xattn_ref(x_text, x_vision, text_mask, vision_mask, Wq, Wk, Wv, W_film_in, b_film_in, W_film_out, b_film_out, g_norm_in, b_norm_in, g_norm_out, b_norm_out, g_ffn, b_ffn, W1, b1, W2, b2, log_dt, A_re, A_im, C_re, C_im, D_skip, mod_gate):
        import jax, jax.numpy as jnp
        import numpy as np
        B, T, DT, G, DV = (16, 128, 256, 144, 192)
        H, DH = (4, 32)
        INNER = H * DH
        HID = 4 * DT
        N_STATE = 64
        K_TOP = 32

        def layernorm(x, g, b, eps=1e-05):
            m = x.mean(-1, keepdims=True)
            v = x.var(-1, keepdims=True)
            return (x - m) * jax.lax.rsqrt(v + eps) * g + b

        def s4d(x, log_dt, A_re, A_im, C_re, C_im, D_skip):
            Bb, L, D = x.shape
            dt = jnp.exp(log_dt)
            A = A_re + 1j * A_im
            C = C_re + 1j * C_im
            dtA = dt[:, None] * A
            dC = C * (jnp.exp(dtA) - 1.0) / A
            powers = jnp.exp(dtA[:, :, None] * jnp.arange(L))
            K = 2.0 * jnp.einsum('dn,dnl->dl', dC, powers).real
            n = 2 * L
            Kf = jnp.fft.rfft(K, n=n, axis=-1)
            xf = jnp.fft.rfft(x, n=n, axis=1)
            y = jnp.fft.irfft(xf * Kf.T[None], n=n, axis=1)[:, :L]
            return y + x * D_skip
        Bb, Tt, D = x_text.shape
        Gg = x_vision.shape[1]
        Q = (x_text @ Wq).reshape(Bb, Tt, H, DH)
        K = (x_vision @ Wk).reshape(Bb, Gg, H, DH)
        scores = jnp.einsum('bthd,bghd->bhtg', Q, K) / np.sqrt(DH).astype(np.float32)
        scores = jnp.where(vision_mask[:, None, None, :], scores, -jnp.inf)
        topv, topi = jax.lax.top_k(scores, K_TOP)
        probs = jax.nn.softmax(topv, axis=-1)
        bi = jnp.arange(Bb)[:, None, None, None]
        hi = jnp.arange(H)[None, :, None, None]
        ti = jnp.arange(Tt)[None, None, :, None]
        attn = jnp.zeros_like(scores).at[bi, hi, ti, topi].set(probs)
        attn_mean = attn.mean(axis=1)
        V = x_vision @ Wv
        c_t = jnp.einsum('btg,bgd->btd', attn_mean, V)
        c_t = c_t * text_mask[..., None]
        x = layernorm(x_text, g_norm_in, b_norm_in)
        scale_in, shift_in = jnp.split(c_t @ W_film_in + b_film_in, 2, axis=-1)
        x = x * (1.0 + mod_gate * scale_in) + mod_gate * shift_in
        y = s4d(x, log_dt, A_re, A_im, C_re, C_im, D_skip)
        scale_out, shift_out = jnp.split(c_t @ W_film_out + b_film_out, 2, axis=-1)
        y = y * (1.0 + mod_gate * scale_out) + mod_gate * shift_out
        xt = x_text + y
        h = layernorm(xt, g_ffn, b_ffn)
        h = jax.nn.gelu(h @ W1 + b1, approximate=False) @ W2 + b2
        xt = xt + h
        return layernorm(xt, g_norm_out, b_norm_out)

    def _L0_ffn_ref(x, W1, b1, W2, b2):
        import jax, jax.numpy as jnp
        import numpy as np
        HIDDEN = 256
        NUM_EXPERTS = 8
        TOP_K = 2
        B, S = (2, 512)
        Bm, Sm, d = x.shape
        E = W1.shape[0]
        x_flat = x.reshape(-1, d)
        h = jnp.mod(x_flat[:, :TOP_K].sum(axis=1).astype(jnp.int32), E)
        sel = jnp.stack([h, jnp.mod(h + 1, E)], axis=1)

        def step(acc, params):
            e, W1e, b1e, W2e, b2e = params
            w = jnp.any(sel == e, axis=1).astype(x.dtype) / TOP_K
            y = jnp.maximum(x_flat @ W1e + b1e, 0.0) @ W2e + b2e
            return (acc + w[:, None] * y, None)
        init = jnp.zeros_like(x_flat)
        out_flat, _ = jax.lax.scan(step, init, (jnp.arange(E), W1, b1, W2, b2))
        return out_flat.reshape(Bm, Sm, d)

    def _L1_xattn_ref(x, context, Wq, Wk, Wv, Wo, bo):
        import jax, jax.numpy as jnp
        import numpy as np
        NUM_HEADS = 8
        DIM_HEAD = 128
        SCALE = DIM_HEAD ** (-0.25)
        B, Tq, _ = x.shape
        Tk = context.shape[1]
        h, C = (NUM_HEADS, DIM_HEAD)
        q = (x @ Wq).reshape(B, Tq, h, C) * SCALE
        k = (context @ Wk).reshape(B, Tk, h, C) * SCALE
        v = (context @ Wv).reshape(B, Tk, h, C)
        attn = jax.nn.softmax(jnp.einsum('bqhc,bkhc->bhqk', q, k), axis=-1)
        out = jnp.einsum('bhqk,bkhc->bqhc', attn, v).reshape(B, Tq, h * C)
        return out @ Wo + bo

    def _L1_ffn_ref(x, ln_scale, ln_bias, gate_w, Wg, Wu, Wd, sWg, sWu, sWd):
        import jax, jax.numpy as jnp
        import numpy as np
        EPS = 1e-05
        LN_EPS = 1e-05
        NUM_EXPERTS = 8
        TOP_K = 2
        HIDDEN = 256
        INTER = 512

        def _swiglu(x, wg, wu, wd):
            return jax.nn.silu(x @ wg) * (x @ wu) @ wd
        B, S, H = x.shape
        xf = x.reshape(-1, H)
        mu = jnp.mean(xf, axis=-1, keepdims=True)
        var = jnp.var(xf, axis=-1, keepdims=True)
        xn = (xf - mu) * jax.lax.rsqrt(var + LN_EPS) * ln_scale + ln_bias
        logits = xn @ gate_w.T
        probs = jax.nn.softmax(logits, axis=-1)
        tk_probs, tk_idx = jax.lax.top_k(probs, TOP_K)
        tk_probs = tk_probs / (jnp.sum(tk_probs, axis=-1, keepdims=True) + EPS)
        onehot = tk_idx[..., None] == jnp.arange(NUM_EXPERTS)[None, None, :]
        w = jnp.sum(tk_probs[..., None] * onehot.astype(tk_probs.dtype), axis=1)
        out = _swiglu(xf, sWg, sWu, sWd)
        for e in range(NUM_EXPERTS):
            out = out + w[:, e:e + 1] * _swiglu(xf, Wg[e], Wu[e], Wd[e])
        return out.reshape(B, S, H)

    def _L2_xattn_ref(query, key_value, Wq, bq, Wk, bk, Wv, bv, Wo, bo):
        import jax, jax.numpy as jnp
        import numpy as np
        NUM_HEADS = 16
        CLAMP = 10000.0
        B, Nq, Cq = query.shape
        Nkv = key_value.shape[1]
        H = NUM_HEADS
        D = Cq // H
        scale = D ** (-0.5)
        q = (query @ Wq + bq).reshape(B, Nq, H, D).transpose(0, 2, 1, 3)
        k = (key_value @ Wk + bk).reshape(B, Nkv, H, D).transpose(0, 2, 1, 3)
        v = (key_value @ Wv + bv).reshape(B, Nkv, H, D).transpose(0, 2, 1, 3)
        attn = jnp.einsum('bhqd,bhkd->bhqk', q, k) * scale
        attn = jnp.clip(attn, -CLAMP, CLAMP)
        attn = jax.nn.softmax(attn, axis=-1)
        attn = jnp.where(jnp.any(jnp.isnan(attn)), jnp.asarray(1.0 / Nkv, attn.dtype), attn)
        x = jnp.einsum('bhqk,bhkd->bqhd', attn, v).reshape(B, Nq, Cq)
        return x @ Wo + bo

    def _L2_ffn_ref(x, W_base, b_base, Wd1, bd1, Wd2, bd2, Wa_down, ba_down, Wa_up, ba_up):
        import jax, jax.numpy as jnp
        import numpy as np
        E = 8
        D = 256
        DO = 256
        R = 64
        H = 64
        B, T = (8, 512)
        base = jnp.einsum('btd,do->bto', x, W_base) + b_base
        h = jax.nn.relu(jnp.einsum('btd,edh->ebth', x, Wd1) + bd1[:, None, None, :])
        recon = jnp.einsum('ebth,ehd->ebtd', h, Wd2) + bd2[:, None, None, :]
        losses = jnp.mean((recon - x[None]) ** 2, axis=(2, 3))
        idx = jnp.argmin(losses, axis=0)
        a = jax.nn.relu(jnp.einsum('btd,bdr->btr', x, Wa_down[idx]) + ba_down[idx][:, None, :])
        adapter_out = jnp.einsum('btr,bro->bto', a, Wa_up[idx]) + ba_up[idx][:, None, :]
        return base + adapter_out

    def _L3_xattn_ref(x, y, pad_mask, Wq, Wkv):
        import jax, jax.numpy as jnp
        import numpy as np
        NUM_HEADS = 16
        B, N, C = x.shape
        N2 = y.shape[1]
        H = NUM_HEADS
        d = C // H
        scale = d ** (-0.5)
        q = (x @ Wq.T).reshape(B, N, H, d).transpose(0, 2, 1, 3)
        kv = (y @ Wkv.T).reshape(B, N2, 2, H, d).transpose(2, 0, 3, 1, 4)
        k, v = (kv[0], kv[1])
        attn = jnp.einsum('bhnd,bhmd->bhnm', q * scale, k)
        attn = jnp.where(pad_mask[:, None, :, None], attn, jnp.float32(-1000000000.0))
        attn = jax.nn.softmax(attn, axis=-1)
        out = jnp.einsum('bhnm,bhmd->bhnd', attn, v)
        return out.transpose(0, 2, 1, 3).reshape(B, N, C)

    def _L3_ffn_ref(x, Wr, Wg, Wu, Wd, Sg, Su, Sd):
        import jax, jax.numpy as jnp
        import numpy as np
        B, S, D = (2, 512, 256)
        E, K, F = (16, 2, 128)
        FS = 256
        b, s, d = x.shape
        T = b * s
        xf = x.reshape(T, d)
        shared = jax.nn.silu(xf @ Sg) * (xf @ Su) @ Sd
        probs = jax.nn.softmax(xf @ Wr, axis=-1)
        topk_p, topk_i = jax.lax.top_k(probs, K)
        n_exp = Wr.shape[1]
        cw = jnp.zeros((T, n_exp), x.dtype).at[jnp.arange(T)[:, None], topk_i].add(topk_p)

        def step(acc, ew):
            wg, wu, wd, c = ew
            y = jax.nn.silu(xf @ wg) * (xf @ wu) @ wd
            return (acc + y * c[:, None], None)
        routed, _ = jax.lax.scan(step, jnp.zeros_like(xf), (Wg, Wu, Wd, cw.T))
        return (routed + shared).reshape(b, s, d)
    x = x + jnp.tanh(g_xattn[0]) * _L0_xattn_ref(_layernorm(x, axis=-1), ctx_768, mask_BxS_bf1, mask_BxS2_bf1, L0_xattn_Wq, L0_xattn_Wk, L0_xattn_Wv, L0_xattn_W_film_in, L0_xattn_b_film_in, L0_xattn_W_film_out, L0_xattn_b_film_out, L0_xattn_g_norm_in, L0_xattn_b_norm_in, L0_xattn_g_norm_out, L0_xattn_b_norm_out, L0_xattn_g_ffn, L0_xattn_b_ffn, L0_xattn_W1, L0_xattn_b1, L0_xattn_W2, L0_xattn_b2, L0_xattn_log_dt, L0_xattn_A_re, L0_xattn_A_im, L0_xattn_C_re, L0_xattn_C_im, L0_xattn_D_skip, L0_xattn_mod_gate)
    x = x + jnp.tanh(g_ffn[0]) * _L0_ffn_ref(_layernorm(x, axis=-1), L0_ffn_W1, L0_ffn_b1, L0_ffn_W2, L0_ffn_b2)
    x = x + jnp.tanh(g_xattn[1]) * _L1_xattn_ref(_layernorm(x, axis=-1), ctx_768, L1_xattn_Wq, L1_xattn_Wk, L1_xattn_Wv, L1_xattn_Wo, L1_xattn_bo)
    x = x + jnp.tanh(g_ffn[1]) * _L1_ffn_ref(_layernorm(x, axis=-1), L1_ffn_ln_scale, L1_ffn_ln_bias, L1_ffn_gate_w, L1_ffn_Wg, L1_ffn_Wu, L1_ffn_Wd, L1_ffn_sWg, L1_ffn_sWu, L1_ffn_sWd)
    x = x + jnp.tanh(g_xattn[2]) * _L2_xattn_ref(_layernorm(x, axis=-1), ctx_768, L2_xattn_Wq, L2_xattn_bq, L2_xattn_Wk, L2_xattn_bk, L2_xattn_Wv, L2_xattn_bv, L2_xattn_Wo, L2_xattn_bo)
    x = x + jnp.tanh(g_ffn[2]) * _L2_ffn_ref(_layernorm(x, axis=-1), L2_ffn_W_base, L2_ffn_b_base, L2_ffn_Wd1, L2_ffn_bd1, L2_ffn_Wd2, L2_ffn_bd2, L2_ffn_Wa_down, L2_ffn_ba_down, L2_ffn_Wa_up, L2_ffn_ba_up)
    x = x + jnp.tanh(g_xattn[3]) * _L3_xattn_ref(_layernorm(x, axis=-1), ctx_768, mask_BxS_bk0, L3_xattn_Wq, L3_xattn_Wkv)
    x = x + jnp.tanh(g_ffn[3]) * _L3_ffn_ref(_layernorm(x, axis=-1), L3_ffn_Wr, L3_ffn_Wg, L3_ffn_Wu, L3_ffn_Wd, L3_ffn_Sg, L3_ffn_Su, L3_ffn_Sd)
    return x

_drawn_inputs = setup_inputs


def setup_inputs(seed=0):
    import zlib

    import numpy as np

    out = dict(_drawn_inputs(seed))
    spreads = {'L0_xattn_b_film_in': (0.0, 0.1),
     'L0_xattn_b_film_out': (0.0, 0.1),
     'L0_xattn_g_norm_in': (1.0, 0.2),
     'L0_xattn_b_norm_in': (0.0, 0.1),
     'L0_xattn_g_norm_out': (1.0, 0.2),
     'L0_xattn_b_norm_out': (0.0, 0.1),
     'L0_xattn_g_ffn': (1.0, 0.6),
     'L0_xattn_b_ffn': (0.0, 0.592),
     'L0_xattn_b1': (0.0, 0.1),
     'L0_xattn_b2': (0.0, 0.1),
     'L0_xattn_A_re': (-0.5, 0.2),
     'L1_xattn_bo': (0.0, 0.1),
     'L1_ffn_ln_scale': (1.0, 0.2),
     'L1_ffn_ln_bias': (0.0, 0.1),
     'L2_xattn_bq': (0.0, 0.718),
     'L2_xattn_bk': (0.0, 2.0),
     'L2_xattn_bv': (0.0, 0.1),
     'L2_xattn_bo': (0.0, 0.1),
     'L2_ffn_b_base': (0.0, 0.1),
     'L2_ffn_bd1': (0.0, 0.1),
     'L2_ffn_bd2': (0.0, 0.1),
     'L2_ffn_ba_down': (0.0, 0.286),
     'L2_ffn_ba_up': (0.0, 0.1)}
    factors = {'L0_xattn_Wq': 10.606,
     'L0_xattn_Wk': 11.24,
     'L0_ffn_b1': 4.707,
     'L0_ffn_b2': 4.421,
     'g_ffn': 25.12}
    for name, (base, spread) in spreads.items():
        noise = np.random.default_rng([zlib.crc32(name.encode()), seed]).standard_normal(out[name].shape)
        drawn = base * np.exp(spread * noise) if base else spread * noise
        out[name] = jnp.asarray(drawn.astype(out[name].dtype))
    for name, factor in factors.items():
        out[name] = (out[name] * factor).astype(out[name].dtype)
    return out
```

```python
from contextlib import ExitStack

import numpy as np

import concourse.bass as bass
from concourse import mybir

F32 = mybir.dt.float32
I32 = mybir.dt.int32
U32 = mybir.dt.uint32
U8 = mybir.dt.uint8
ACT = mybir.ActivationFunctionType
ALU = mybir.AluOpType
AX = mybir.AxisListType

P = 128
BATCH, SEQ, DIM = 8, 256, 256
KEYS, CTX = 77, 192
CP = 96
CK = CTX // CP
DK = DIM // P
TILES = BATCH * SEQ // P
TOKENS = BATCH * SEQ
TPB = SEQ // P
EPS = 1e-5
BLOCK = 512
BLOCKS = TOKENS // BLOCK
TPK = BLOCK // P
MAGIC = 12582912.0
NEG = -3.0e38


def pieces(i, n=1):
    return bass.ds(i, n)


class Core:

    stages = 0

    def count(self):
        self.stages += 1
        return self.stages


def sub_memory(nc, ctx, prefix=""):
    def sb(name, shape, dt=F32):
        return ctx.enter_context(nc.sbuf_tensor(prefix + name, shape, dt))

    def ps(name, shape, dt=F32):
        return ctx.enter_context(nc.psum_tensor(prefix + name, shape, dt))

    def sem(name):
        handle = ctx.enter_context(nc.semaphore(prefix + name))
        ctx.callback(nc.sync.sem_clear, handle)
        return handle

    return sb, ps, sem


def row(ap):
    return ap.rearrange("(a n) -> a n", a=1)


def spread(ap):
    return ap.partition_broadcast(P)


def load_inputs(nc, c, a):
    with ExitStack() as ctx:
        sb, ps, sem = sub_memory(nc, ctx)
        gates = sb("gates", [P, 8])
        loaded, gates_done = sem("setup_loaded"), sem("setup_gates")
        block = ctx.enter_context(nc.Block())

        @block.sync
        def _(sp):
            sp.dma_start(gates[:, 0:4], spread(a["g_xattn"])).then_inc(loaded, 16)
            sp.dma_start(gates[:, 4:8], spread(a["g_ffn"])).then_inc(loaded, 16)
            sp.dma_start(c.X[:, :, :], a["x"].rearrange("b (i p) d -> p (b i) d", p=P)).then_inc(loaded, 16)
            sp.dma_start(c.ident[:, :], a["ident"]).then_inc(loaded, 16)
            sp.dma_start(c.headmask[:, :], a["headmask"]).then_inc(loaded, 16)
            sp.dma_start(c.iota8[:, :], a["iota8"]).then_inc(loaded, 16)

        @block.scalar
        def _(act):
            act.wait_ge(loaded, 96)
            nc.scalar.activation(c.gate[:, :], gates[:, :], ACT.Tanh).then_inc(gates_done, 1)
            act.wait_ge(gates_done, 1)


def normalise(nc, c, source, natural=None, transposed=True, gain=None, shift=None, add=None, store=None):
    with ExitStack() as ctx:
        sb, ps, sem = sub_memory(nc, ctx, f"n{c.count()}_")
        stats = sb("ln_stats", [P, TILES, 6])
        mean = sb("ln_mean", [P, TILES])
        diff = sb("ln_diff", [P, TILES])
        var = sb("ln_var", [P, TILES])
        dev = sb("ln_dev", [P, TILES])
        rstd = sb("ln_rstd", [P, TILES])
        scratch = sb("ln_scratch", [P, 2, TPB, DIM])
        affine = sb("ln_affine", [P, 2, DIM])
        turned = [ps(f"ln_turned{u}", [P, DK, SEQ]) for u in range(2)]
        affine_loaded = sem("ln_affine_loaded")
        var_ready, dev_ready = sem("ln_var_ready"), sem("ln_dev_ready")
        scratch_ready = sem("ln_scratch_ready")
        scratch_turned, scratch_copied = sem("ln_scratch_turned"), sem("ln_scratch_copied")
        turned_free = sem("ln_turned_free")
        block = ctx.enter_context(nc.Block())

        if gain is not None:
            @block.sync
            def _(sp):
                sp.dma_start(affine[:, 0, :], spread(gain)).then_inc(affine_loaded, 16)
                sp.dma_start(affine[:, 1, :], spread(shift)).then_inc(affine_loaded, 16)

        @block.vector
        def _(dve):
            v = nc.vector
            if add is not None:
                for h in range(2):
                    t = slice(h * TILES // 2, (h + 1) * TILES // 2)
                    v.scalar_tensor_tensor(c.X[:, t, :], c.ACC[:, t, :], c.gate[:, add:add + 1], c.X[:, t, :],
                                           ALU.mult, ALU.add)
                dve.drain()
            with dve.Fori(0, TILES) as t:
                v.bn_stats(stats[:, pieces(t), :].rearrange("p a s -> p (a s)"),
                           source[:, pieces(t), :].rearrange("p a s -> p (a s)"))
            dve.drain()
            v.tensor_tensor(mean[:, :], stats[:, :, 1], stats[:, :, 4], ALU.add)
            v.tensor_tensor(diff[:, :], stats[:, :, 1], stats[:, :, 4], ALU.subtract)
            v.tensor_tensor(var[:, :], stats[:, :, 2], stats[:, :, 5], ALU.add)
            dve.drain()
            v.tensor_scalar(mean[:, :], mean[:, :], 0.5, None, ALU.mult)
            v.tensor_tensor(diff[:, :], diff[:, :], diff[:, :], ALU.mult)
            v.tensor_scalar(var[:, :], var[:, :], 1.0 / DIM, EPS, ALU.mult, ALU.add)
            dve.drain()
            v.scalar_tensor_tensor(var[:, :], diff[:, :], 0.25, var[:, :], ALU.mult, ALU.add).then_inc(var_ready, 1)
            dve.wait_ge(dev_ready, 1)
            v.reciprocal(rstd[:, :], dev[:, :])
            dve.drain()
            v.tensor_tensor(dev[:, :], rstd[:, :], rstd[:, :], ALU.mult)
            dve.drain()
            v.tensor_tensor(dev[:, :], dev[:, :], var[:, :], ALU.mult)
            dve.drain()
            v.tensor_scalar(dev[:, :], dev[:, :], -0.5, 1.5, ALU.mult, ALU.add)
            dve.drain()
            v.tensor_tensor(rstd[:, :], rstd[:, :], dev[:, :], ALU.mult)
            dve.drain()
            if transposed:
                dve.sem_inc(scratch_turned, 2)
            if natural is not None:
                dve.sem_inc(scratch_copied, 2)
            if gain is not None:
                dve.wait_ge(affine_loaded, 32)
            with dve.Fori(0, BATCH // 2) as g:
                for u in range(2):
                    if transposed:
                        dve.wait_ge(scratch_turned, g * 2 + u + 1)
                    if natural is not None:
                        dve.wait_ge(scratch_copied, g * 2 + u + 1)
                    for i in range(TPB):
                        t = g * 4 + (2 * u + i)
                        last = v.tensor_scalar(scratch[:, u, i, :].unsqueeze(1), source[:, pieces(t), :],
                                               mean[:, pieces(t)], rstd[:, pieces(t)], ALU.subtract, ALU.mult)
                    if gain is not None:
                        for k, op in ((0, ALU.mult), (1, ALU.add)):
                            dve.drain()
                            last = v.tensor_tensor(scratch[:, u, :, :], scratch[:, u, :, :],
                                                   affine[:, k, :].unsqueeze(1).to_broadcast([P, TPB, DIM]), op)
                    last.then_inc(scratch_ready, 1)

        if natural is not None:
            @block.gpsimd
            def _(pool):
                with pool.Fori(0, BATCH // 2) as g:
                    for u in range(2):
                        pool.wait_ge(scratch_ready, g * 2 + u + 1)
                        nc.gpsimd.tensor_copy(natural[:, pieces(g * 4 + 2 * u, TPB), :],
                                              scratch[:, u, :, :]).then_inc(scratch_copied, 1)

        if transposed:
            @block.tensor
            def _(pe):
                with pe.Fori(0, BATCH // 2) as g:
                    for u in range(2):
                        pe.wait_ge(scratch_ready, g * 2 + u + 1)
                        pe.wait_ge(turned_free, g * 2 + u + 1)
                        for i in range(TPB):
                            for k in range(DK):
                                last = nc.tensor.transpose(turned[u][:, k, i * P:(i + 1) * P],
                                                           scratch[:, u, i, k * P:(k + 1) * P], c.ident[:, :])
                        last.then_inc(scratch_turned, 1)

        @block.scalar
        def _(act):
            act.wait_ge(var_ready, 1)
            nc.scalar.activation(dev[:, :], var[:, :], ACT.Sqrt).then_inc(dev_ready, 1)
            if transposed:
                act.sem_inc(turned_free, 2)
                with act.Fori(0, BATCH // 2) as g:
                    for u in range(2):
                        act.wait_ge(scratch_turned, g * 2 + u + 3)
                        nc.scalar.activation(c.XT[:, :, pieces(g * 2 * SEQ + u * SEQ, SEQ)], turned[u][:, :, :],
                                             ACT.Copy).then_inc(turned_free, 1)


def experts(nc, c, name, count, width, up, down, gate=None, func=ACT.Silu, up_bias=None, down_bias=None,
            weights=None, fresh=True):
    NF = width // P
    gated = gate is not None
    both = not gated and func == ACT.Relu
    ring = 2 if gated else 4
    loads = (3 if gated else 2) + (down_bias is not None) + (up_bias is not None)
    pairs = count // 2
    slots = 2 if count > 1 else 1
    with ExitStack() as ctx:
        sb, ps, sem = sub_memory(nc, ctx)
        w_up = sb(name + "_w_up", [P, slots, DK, width])
        w_gate = sb(name + "_w_gate", [P, slots, DK, width]) if gated else None
        w_down = sb(name + "_w_down", [P, slots, NF, DIM])
        hidden = sb(name + "_hidden", [P, 2, NF, BLOCK])
        b_down = sb(name + "_b_down", [P, slots, DIM]) if down_bias is not None else None
        b_up = sb(name + "_b_up", [P, slots, NF]) if up_bias is not None else None
        silu = sb(name + "_silu", [P, 2, BLOCK]) if gated else None
        partial = sb(name + "_partial", [P, TPK, DIM]) if down_bias is not None else None
        up_ps = [ps(f"{name}_up{i}", [P, BLOCK]) for i in range(ring)]
        gate_ps = [ps(f"{name}_gate{i}", [P, BLOCK]) for i in range(ring)] if gated else None
        out_ps = [ps(f"{name}_out{i}", [P, BLOCK]) for i in range(4)]
        loaded = [sem(f"{name}_loaded{u}") for u in range(slots)]
        up_ready = sem(name + "_up_ready")
        gate_done = sem(name + "_gate_done")
        hidden_act, hidden_dve = sem(name + "_hidden_act"), sem(name + "_hidden_dve")
        out_ready, out_free = sem(name + "_out_ready"), sem(name + "_out_free")
        block = ctx.enter_context(nc.Block())
        on_act = [not gated and (not both or f % 2 == 0) for f in range(NF)]
        share = {True: sum(on_act), False: NF - sum(on_act)}
        credit = {True: ring // 2 if both else ring, False: ring // 2 if both else ring}
        done = {True: hidden_act, False: hidden_dve}
        order = []
        for f in range(NF):
            order.append(sum(on_act[j] == on_act[f] for j in range(f)))
        OUT0 = 2 * TPK

        def load(sp, e, u):
            fill = [(w_up, up), (w_gate, gate)] if gated else [(w_up, up)]
            for dst, src in fill:
                sp.dma_start(dst[:, u, :, :].unsqueeze(1),
                             src[pieces(e), :, :].rearrange("a (k p) n -> p a k n", p=P)).then_inc(loaded[u], 16)
            sp.dma_start(w_down[:, u, :, :].unsqueeze(1),
                         down[pieces(e), :, :].rearrange("a (k p) n -> p a k n", p=P)).then_inc(loaded[u], 16)
            if up_bias is not None:
                sp.dma_start(b_up[:, u, :].unsqueeze(1), up_bias[pieces(e), :, :].rearrange("a p f -> p a f"))\
                  .then_inc(loaded[u], 16)
            if down_bias is not None:
                sp.dma_start(b_down[:, u, :].unsqueeze(1), down_bias[pieces(e), :].partition_broadcast(P))\
                  .then_inc(loaded[u], 16)

        @block.sync
        def _(sp):
            for u in range(slots):
                load(sp, u, u)
            if pairs > 1:
                with sp.Fori(1, pairs) as g:
                    for u in range(2):
                        sp.wait_ge(out_free, g * (2 * TILES) + (4 + TILES * (u - 1)))
                        load(sp, g * 2 + u, u)

        def over_experts(eng, body):
            if pairs:
                with eng.Fori(0, pairs) as g:
                    for u in range(2):
                        body(g, u)
            else:
                body(0, 0)

        @block.tensor
        def _(pe):
            pe.sem_inc(out_ready, OUT0)

            def body(g, u):
                pe.wait_ge(loaded[u], (g + 1) * (16 * loads))

                def up_block(k):
                    n = u * BLOCKS + k
                    for f in range(NF):
                        s = on_act[f]
                        pe.wait_ge(done[s], g * (2 * BLOCKS * share[s]) + (n * share[s] + order[f] + 1))
                        slot = f % ring if not gated else (n * NF + f) % ring
                        w = (w_up, w_gate) if gated else (w_up,)
                        for wt, tile in zip(w, (up_ps, gate_ps)):
                            for kk in range(DK):
                                last = nc.tensor.matmul(tile[slot][:, :], wt[:, u, kk, f * P:(f + 1) * P],
                                                        c.XT[:, kk, k * BLOCK:(k + 1) * BLOCK],
                                                        start=kk == 0, stop=kk == DK - 1)
                        last.then_inc(up_ready, 1)

                def down_block(k):
                    n = u * BLOCKS + k
                    for s in (True, False):
                        if share[s]:
                            pe.wait_ge(done[s], g * (2 * BLOCKS * share[s]) + ((n + 1) * share[s] + credit[s]))
                    for i in range(TPK):
                        pe.wait_ge(out_free, g * (2 * TILES) + (n * TPK + i + 1))
                        for f in range(NF):
                            last = nc.tensor.matmul(out_ps[i][:, 0:DIM], hidden[:, k % 2, f, i * P:(i + 1) * P],
                                                    w_down[:, u, f, :], start=f == 0, stop=f == NF - 1)
                        last.then_inc(out_ready, 1)

                for k in range(BLOCKS):
                    up_block(k)
                    if k:
                        down_block(k - 1)
                down_block(BLOCKS - 1)

            over_experts(pe, body)

        @block.scalar
        def _(act):
            if not gated:
                act.sem_inc(hidden_act, credit[True])

            def body(g, u):
                if up_bias is not None:
                    act.wait_ge(loaded[u], (g + 1) * (16 * loads))
                for k in range(BLOCKS):
                    n = u * BLOCKS + k
                    if not gated:
                        act.wait_ge(out_ready, g * (2 * TILES) + (OUT0 + TPK * (n - 1)))
                    for f in range(NF):
                        slot = (n * NF + f) % ring
                        if gated:
                            act.wait_ge(hidden_dve, g * (2 * BLOCKS * NF) + (n * NF + f + 1))
                            act.wait_ge(up_ready, g * (2 * BLOCKS * NF) + (n * NF + f + 1))
                            nc.scalar.activation(silu[:, slot, :], gate_ps[slot][:, :], func).then_inc(gate_done, 1)
                        elif on_act[f]:
                            act.wait_ge(up_ready, g * (2 * BLOCKS * NF) + (n * NF + f + 1))
                            nc.scalar.activation(hidden[:, k % 2, f, :], up_ps[slot][:, :], func,
                                                 bias=b_up[:, u, f:f + 1]).then_inc(hidden_act, 1)

            over_experts(act, body)

        @block.vector
        def _(dve):
            v = nc.vector
            if gated or both:
                dve.sem_inc(hidden_dve, credit[False])
            dve.sem_inc(out_free, 4)
            if fresh:
                v.memset(c.ACC[:, :, :], 0.0)

            def body(g, u):
                e = g * 2 + u
                dve.drain()
                if up_bias is not None:
                    dve.wait_ge(loaded[u], (g + 1) * (16 * loads))

                def hidden_block(k):
                    n = u * BLOCKS + k
                    if gated or both:
                        dve.wait_ge(out_ready, g * (2 * TILES) + (OUT0 + TPK * (n - 1)))
                    for f in range(NF):
                        slot = (n * NF + f) % ring
                        if gated:
                            dve.wait_ge(gate_done, g * (2 * BLOCKS * NF) + (n * NF + f + 1))
                            v.tensor_tensor(hidden[:, k % 2, f, :], up_ps[slot][:, :], silu[:, slot, :],
                                            ALU.mult).then_inc(hidden_dve, 1)
                        elif not on_act[f]:
                            dve.wait_ge(up_ready, g * (2 * BLOCKS * NF) + (n * NF + f + 1))
                            v.tensor_scalar(hidden[:, k % 2, f, :], up_ps[slot][:, :], b_up[:, u, f:f + 1],
                                            0.0, ALU.add, ALU.max).then_inc(hidden_dve, 1)

                def out_block(k):
                    n = u * BLOCKS + k
                    if down_bias is not None:
                        dve.wait_ge(loaded[u], (g + 1) * (16 * loads))
                        for i in range(TPK):
                            dve.wait_ge(out_ready, g * (2 * TILES) + (OUT0 + n * TPK + i + 1))
                            v.tensor_tensor(partial[:, i, :], out_ps[i][:, 0:DIM], b_down[:, u, :],
                                            ALU.add).then_inc(out_free, 1)
                        dve.drain()
                    for i in range(TPK):
                        t = k * TPK + i
                        acc = c.ACC[:, t, :]
                        if down_bias is not None:
                            val = partial[:, i, :]
                        else:
                            dve.wait_ge(out_ready, g * (2 * TILES) + (OUT0 + n * TPK + i + 1))
                            val = out_ps[i][:, 0:DIM]
                        if weights is not None:
                            last = v.scalar_tensor_tensor(acc, val, weights[:, pieces(e), t], acc, ALU.mult, ALU.add)
                        else:
                            last = v.tensor_tensor(acc, val, acc, ALU.add)
                        if down_bias is None:
                            last.then_inc(out_free, 1)
                    if down_bias is not None:
                        dve.drain()

                for k in range(BLOCKS):
                    hidden_block(k)
                    if k:
                        out_block(k - 1)
                out_block(BLOCKS - 1)

            over_experts(dve, body)
            dve.drain()


def hash_router(nc, c, W):
    with ExitStack() as ctx:
        sb, ps, sem = sub_memory(nc, ctx)
        s, a, k, g, h = (sb(f"hash_{n}", [P, TILES]) for n in ("sum", "abs", "whole", "over", "bucket"))
        hit = sb("hash_hit", [P, 8, TILES])
        block = ctx.enter_context(nc.Block())

        @block.vector
        def _(dve):
            v = nc.vector

            def ts(*args):
                v.tensor_scalar(*args)
                dve.drain()

            def tt(*args):
                v.tensor_tensor(*args)
                dve.drain()

            S, A, K, G, H = (x[:, :] for x in (s, a, k, g, h))
            tt(S, c.XN[:, :, 0], c.XN[:, :, 1], ALU.add)
            ts(A, S, -1.0, None, ALU.mult)
            tt(A, A, S, ALU.max)
            ts(K, A, MAGIC, None, ALU.add)
            ts(K, K, MAGIC, None, ALU.subtract)
            tt(G, K, A, ALU.is_gt)
            tt(K, K, G, ALU.subtract)
            ts(G, S, 0.0, -2.0, ALU.is_lt, ALU.mult)
            ts(G, G, 1.0, None, ALU.add)
            tt(K, K, G, ALU.mult)
            ts(G, K, 0.125, -0.4375, ALU.mult, ALU.add)
            ts(G, G, MAGIC, None, ALU.add)
            ts(G, G, MAGIC, -8.0, ALU.subtract, ALU.mult)
            tt(H, K, G, ALU.add)
            iota = c.iota8[:, 0:8].unsqueeze(2).to_broadcast([P, 8, TILES])
            before = c.iota8[:, 16:24].unsqueeze(2).to_broadcast([P, 8, TILES])
            bucket = H.unsqueeze(1).to_broadcast([P, 8, TILES])
            tt(hit[:, :, :], iota, bucket, ALU.is_equal)
            tt(W[:, :, :], before, bucket, ALU.is_equal)
            tt(W[:, :, :], W[:, :, :], hit[:, :, :], ALU.add)
            ts(W[:, :, :], W[:, :, :], 0.5, None, ALU.mult)


def softmax_router(nc, c, name, router, E, W, eps=None):
    with ExitStack() as ctx:
        sb, ps, sem = sub_memory(nc, ctx)
        w = sb(name + "_w", [P, DK, E])
        p = sb(name + "_probs", [P, TILES, E])
        one = sb(name + "_stat", [P, TILES])
        top = sb(name + "_top", [P, TILES, 8])
        at = sb(name + "_at", [P, TILES, 8], U32)
        atf = sb(name + "_atf", [P, TILES, 8])
        hit = sb(name + "_hit", [P, E, TILES])
        logits = ps(name + "_logits", [P, TILES, E])
        loaded, logits_ready = sem(name + "_loaded"), sem(name + "_logits_ready")
        shifted, exp_ready = sem(name + "_shifted"), sem(name + "_exp_ready")
        block = ctx.enter_context(nc.Block())

        @block.sync
        def _(sp):
            sp.dma_start(w[:, :, :], router.rearrange("(k p) e -> p k e", p=P)).then_inc(loaded, 16)

        @block.tensor
        def _(pe):
            pe.wait_ge(loaded, 16)
            for t in range(TILES):
                for k in range(DK):
                    last = nc.tensor.matmul(logits[:, t, :], c.XT[:, k, t * P:(t + 1) * P], w[:, k, :],
                                            start=k == 0, stop=k == DK - 1)
            last.then_inc(logits_ready, 1)

        @block.scalar
        def _(act):
            act.wait_ge(shifted, 1)
            nc.scalar.activation(p[:, :, :], p[:, :, :], ACT.Exp).then_inc(exp_ready, 1)

        @block.vector
        def _(dve):
            v = nc.vector
            wide = [P, TILES, E]
            dve.wait_ge(logits_ready, 1)
            v.tensor_reduce(one[:, :], logits[:, :, :], AX.X, ALU.max)
            dve.drain()
            v.tensor_tensor(p[:, :, :], logits[:, :, :], one[:, :].unsqueeze(2).to_broadcast(wide), ALU.subtract)\
             .then_inc(shifted, 1)
            dve.wait_ge(exp_ready, 1)
            v.tensor_reduce(one[:, :], p[:, :, :], AX.X, ALU.add)
            dve.drain()
            v.reciprocal(one[:, :], one[:, :])
            dve.drain()
            v.tensor_tensor(p[:, :, :], p[:, :, :], one[:, :].unsqueeze(2).to_broadcast(wide), ALU.mult)
            dve.drain()
            for t in range(TILES):
                v.max(top[:, t, :], p[:, t, :])
            dve.drain()
            for t in range(TILES):
                v.max_index(at[:, t, :], top[:, t, :], p[:, t, :])
            dve.drain()
            v.tensor_copy(atf[:, :, :], at[:, :, :])
            if eps is not None:
                v.tensor_tensor(one[:, :], top[:, :, 0], top[:, :, 1], ALU.add)
                dve.drain()
                v.tensor_scalar(one[:, :], one[:, :], eps, None, ALU.add)
                dve.drain()
                v.reciprocal(one[:, :], one[:, :])
                dve.drain()
                v.tensor_tensor(top[:, :, 0:2], top[:, :, 0:2], one[:, :].unsqueeze(2).to_broadcast([P, TILES, 2]),
                                ALU.mult)
            dve.drain()
            by_expert = [P, E, TILES]
            iota = c.iota8[:, 0:E].unsqueeze(2).to_broadcast(by_expert)
            for rank, out in ((0, W), (1, hit)):
                v.tensor_tensor(out[:, :, :], iota, atf[:, :, rank].unsqueeze(1).to_broadcast(by_expert), ALU.is_equal)
                dve.drain()
                v.tensor_tensor(out[:, :, :], out[:, :, :], top[:, :, rank].unsqueeze(1).to_broadcast(by_expert),
                                ALU.mult)
                dve.drain()
            v.tensor_tensor(W[:, :, :], W[:, :, :], hit[:, :, :], ALU.add)
            dve.drain()


def store_output(nc, c, out):
    with ExitStack() as ctx:
        sb, ps, sem = sub_memory(nc, ctx)
        final, stored = sem("final"), sem("stored")
        block = ctx.enter_context(nc.Block())
        HALF = TILES // 2

        @block.vector
        def _(dve):
            for h in range(2):
                t = slice(h * HALF, (h + 1) * HALF)
                nc.vector.scalar_tensor_tensor(c.X[:, t, :], c.ACC[:, t, :], c.gate[:, c.last:c.last + 1], c.X[:, t, :],
                                               ALU.mult, ALU.add).then_inc(final, 1)

        @block.sync
        def _(sp):
            y = out.rearrange("b (i p) d -> p (b i) d", p=P)
            for h in range(2):
                t = slice(h * HALF, (h + 1) * HALF)
                sp.wait_ge(final, h + 1)
                sp.dma_start(y[:, t, :], c.X[:, t, :]).then_inc(stored, 16)
            sp.wait_ge(stored, 32)


def layer1_attention(nc, c, a):
    HEADS, DH = 8, 128
    INNER = HEADS * DH
    HALF = HEADS // 2
    SCALE = float(DH) ** -0.25
    ROWS = TPB * HEADS
    with ExitStack() as ctx:
        sb, ps, sem = sub_memory(nc, ctx, "a1_")
        wq = sb("wq", [P, DK, INNER])
        wk = sb("wk", [CP, CK, INNER])
        wv = sb("wv", [CP, CK, INNER])
        wo = sb("wo", [P, HEADS, DIM])
        bo = sb("bo", [P, DIM])
        context = sb("context", [CP, 2, CK, KEYS])
        q = sb("q", [P, HEADS, SEQ])
        k = sb("k", [P, HEADS, KEYS])
        v = sb("v", [KEYS, 2, INNER])
        probs = sb("probs", [P, TPB * 2, HALF * KEYS])
        stat = sb("stat", [P, ROWS])
        probs_t = sb("probs_t", [KEYS, ROWS, P])
        mixed = sb("mixed", [P, HEADS, SEQ])
        A = ps("A", [P, 4, 512])
        B = ps("B", [P, 4, 512])
        w_loaded = sem("w_loaded")
        ctx_loaded = [sem(f"ctx_loaded{u}") for u in range(2)]
        q_ready, kv_ready, kv_done = sem("q_ready"), sem("kv_ready"), sem("kv_done")
        q_done = sem("q_done")
        scores_ready, scores_read = sem("scores_ready"), sem("scores_read")
        shifted, exp_done, probs_ready = sem("shifted"), sem("exp_done"), sem("probs_ready")
        turned, turned_done = sem("turned"), sem("turned_done")
        mixed_ready, mixed_done = sem("mixed_ready"), sem("mixed_done")
        out_ready, out_done = sem("out_ready"), sem("out_done")
        block = ctx.enter_context(nc.Block())

        def batches(eng, body):
            with eng.Fori(0, BATCH // 2 - 1) as g:
                for u in range(2):
                    body(g * 2 + u, u, False)
            for b in range(BATCH - 2, BATCH):
                body(b, b % 2, b == BATCH - 1)

        @block.sync
        def _(sp):
            def load(b, u):
                sp.dma_start(context[:, u, :, :].unsqueeze(1),
                             a["context_T"][pieces(b), :, :].rearrange("b (k p) s -> p b k s", p=CP))\
                  .then_inc(ctx_loaded[u], 16)

            load(0, 0)
            load(1, 1)
            sp.dma_start(wq[:, :, :], a["L1_xattn_Wq"].rearrange("(k p) n -> p k n", p=P)).then_inc(w_loaded, 16)
            sp.dma_start(wk[:, :, :], a["L1_xattn_Wk"].rearrange("(k p) n -> p k n", p=CP)).then_inc(w_loaded, 16)
            sp.dma_start(wv[:, :, :], a["L1_xattn_Wv"].rearrange("(k p) n -> p k n", p=CP)).then_inc(w_loaded, 16)
            sp.dma_start(wo[:, :, :], a["L1_xattn_Wo"].rearrange("(h p) n -> p h n", p=P)).then_inc(w_loaded, 16)
            sp.dma_start(bo[:, :], spread(a["L1_xattn_bo"])).then_inc(w_loaded, 16)
            with sp.Fori(1, BATCH // 2) as g:
                for u in range(2):
                    sp.wait_ge(kv_ready, g * 2 + (u - 1))
                    load(g * 2 + u, u)

        @block.tensor
        def _(pe):
            def project(b, u):
                pe.wait_ge(out_done, b + 1)
                for h in range(HEADS):
                    for kk in range(DK):
                        last = nc.tensor.matmul(B[:, h // 2, (h % 2) * SEQ:(h % 2 + 1) * SEQ],
                                                wq[:, kk, h * DH:(h + 1) * DH],
                                                c.XT[:, kk, pieces(b * SEQ, SEQ)], start=kk == 0, stop=kk == DK - 1)
                last.then_inc(q_ready, 1)
                pe.wait_ge(ctx_loaded[u], (b // 2 + 1) * 16 if isinstance(b, int) else b * 8 + (16 - 8 * u))
                pe.wait_ge(scores_read, b + 1)
                for h in range(HEADS):
                    for kk in range(CK):
                        nc.tensor.matmul(A[:, h // HALF, (h % HALF) * KEYS:(h % HALF + 1) * KEYS],
                                         wk[:, kk, h * DH:(h + 1) * DH], context[:, u, kk, :],
                                         start=kk == 0, stop=kk == CK - 1)
                for n in range(INNER // 512):
                    for kk in range(CK):
                        last = nc.tensor.matmul(A[0:KEYS, 2 + n, :], context[:, u, kk, :],
                                                wv[:, kk, n * 512:(n + 1) * 512], start=kk == 0, stop=kk == CK - 1)
                last.then_inc(kv_ready, 1)

            def body(b, u, final):
                pe.wait_ge(q_done, b + 1)
                pe.wait_ge(kv_done, b + 1)
                pe.wait_ge(mixed_done, b + 1)
                for i in range(TPB):
                    for h in range(HEADS):
                        last = nc.tensor.matmul(A[:, 2 * i + h // HALF, (h % HALF) * KEYS:(h % HALF + 1) * KEYS],
                                                q[:, h, i * P:(i + 1) * P], k[:, h, :], start=True, stop=True)
                last.then_inc(scores_ready, 1)
                if not final:
                    project(b + 1, 1 - u)
                pe.wait_ge(probs_ready, b + 1)
                if not final:
                    pe.wait_ge(q_done, b + 2)
                else:
                    pe.wait_ge(out_done, b + 2)
                for r in range(ROWS):
                    last = nc.tensor.transpose(B[0:KEYS, r // 4, (r % 4) * P:(r % 4 + 1) * P],
                                               probs[:, r // HALF, (r % HALF) * KEYS:(r % HALF + 1) * KEYS],
                                               c.ident[:, :])
                last.then_inc(turned, 1)
                pe.wait_ge(turned_done, b + 1)
                if not final:
                    pe.wait_ge(kv_done, b + 2)
                for h in range(HEADS):
                    last = nc.tensor.matmul(A[:, h // 2, (h % 2) * SEQ:(h % 2 + 1) * SEQ]
                                            .rearrange("p (i t) -> p i t", t=P),
                                            v[:, u, h * DH:(h + 1) * DH],
                                            probs_t[:, h:ROWS:HEADS, :], start=True, stop=True)
                last.then_inc(mixed_ready, 1)
                pe.wait_ge(mixed_done, b + 2)
                for i in range(TPB):
                    for h in range(HEADS):
                        last = nc.tensor.matmul(B[:, i, 0:DIM], mixed[:, h, i * P:(i + 1) * P], wo[:, h, :],
                                                start=h == 0, stop=h == HEADS - 1)
                last.then_inc(out_ready, 1)

            pe.wait_ge(w_loaded, 80)
            project(0, 0)
            batches(pe, body)

        @block.scalar
        def _(act):
            act.sem_inc(mixed_done, 1)

            def evacuate_qkv(b, u):
                act.wait_ge(q_ready, b + 1)
                nc.scalar.activation(q[:, :, :].rearrange("p (b h) s -> p b (h s)", b=4), B[:, :, :], ACT.Copy,
                                     scale=SCALE).then_inc(q_done, 1)
                act.wait_ge(kv_ready, b + 1)
                nc.scalar.activation(k[:, :, :].rearrange("p (b h) s -> p b (h s)", b=2),
                                     A[:, 0:2, 0:HALF * KEYS], ACT.Copy, scale=SCALE)
                nc.scalar.activation(v[:, u, :].rearrange("p (b n) -> p b n", b=2), A[0:KEYS, 2:4, :],
                                     ACT.Copy).then_inc(kv_done, 1)

            def body(b, u, final):
                if not final:
                    act.wait_ge(scores_ready, b + 1)
                    evacuate_qkv(b + 1, 1 - u)
                act.wait_ge(shifted, b + 1)
                nc.scalar.activation(probs[:, :, :], probs[:, :, :], ACT.Exp).then_inc(exp_done, 1)
                act.wait_ge(turned, b + 1)
                nc.scalar.activation(probs_t[:, :, :].rearrange("p (b r) t -> p b (r t)", b=4), B[0:KEYS, :, :],
                                     ACT.Copy).then_inc(turned_done, 1)
                act.wait_ge(mixed_ready, b + 1)
                nc.scalar.activation(mixed[:, :, :].rearrange("p (b h) s -> p b (h s)", b=4), A[:, :, :],
                                     ACT.Copy).then_inc(mixed_done, 1)

            evacuate_qkv(0, 0)
            batches(act, body)

        @block.vector
        def _(dve):
            vv = nc.vector
            grid = [P, ROWS, KEYS]
            probs_r = probs[:, :, :].rearrange("p a (h s) -> p (a h) s", s=KEYS)
            scores_r = A[:, :, 0:HALF * KEYS].rearrange("p a (h s) -> p a h s", s=KEYS)
            stat_r = stat[:, :].rearrange("p (a h) -> p a h", h=HALF)
            dve.sem_inc(scores_read, 1)
            dve.sem_inc(out_done, 2)
            dve.wait_ge(w_loaded, 80)

            def body(b, u, final):
                dve.wait_ge(scores_ready, b + 1)
                vv.tensor_reduce(stat_r, scores_r, AX.X, ALU.max)
                dve.drain()
                vv.tensor_tensor(probs[:, :, :].rearrange("p a (h s) -> p a h s", s=KEYS), scores_r,
                                 stat_r.unsqueeze(3).to_broadcast([P, 2 * TPB, HALF, KEYS]), ALU.subtract)
                dve.drain()
                dve.sem_inc(scores_read, 1)
                dve.sem_inc(shifted, 1)
                dve.wait_ge(exp_done, b + 1)
                vv.tensor_reduce(stat[:, :], probs_r, AX.X, ALU.add)
                dve.drain()
                vv.reciprocal(stat[:, :], stat[:, :])
                dve.drain()
                vv.tensor_tensor(probs_r, probs_r, stat[:, :].unsqueeze(2).to_broadcast(grid), ALU.mult)\
                  .then_inc(probs_ready, 1)
                dve.wait_ge(out_ready, b + 1)
                vv.tensor_tensor(c.ACC[:, pieces(b * TPB, TPB), :], B[:, 0:TPB, 0:DIM],
                                 bo[:, :].unsqueeze(1).to_broadcast([P, TPB, DIM]), ALU.add).then_inc(out_done, 1)

            batches(dve, body)


def narrow_attention(nc, c, a, layer):
    HEADS, DH = 16, 16
    HT = P // DH
    SCALE = float(DH) ** -0.5
    CLAMP = 10000.0
    final_layer = layer == 3
    with ExitStack() as ctx:
        sb, ps, sem = sub_memory(nc, ctx, f"a{layer}_")
        wq = sb("wq", [P, DK, DIM])
        wk = sb("wk", [CP, CK, DIM])
        wv = sb("wv", [CP, CK, DIM])
        context = sb("context", [CP, 2, CK, KEYS])
        q = sb("q", [P, DK, SEQ])
        k = sb("k", [P, 2, DK, KEYS])
        k_wide = sb("k_wide", [P, DK, HT, KEYS])
        v = sb("v", [KEYS, 2, DIM])
        probs = sb("probs", [P, TPB, HEADS, KEYS])
        stat = sb("stat", [P, TPB, HEADS])
        probs_t = sb("probs_t", [KEYS, 2, 8, P])
        if final_layer:
            mask8 = sb("mask8", [P, TILES], U8)
            keep = sb("keep", [P, TILES])
            fill = sb("fill", [P, TILES])
        else:
            wo = sb("wo", [P, DK, DIM])
            bqk = sb("bqk", [P, 2, DK])
            bo = sb("bo", [P, DIM])
            bv = sb("bv", [P, DIM])
            mixed = sb("mixed", [P, DIM])
            mixed_t = sb("mixed_t", [P, DK, P])
        S = ps("scores", [P, 4, 512])
        T = ps("turned", [P, 2, 512])
        Q = ps("q_ps", [P, DK, SEQ])
        KV = ps("kv_ps", [P, 512])
        w_loaded = sem("w_loaded")
        ctx_loaded = [sem(f"ctx_loaded{u}") for u in range(2)]
        setup_done = sem("setup_done")
        q_ready, kv_ready, q_done, kv_done = sem("q_ready"), sem("kv_ready"), sem("q_done"), sem("kv_done")
        k_wide_ready = sem("k_wide_ready")
        scores_ready, scores_read = sem("scores_ready"), sem("scores_read")
        shifted, exp_done = sem("shifted"), sem("exp_done")
        turned, turned_done = sem("turned"), sem("turned_done")
        mixed_ready, mixed_done = sem("mixed_ready"), sem("mixed_done")
        mt_ready, mt_done = sem("mt_ready"), sem("mt_done")
        out_ready, out_done = sem("out_ready"), sem("out_done")
        block = ctx.enter_context(nc.Block())
        LOADS = 48 + (16 if final_layer else 80)

        def batches(eng, body):
            with eng.Fori(0, BATCH // 2 - 1) as g:
                for u in range(2):
                    body(g * 2 + u, u, False)
            for b in range(BATCH - 2, BATCH):
                body(b, b % 2, b == BATCH - 1)

        @block.sync
        def _(sp):
            def load(b, u):
                sp.dma_start(context[:, u, :, :].unsqueeze(1),
                             a["context_T"][pieces(b), :, :].rearrange("b (k p) s -> p b k s", p=CP))\
                  .then_inc(ctx_loaded[u], 16)

            load(0, 0)
            load(1, 1)
            if final_layer:
                weights = [(wq, a["L3_Wq_T"], P), (wk, a["L3_Wkv_T"][:, 0:DIM], CP),
                           (wv, a["L3_Wkv_T"][:, DIM:2 * DIM], CP)]
            else:
                weights = [(wq, a["L2_xattn_Wq"], P), (wk, a["L2_xattn_Wk"], CP), (wv, a["L2_xattn_Wv"], CP),
                           (wo, a["L2_xattn_Wo"], P)]
            for dst, src, p in weights:
                sp.dma_start(dst[:, :, :], src.rearrange("(k p) n -> p k n", p=p)).then_inc(w_loaded, 16)
            if final_layer:
                sp.dma_start(mask8[:, :], a["mask_BxS_bk0"]).then_inc(w_loaded, 16)
            else:
                sp.dma_start(bqk[:, 0, :], a["L2_bq"]).then_inc(w_loaded, 16)
                sp.dma_start(bqk[:, 1, :], a["L2_bk"]).then_inc(w_loaded, 16)
                sp.dma_start(bo[:, :], spread(a["L2_xattn_bo"])).then_inc(w_loaded, 16)
                sp.dma_start(bv[:, :], spread(a["L2_xattn_bv"])).then_inc(w_loaded, 16)
            with sp.Fori(1, BATCH // 2) as g:
                for u in range(2):
                    sp.wait_ge(kv_ready, g * 2 + (u - 1))
                    load(g * 2 + u, u)

        @block.tensor
        def _(pe):
            def project(b, u):
                pe.wait_ge(out_done, b * TPB + 1)
                for m in range(DK):
                    for kk in range(DK):
                        last = nc.tensor.matmul(Q[:, m, :], wq[:, kk, m * P:(m + 1) * P],
                                                c.XT[:, kk, pieces(b * SEQ, SEQ)], start=kk == 0, stop=kk == DK - 1)
                last.then_inc(q_ready, 1)
                pe.wait_ge(ctx_loaded[u], (b // 2 + 1) * 16 if isinstance(b, int) else b * 8 + (16 - 8 * u))
                pe.wait_ge(kv_done, b + 1)
                for m in range(DK):
                    for kk in range(CK):
                        nc.tensor.matmul(KV[:, m * KEYS:(m + 1) * KEYS], wk[:, kk, m * P:(m + 1) * P],
                                         context[:, u, kk, :], start=kk == 0, stop=kk == CK - 1)
                for kk in range(CK):
                    last = nc.tensor.matmul(KV[0:KEYS, DIM:2 * DIM], context[:, u, kk, :], wv[:, kk, :],
                                            start=kk == 0, stop=kk == CK - 1)
                last.then_inc(kv_ready, 1)

            def scores(b, i):
                n = b * TPB + i
                pe.wait_ge(scores_read, n + 1)
                for h in range(0, HEADS, 4):
                    m = h // HT
                    last = nc.tensor.matmul(S[:, h // 4, 0:4 * KEYS], q[:, m, i * P:(i + 1) * P],
                                            k_wide[:, m, h % HT:h % HT + 4, :].rearrange("p h s -> p (h s)"),
                                            start=True, stop=True)
                last.then_inc(scores_ready, 1)

            def mix(b, i, u):
                n = b * TPB + i
                pe.wait_ge(exp_done, n + 1)
                for half in range(2):
                    pe.wait_ge(turned_done, n * 2 + half + 1)
                    for r in range(8):
                        last = nc.tensor.transpose(T[0:KEYS, r // 4, (r % 4) * P:(r % 4 + 1) * P],
                                                   probs[:, i, half * 8 + r, :], c.ident[:, :])
                    last.then_inc(turned, 1)
                    if half == 0:
                        pe.wait_ge(out_done, n + 3)
                        if i == 0:
                            pe.wait_ge(q_done, (b + 2) if not isinstance(b, int) or b + 1 < BATCH else b + 1)
                    pe.wait_ge(turned_done, n * 2 + half + 2)
                    for r in range(8):
                        h = half * 8 + r
                        last = nc.tensor.matmul(Q[:, 0, h * DH:(h + 1) * DH], probs_t[:, half, r, :],
                                                v[:, u, h * DH:(h + 1) * DH], start=True, stop=True)
                last.then_inc(mixed_ready, 1)
                if not final_layer:
                    pe.wait_ge(mixed_done, n + 1)
                    for m in range(DK):
                        last = nc.tensor.transpose(Q[:, 1, m * P:(m + 1) * P], mixed[:, m * P:(m + 1) * P],
                                                   c.ident[:, :])
                    last.then_inc(mt_ready, 1)
                    pe.wait_ge(mt_done, n + 1)
                    for m in range(DK):
                        last = nc.tensor.matmul(Q[:, 0, :], mixed_t[:, m, :], wo[:, m, :], start=m == 0,
                                                stop=m == DK - 1)
                    last.then_inc(out_ready, 1)

            def body(b, u, final):
                pe.wait_ge(q_done, b + 1)
                pe.wait_ge(k_wide_ready, b + 1)
                pe.wait_ge(kv_done, b + 2)
                scores(b, 0)
                scores(b, 1)
                if not final:
                    project(b + 1, 1 - u)
                mix(b, 0, u)
                mix(b, 1, u)

            pe.wait_ge(w_loaded, LOADS)
            project(0, 0)
            batches(pe, body)

        @block.scalar
        def _(act):
            act.sem_inc(kv_done, 1)
            act.sem_inc(turned_done, 1)
            act.wait_ge(setup_done, 1)

            def evacuate_qkv(b, u):
                act.wait_ge(q_ready, b + 1)
                for m in range(DK):
                    if final_layer:
                        last = nc.scalar.activation(q[:, m, :], Q[:, m, :], ACT.Copy, scale=SCALE)
                    else:
                        last = nc.scalar.activation(q[:, m, :], Q[:, m, :], ACT.Identity, bias=bqk[:, 0, m:m + 1])
                last.then_inc(q_done, 1)
                act.wait_ge(kv_ready, b + 1)
                for m in range(DK):
                    if final_layer:
                        nc.scalar.activation(k[:, u, m, :], KV[:, m * KEYS:(m + 1) * KEYS], ACT.Copy)
                    else:
                        nc.scalar.activation(k[:, u, m, :], KV[:, m * KEYS:(m + 1) * KEYS], ACT.Identity,
                                             bias=bqk[:, 1, m:m + 1])
                nc.scalar.activation(v[:, u, :], KV[0:KEYS, DIM:2 * DIM], ACT.Copy).then_inc(kv_done, 1)

            def body(b, u, final):
                if not final:
                    act.wait_ge(scores_ready, b * TPB + TPB)
                    evacuate_qkv(b + 1, 1 - u)
                for i in range(TPB):
                    n = b * TPB + i
                    act.wait_ge(shifted, n + 1)
                    nc.scalar.activation(probs[:, i, :, :], probs[:, i, :, :], ACT.Exp,
                                         scale=1.0 if final_layer else SCALE).then_inc(exp_done, 1)
                for i in range(TPB):
                    n = b * TPB + i
                    for half in range(2):
                        act.wait_ge(turned, n * 2 + half + 1)
                        nc.scalar.activation(probs_t[:, half, :, :].rearrange("p (b r) t -> p b (r t)", b=2),
                                             T[0:KEYS, :, :], ACT.Copy).then_inc(turned_done, 1)
                    if not final_layer:
                        act.wait_ge(mt_ready, n + 1)
                        nc.scalar.activation(mixed_t[:, :, :], Q[:, 1, :].rearrange("p (m t) -> p m t", t=P),
                                             ACT.Copy).then_inc(mt_done, 1)

            evacuate_qkv(0, 0)
            batches(act, body)

        @block.gpsimd
        def _(pool):
            pool.wait_ge(setup_done, 1)
            wide = [P, HT, KEYS]

            def body(b, u, final):
                pool.wait_ge(kv_done, b + 2)
                pool.wait_ge(scores_ready, b * TPB)
                for m in range(DK):
                    last = nc.gpsimd.tensor_tensor(k_wide[:, m, :, :], k[:, u, m, :].unsqueeze(1).to_broadcast(wide),
                                                   c.headmask[:, 4:4 + HT].unsqueeze(2).to_broadcast(wide), ALU.mult)
                last.then_inc(k_wide_ready, 1)

            pool.wait_ge(kv_done, 2)
            for m in range(DK):
                last = nc.gpsimd.tensor_tensor(k_wide[:, m, :, :], k[:, 0, m, :].unsqueeze(1).to_broadcast(wide),
                                               c.headmask[:, 4:4 + HT].unsqueeze(2).to_broadcast(wide), ALU.mult)
            last.then_inc(k_wide_ready, 1)
            with pool.Fori(0, BATCH // 2 - 1) as g:
                for u in range(2):
                    body(g * 2 + (u + 1), 1 - u, False)
            body(BATCH - 1, 1, True)

        @block.vector
        def _(dve):
            vv = nc.vector
            dve.sem_inc(scores_read, 1)
            dve.sem_inc(out_done, 3)
            dve.wait_ge(w_loaded, LOADS)
            if final_layer:
                vv.tensor_copy(keep[:, :], mask8[:, :])
                dve.drain()
                vv.tensor_scalar(fill[:, :], keep[:, :], 1.0, 1.0e9, ALU.subtract, ALU.mult)
                dve.drain()
            dve.sem_inc(setup_done, 1)
            scores_r = S[:, :, 0:4 * KEYS]

            def body(b, u, final):
                for i in range(TPB):
                    n = b * TPB + i
                    pr = probs[:, i, :, :]
                    st = stat[:, i, :]
                    dve.wait_ge(scores_ready, n + 1)
                    grouped = pr.rearrange("p (b h) s -> p b (h s)", b=4)
                    if final_layer:
                        vv.tensor_scalar(grouped, scores_r, keep[:, pieces(n)], fill[:, pieces(n)],
                                         ALU.mult, ALU.add).then_inc(scores_read, 1)
                    else:
                        vv.tensor_scalar(grouped, scores_r, CLAMP / SCALE, -CLAMP / SCALE,
                                         ALU.min, ALU.max).then_inc(scores_read, 1)
                    dve.drain()
                    vv.tensor_reduce(st, pr, AX.X, ALU.max)
                    dve.drain()
                    vv.tensor_tensor(pr, pr, st.unsqueeze(2).to_broadcast([P, HEADS, KEYS]), ALU.subtract)\
                      .then_inc(shifted, 1)
                for i in range(TPB):
                    n = b * TPB + i
                    st = stat[:, i, :]
                    dve.wait_ge(exp_done, n + 1)
                    vv.tensor_reduce(st, probs[:, i, :, :], AX.X, ALU.add)
                    dve.drain()
                    vv.reciprocal(st, st)
                    dve.drain()
                    dve.wait_ge(mixed_ready, n + 1)
                    split = [P, HEADS, DH]
                    mixed_ps = Q[:, 0, :].rearrange("p (h d) -> p h d", d=DH)
                    norm = st.unsqueeze(2).to_broadcast(split)
                    if final_layer:
                        vv.tensor_tensor(c.ACC[:, pieces(n), :].rearrange("p a (h d) -> p (a h) d", d=DH), mixed_ps,
                                         norm, ALU.mult).then_inc(out_done, 1)
                    else:
                        vv.tensor_tensor(mixed[:, :].rearrange("p (h d) -> p h d", d=DH), mixed_ps, norm, ALU.mult)
                        dve.drain()
                        vv.tensor_tensor(mixed[:, :], mixed[:, :], bv[:, :], ALU.add).then_inc(mixed_done, 1)
                        dve.wait_ge(out_ready, n + 1)
                        vv.tensor_tensor(c.ACC[:, pieces(n), :], Q[:, 0, :].unsqueeze(1), bo[:, :].unsqueeze(1),
                                         ALU.add).then_inc(out_done, 1)

            batches(dve, body)


def adapter_layer(nc, c, a):
    E, H = 8, 64
    PAIR = P // H
    M = E // PAIR
    with ExitStack() as ctx:
        sb, ps, sem = sub_memory(nc, ctx, "f2_")
        w_base = sb("w_base", [P, DK, DIM])
        w_in = sb("w_in", [P, 2, DK, E, H])
        w_out = sb("w_out", [P, 2, M, DIM])
        b_in = sb("b_in", [P, 2, M])
        b_recon = sb("b_recon", [P, E, DK])
        b_base = sb("b_base", [P, DIM])
        b_up = sb("b_up", [E, DIM])
        hidden = sb("hidden", [P, 2, M, BLOCK])
        diff = sb("diff", [P, 2, BLOCK])
        losses = sb("losses", [P, BATCH, E * DK])
        loss = sb("loss", [P, BATCH, E])
        least = sb("least", [P, BATCH])
        pick = sb("pick", [P, BATCH, E])
        pick_rows = sb("pick_rows", [E, BATCH])
        pick_wide = sb("pick_wide", [E, BATCH, P])
        scale = sb("scale", [P, M, BATCH])
        shift = sb("shift", [P, M, BATCH])
        ones = sb("ones", [P, P])
        hid_ps = [ps(f"hid{i}", [P, BLOCK]) for i in range(2)]
        rec_ps = [ps(f"rec{i}", [P, BLOCK]) for i in range(2)]
        out_ps = [ps(f"out{i}", [P, BLOCK]) for i in range(2)]
        loss_ps = ps("loss_ps", [P, BATCH, E * DK])
        loaded = sem("loaded")
        hid_ready, hid_done = sem("hid_ready"), sem("hid_done")
        rec_ready, rec_free = sem("rec_ready"), sem("rec_free")
        squared = sem("squared")
        ones_ready, loss_ready, picked = sem("ones_ready"), sem("loss_ready"), sem("picked")
        out_ready, out_done = sem("out_ready"), sem("out_done")
        block = ctx.enter_context(nc.Block())
        SB = BLOCK // SEQ
        RECS = E * DK

        @block.sync
        def _(sp):
            with nc.allow_non_contiguous_dma("small biases"):
                for n, w in enumerate(("L2_ffn_Wd1", "L2_ffn_Wa_down")):
                    for kk in range(DK):
                        sp.dma_start(w_in[:, n, kk, :, :],
                                     a[w][:, kk * P:(kk + 1) * P, :].rearrange("e p h -> p e h")).then_inc(loaded, 16)
                for n, w in enumerate(("L2_ffn_Wd2", "L2_ffn_Wa_up")):
                    sp.dma_start(w_out[:, n, :, :], a[w].rearrange("(m a) h d -> (a h) m d", a=PAIR))\
                      .then_inc(loaded, 16)
                sp.dma_start(b_in[:, 0, :], a["L2_bd1"]).then_inc(loaded, 16)
                sp.dma_start(b_in[:, 1, :], a["L2_ba_down"]).then_inc(loaded, 16)
                sp.dma_start(b_recon[:, :, :], a["L2_bd2"]).then_inc(loaded, 16)
                sp.dma_start(w_base[:, :, :], a["L2_ffn_W_base"].rearrange("(k p) n -> p k n", p=P)).then_inc(loaded, 16)
                sp.dma_start(b_base[:, :], spread(a["L2_ffn_b_base"])).then_inc(loaded, 16)
                sp.dma_start(b_up[:, :], a["L2_ffn_ba_up"]).then_inc(loaded, 16)
        LOADS = 12 * 16

        @block.tensor
        def _(pe):
            def hidden_block(g, u, which, columns):
                n = g * 2 + (u + which * BLOCKS)
                for m in range(M):
                    pe.wait_ge(hid_done, n * M + (m + 1))
                    for kk in range(DK):
                        last = nc.tensor.matmul(hid_ps[m % 2][:, :],
                                                w_in[:, which, kk, m * PAIR:(m + 1) * PAIR, :]
                                                .rearrange("p e h -> p (e h)"),
                                                c.XT[:, kk, columns], start=kk == 0, stop=kk == DK - 1)
                    last.then_inc(hid_ready, 1)

            pe.wait_ge(loaded, LOADS)
            with pe.Fori(0, BLOCKS // 2) as g:
                for u in range(2):
                    hidden_block(g, u, 0, pieces(g * (2 * BLOCK) + u * BLOCK, BLOCK))
                    pe.wait_ge(hid_done, g * (2 * M) + (u * M + M + 2))
                    for e in range(E):
                        rows = slice((e % PAIR) * H, (e % PAIR + 1) * H)
                        for m in range(DK):
                            r = e * DK + m
                            pe.wait_ge(rec_free, g * (2 * RECS) + (u * RECS + r + 1))
                            nc.tensor.matmul(rec_ps[r % 2][:, :], w_out[rows, 0, e // PAIR, m * P:(m + 1) * P],
                                             hidden[rows, u, e // PAIR, :], start=True, stop=True)\
                              .then_inc(rec_ready, 1)
            pe.wait_ge(squared, BLOCKS * RECS + 2)
            pe.wait_ge(ones_ready, 1)
            nc.tensor.matmul(loss_ps[:, :, :].rearrange("p b r -> p (b r)"), ones[:, :],
                             losses[:, :, :].rearrange("p b r -> p (b r)"), start=True, stop=True)\
              .then_inc(loss_ready, 1)
            pe.wait_ge(picked, 1)
            for blk in range(BLOCKS):
                hidden_block(blk // 2, blk % 2, 1, slice(blk * BLOCK, (blk + 1) * BLOCK))
                pe.wait_ge(hid_done, (BLOCKS + blk + 1) * M + 2)
                for i in range(TPK):
                    t = blk * TPK + i
                    pe.wait_ge(out_done, t + 1)
                    o = out_ps[t % 2][:, 0:DIM]
                    for kk in range(DK):
                        nc.tensor.matmul(o, c.XT[:, kk, t * P:(t + 1) * P], w_base[:, kk, :], start=kk == 0, stop=False)
                    for m in range(M):
                        nc.tensor.matmul(o, hidden[:, blk % 2, m, i * P:(i + 1) * P], w_out[:, 1, m, :], start=False,
                                         stop=False)
                    nc.tensor.matmul(o, pick_wide[:, t // TPB, :], b_up[:, :], start=False, stop=True)\
                      .then_inc(out_ready, 1)

        @block.scalar
        def _(act):
            act.sem_inc(hid_done, 2)
            act.sem_inc(squared, 2)
            act.wait_ge(loaded, LOADS)
            with act.Fori(0, BLOCKS // 2) as g:
                for u in range(2):
                    for m in range(M):
                        act.wait_ge(hid_ready, g * (2 * M) + (u * M + m + 1))
                        nc.scalar.activation(hidden[:, u, m, :], hid_ps[m % 2][:, :], ACT.Relu,
                                             bias=b_in[:, 0, m:m + 1]).then_inc(hid_done, 1)
                    for r in range(RECS):
                        act.wait_ge(rec_free, g * (2 * RECS) + (u * RECS + r + 3))
                        for s in range(SB):
                            b = g * (2 * SB) + (u * SB + s)
                            last = nc.scalar.activation(diff[:, r % 2, s * SEQ:(s + 1) * SEQ],
                                                        diff[:, r % 2, s * SEQ:(s + 1) * SEQ], ACT.Square,
                                                        accum_out=losses[:, pieces(b), r])
                        last.then_inc(squared, 1)
            act.wait_ge(picked, 1)
            for blk in range(BLOCKS):
                if blk >= 2:
                    act.wait_ge(out_ready, (blk - 1) * TPK)
                for m in range(M):
                    act.wait_ge(hid_ready, (BLOCKS + blk) * M + m + 1)
                    for s in range(SB):
                        b = blk * SB + s
                        cols = slice(s * SEQ, (s + 1) * SEQ)
                        last = nc.scalar.activation(hidden[:, blk % 2, m, cols], hid_ps[m % 2][:, cols], ACT.Relu,
                                                    bias=shift[:, m, b:b + 1], scale=scale[:, m, b:b + 1])
                    last.then_inc(hid_done, 1)

        @block.vector
        def _(dve):
            v = nc.vector
            dve.sem_inc(rec_free, 2)
            dve.sem_inc(out_done, 2)
            v.memset(ones[:, :], 1.0).then_inc(ones_ready, 1)
            dve.wait_ge(loaded, LOADS)
            with dve.Fori(0, BLOCKS // 2) as g:
                for u in range(2):
                    columns = pieces(g * (2 * BLOCK) + u * BLOCK, BLOCK)
                    for e in range(E):
                        for m in range(DK):
                            r = e * DK + m
                            dve.wait_ge(rec_ready, g * (2 * RECS) + (u * RECS + r + 1))
                            dve.wait_ge(squared, g * (2 * RECS) + (u * RECS + r + 1))
                            v.scalar_tensor_tensor(diff[:, r % 2, :], rec_ps[r % 2][:, :], b_recon[:, e, m:m + 1],
                                                   c.XT[:, m, columns], ALU.add, ALU.subtract).then_inc(rec_free, 1)
            dve.wait_ge(loss_ready, 1)
            wide = [P, BATCH, E]

            def tt(*args):
                v.tensor_tensor(*args)
                dve.drain()

            v.tensor_reduce(loss[:, :, :], loss_ps[:, :, :].rearrange("p b (e m) -> p b e m", m=DK), AX.X, ALU.add)
            dve.drain()
            v.tensor_reduce(least[:, :], loss[:, :, :], AX.X, ALU.min)
            dve.drain()
            iota = c.iota8[:, 0:E].unsqueeze(1).to_broadcast(wide)
            tt(pick[:, :, :], loss[:, :, :], least[:, :].unsqueeze(2).to_broadcast(wide), ALU.is_gt)
            v.scalar_tensor_tensor(pick[:, :, :], pick[:, :, :], float(E), iota, ALU.mult, ALU.add)
            dve.drain()
            v.tensor_reduce(least[:, :], pick[:, :, :], AX.X, ALU.min)
            dve.drain()
            tt(pick[:, :, :], iota, least[:, :].unsqueeze(2).to_broadcast(wide), ALU.is_equal)
            for half in range(PAIR):
                rows = slice(half * H, (half + 1) * H)
                v.tensor_copy(scale[rows, :, :], pick[rows, :, half:E:PAIR].rearrange("p b m -> p m b"))
            dve.drain()
            tt(shift[:, :, :], scale[:, :, :], b_in[:, 1, :].unsqueeze(2).to_broadcast([P, M, BATCH]), ALU.mult)
            tt(loss[0:E, :, :], pick[0:E, :, :], c.ident[0:E, 0:E].unsqueeze(1).to_broadcast([E, BATCH, E]), ALU.mult)
            v.tensor_reduce(pick_rows[:, :], loss[0:E, :, :], AX.X, ALU.add)
            dve.drain()
            v.tensor_copy(pick_wide[:, :, :], pick_rows[:, :].unsqueeze(2).to_broadcast([E, BATCH, P]))
            dve.drain()
            dve.sem_inc(picked, 1)
            for t in range(TILES):
                dve.wait_ge(out_ready, t + 1)
                v.tensor_tensor(c.ACC[:, t, :], out_ps[t % 2][:, 0:DIM], b_base[:, :], ALU.add).then_inc(out_done, 1)
            dve.drain()


def state_space_kernel(nc, c, a, KA, KB, KC):
    N, J, S = 64, 128, 16
    CH = 16
    CHUNKS = J // CH
    TWO_PI = 2 * np.pi
    C1 = 6.28125
    C2 = float(np.float32(TWO_PI - C1) .view(np.int32).__and__(-4096).view(np.float32))
    C3 = float(TWO_PI - C1 - C2)
    LN2_HI = 0.693359375
    LN2_LO = float(np.log(2.0) - LN2_HI)
    with ExitStack() as ctx:
        sb, ps, sem = sub_memory(nc, ctx, "ss_")
        small = {n: sb(n, [P, J]) for n in ("are", "aim", "cre", "cim", "ldt", "dt", "theta", "rho", "er", "ei",
                                            "t0", "t1", "t2", "dcr", "dci", "cos0", "sin0")}
        bits = sb("bits", [P, J], I32)
        steps = sb("steps", [P, 2 * S])
        big = {n: sb(n, [P, J, S]) for n in ("qr", "qi", "w")}
        halves = [t[:, :, :].rearrange("p t d -> p (t d)")[:, h * J * S:(h + 1) * J * S]
                  for t in (c.XN, c.XT, c.ACC) for h in range(2)]
        for n, part in zip(("phase", "turns", "mag", "pr", "pi", "u"), halves):
            big[n] = part.rearrange("p (j s) -> p j s", s=S)
        slot = sb("slot", [P, 2, 4, CH, S])
        d_skip = sb("d_skip", [1, DIM])
        k_sb = sb("k_sb", [S, S, DIM])
        fwd = sb("fwd", [S, S, 2 * SEQ])
        k_ps = [[ps(f"k{u}{h}", [S, CH, S]) for h in range(2)] for u in range(2)]
        f_ps = [ps(f"f{i}", [P, DIM]) for i in range(4)]
        loaded, asked, answered = sem("loaded"), sem("asked"), sem("answered")
        slot_ready, k_ready, k_free = sem("slot_ready"), sem("k_ready"), sem("k_free")
        k_whole, f_ready, begun = sem("k_whole"), sem("f_ready"), sem("begun")
        block = ctx.enter_context(nc.Block())

        @block.sync
        def _(sp):
            for n, k in (("are", "A_re"), ("aim", "A_im"), ("cre", "C_re"), ("cim", "C_im")):
                sp.dma_start(small[n][:, :], a["S_" + k]).then_inc(loaded, 16)
            for h in range(2):
                sp.dma_start(small["ldt"][h * N:(h + 1) * N, :],
                             a["L0_xattn_log_dt"][h * J:(h + 1) * J].partition_broadcast(N)).then_inc(loaded, 16)
            sp.dma_start(steps[:, :], a["steps"]).then_inc(loaded, 16)
            sp.dma_start(d_skip[:, :], row(a["L0_xattn_D_skip"])).then_inc(loaded, 16)
            sp.dma_start(fwd[:, :, :], a["fwd"].rearrange("(a b) f -> b a f", b=S)).then_inc(loaded, 16)

        @block.vector
        def _(dve):
            v = nc.vector

            def tt(*args):
                v.tensor_tensor(*args)
                dve.drain()

            def ts(*args):
                v.tensor_scalar(*args)
                dve.drain()

            def stt(*args):
                v.scalar_tensor_tensor(*args)
                dve.drain()

            def ask(n, done):
                dve.sem_inc(asked, 1)
                dve.wait_ge(answered, done)

            def reduce_angle(x, k):
                ts(k, x, 1.0 / TWO_PI, MAGIC, ALU.mult, ALU.add)
                ts(k, k, MAGIC, None, ALU.subtract)
                for part in (C1, C2, C3):
                    stt(x, k, -part, x, ALU.mult, ALU.add)
                ts(x, x, 3.1415925, -3.1415925, ALU.min, ALU.max)

            m = {n: t[:, :] for n, t in small.items()}
            dve.wait_ge(loaded, 9 * 16)
            ts(m["t0"], m["ldt"], float(1 / np.log(2.0)), MAGIC, ALU.mult, ALU.add)
            ts(m["t0"], m["t0"], MAGIC, -126.0, ALU.subtract, ALU.max)
            stt(m["t1"], m["t0"], -LN2_HI, m["ldt"], ALU.mult, ALU.add)
            stt(m["t1"], m["t0"], -LN2_LO, m["t1"], ALU.mult, ALU.add)
            coefs = [1.0 / 5040, 1.0 / 720, 1.0 / 120, 1.0 / 24, 1.0 / 6, 0.5, 1.0]
            ts(m["t2"], m["t1"], coefs[0], None, ALU.mult)
            for co in coefs[1:]:
                stt(m["t2"], m["t2"], co, m["t1"], ALU.add, ALU.mult)
            ts(bits[:, :], m["t0"], 127.0, 8388608.0, ALU.add, ALU.mult)
            stt(m["dt"], m["t2"], 1.0, bits[:, :].bitcast(F32), ALU.add, ALU.mult)
            tt(m["theta"], m["dt"], m["aim"], ALU.mult)
            tt(m["rho"], m["dt"], m["are"], ALU.mult)
            v.tensor_copy(m["t0"], m["theta"])
            dve.drain()
            reduce_angle(m["t0"], m["t1"])
            ask(1, 3)
            tt(m["cos0"], m["cos0"], m["cos0"], ALU.mult)
            ts(m["t1"], m["t0"], -1.0, 1.0, ALU.mult, ALU.add)
            v.reciprocal(m["t1"], m["t1"])
            dve.drain()
            stt(m["t0"], m["t0"], 2.0, m["t1"], ALU.mult, ALU.mult)
            ts(m["t1"], m["cos0"], -2.0, None, ALU.mult)
            stt(m["er"], m["t1"], 1.0, m["t0"], ALU.add, ALU.mult)
            tt(m["er"], m["er"], m["t1"], ALU.add)
            stt(m["ei"], m["t0"], 1.0, m["sin0"], ALU.add, ALU.mult)
            tt(m["t0"], m["cre"], m["er"], ALU.mult)
            tt(m["t1"], m["cim"], m["ei"], ALU.mult)
            tt(m["t0"], m["t0"], m["t1"], ALU.subtract)
            tt(m["t1"], m["cre"], m["ei"], ALU.mult)
            tt(m["t2"], m["cim"], m["er"], ALU.mult)
            tt(m["t1"], m["t1"], m["t2"], ALU.add)
            tt(m["er"], m["are"], m["are"], ALU.mult)
            tt(m["ei"], m["aim"], m["aim"], ALU.mult)
            tt(m["er"], m["er"], m["ei"], ALU.add)
            v.reciprocal(m["er"], m["er"])
            dve.drain()
            for out, x, y, op in (("dcr", "t0", "t1", ALU.add), ("dci", "t1", "t0", ALU.subtract)):
                tt(m[out], m[x], m["are"], ALU.mult)
                tt(m["t2"], m[y], m["aim"], ALU.mult)
                tt(m[out], m[out], m["t2"], op)
                stt(m[out], m[out], 2.0, m["er"], ALU.mult, ALU.mult)
            b = {n: t[:, :, :] for n, t in big.items()}
            wide = [P, J, S]
            for f, re, im in ((0, "qr", "qi"), (1, "pr", "pi")):
                at = steps[:, f * S:(f + 1) * S].unsqueeze(1).to_broadcast(wide)
                tt(b["phase"], m["theta"].unsqueeze(2).to_broadcast(wide), at, ALU.mult)
                tt(b["mag"], m["rho"].unsqueeze(2).to_broadcast(wide), at, ALU.mult)
                reduce_angle(b["phase"], b["turns"])
                ask(2 + f, 6 + 3 * f)
                tt(b[re], b[re], b[re], ALU.mult)
                ts(b[re], b[re], -2.0, 1.0, ALU.mult, ALU.add)
                tt(b[re], b[re], b["mag"], ALU.mult)
                tt(b[im], b[im], b["mag"], ALU.mult)
            dcr, dci = (m[n].unsqueeze(2).to_broadcast(wide) for n in ("dcr", "dci"))
            tt(b["u"], b["pr"], dcr, ALU.mult)
            tt(b["w"], b["pi"], dci, ALU.mult)
            tt(b["u"], b["u"], b["w"], ALU.subtract)
            tt(b["pr"], b["pr"], dci, ALU.mult)
            tt(b["pi"], b["pi"], dcr, ALU.mult)
            stt(b["w"], b["pr"], -1.0, b["pi"], ALU.mult, ALU.subtract)
            with dve.Fori(0, CHUNKS // 2) as g:
                for u in range(2):
                    dve.wait_ge(k_ready, g * 2 + u + 1)
                    for n, x in enumerate(("qr", "qi", "u", "w")):
                        last = v.tensor_copy(slot[:, u, n, :, :], big[x][:, pieces(g * (2 * CH) + u * CH, CH), :])
                    last.then_inc(slot_ready, 1)
            dve.wait_ge(k_free, CHUNKS + 2)
            v.tensor_tensor(k_sb[0:1, 0, :], k_sb[0:1, 0, :], d_skip[:, :], ALU.add).then_inc(k_whole, 1)
            dve.wait_ge(f_ready, 4)
            for h in range(2):
                v.tensor_copy(KA[:, h, :], f_ps[h][:, :])
                v.tensor_copy(KC[:, h, :], f_ps[h][:, :])
                v.tensor_copy(KB[:, h, :], f_ps[2 + h][:, :])
            dve.drain()
            v.tensor_copy(KC[0:1, 0, :], f_ps[2][0:1, :])
            v.memset(KB[0:1, 0, :], 0.0)
            dve.drain()

        @block.scalar
        def _(act):
            act.sem_inc(k_free, 2)
            act.wait_ge(loaded, 9 * 16)
            act.wait_ge(asked, 1)
            s = {n: t[:, :] for n, t in small.items()}
            nc.scalar.activation(s["sin0"], s["t0"], ACT.Sin).then_inc(answered, 1)
            nc.scalar.activation(s["cos0"], s["t0"], ACT.Sin, scale=0.5).then_inc(answered, 1)
            act.wait_ge(answered, 2)
            nc.scalar.activation(s["t0"], s["rho"], ACT.Tanh, scale=0.5).then_inc(answered, 1)
            for f, re, im in ((0, "qr", "qi"), (1, "pr", "pi")):
                act.wait_ge(asked, 2 + f)
                nc.scalar.activation(big[im][:, :, :], big["phase"][:, :, :], ACT.Sin).then_inc(answered, 1)
                nc.scalar.activation(big[re][:, :, :], big["phase"][:, :, :], ACT.Sin, scale=0.5).then_inc(answered, 1)
                nc.scalar.activation(big["mag"][:, :, :], big["mag"][:, :, :], ACT.Exp).then_inc(answered, 1)
            with act.Fori(0, CHUNKS // 2) as g:
                for u in range(2):
                    act.wait_ge(k_ready, g * 2 + u + 3)
                    for h in range(2):
                        last = nc.scalar.activation(k_sb[:, :, pieces(g * (2 * CH) + (u * CH + h * J), CH)],
                                                    k_ps[u][h][:, :, :].rearrange("b j a -> b a j"), ACT.Copy)
                    last.then_inc(k_free, 1)

        @block.tensor
        def _(pe):
            pe.sem_inc(k_ready, 2)
            with pe.Fori(0, CHUNKS // 2) as g:
                for u in range(2):
                    pe.wait_ge(slot_ready, g * 2 + u + 1)
                    pe.wait_ge(k_free, g * 2 + u + 1)
                    pe.sem_inc(begun, 1)
                    for j in range(CH):
                        for h in range(2):
                            r = slice(h * N, (h + 1) * N)
                            nc.tensor.matmul(k_ps[u][h][:, j, :], slot[r, u, 0, j, :], slot[r, u, 2, j, :],
                                             start=True, stop=False)
                            last = nc.tensor.matmul(k_ps[u][h][:, j, :], slot[r, u, 1, j, :], slot[r, u, 3, j, :],
                                                    start=False, stop=True)
                    last.then_inc(k_ready, 1)
            pe.wait_ge(k_whole, 1)
            pe.wait_ge(loaded, 9 * 16)
            for f in range(4):
                for s in range(S):
                    last = nc.tensor.matmul(f_ps[f][:, :], fwd[:, s, f * P:(f + 1) * P], k_sb[:, s, :],
                                            start=s == 0, stop=s == S - 1)
                last.then_inc(f_ready, 1)


def film_attention(nc, c, a, X2, FO):
    HEADS, DH, TOP = 4, 32, 32
    SCALE = float(1.0 / np.sqrt(np.float32(DH)))
    with ExitStack() as ctx:
        sb, ps, sem = sub_memory(nc, ctx, "a0_")
        wq = sb("wq", [P, DK, P])
        wk = sb("wk", [CP, CK, P])
        wv = sb("wv", [CP, CK, DIM])
        wf = sb("wf", [P, 2, DK, 2 * DIM])
        bf = sb("bf", [P, 2, 2 * DIM])
        mod = sb("mod", [P, 1])
        context = sb("context", [CP, 2, CK, KEYS])
        mask8 = sb("mask8", [P, TILES], U8)
        share = sb("share", [P, TILES])
        key_mask8 = sb("key_mask8", [P, BATCH, KEYS], U8)
        key_fill = sb("key_fill", [P, BATCH, KEYS])
        q = sb("q", [P, SEQ])
        k_wide = sb("k_wide", [P, HEADS, KEYS])
        v = sb("v", [KEYS, 2, DIM])
        score = sb("score", [P, TPB, HEADS, KEYS])
        rest = sb("rest", [P, TPB, HEADS, KEYS])
        top = sb("top", [P, TPB, HEADS, 8])
        top_n = sb("top_n", [P, TPB, HEADS, 8])
        stat = sb("stat", [P, TPB, HEADS])
        mean = sb("mean", [P, TPB, KEYS])
        mean_t = sb("mean_t", [KEYS, SEQ])
        ct = sb("ct", [P, DK, SEQ])
        film = sb("film", [P, 2, 2 * DIM])
        Q = ps("q_ps", [P, SEQ])
        KV = ps("kv_ps", [P, 512])
        S = [ps(f"s{i}", [P, HEADS * KEYS]) for i in range(TPB)]
        T = ps("t", [KEYS, SEQ])
        CT = ps("ct_ps", [P, DK, SEQ])
        F = [ps(f"f{i}", [P, 2 * DIM]) for i in range(2)]
        w_loaded = sem("w_loaded")
        ctx_loaded = [sem(f"ctx_loaded{u}") for u in range(2)]
        setup_done = sem("setup_done")
        qkv_ready, q_done, kv_done = sem("qkv_ready"), sem("q_done"), sem("kv_done")
        scores_ready, scores_read = sem("scores_ready"), sem("scores_read")
        shifted, exp_done = sem("shifted"), sem("exp_done")
        mean_ready, turned, turned_done = sem("mean_ready"), sem("turned"), sem("turned_done")
        ct_ready, ct_done = sem("ct_ready"), sem("ct_done")
        film_ready, film_done = sem("film_ready"), sem("film_done")
        block = ctx.enter_context(nc.Block())
        LOADS = 16 * 10

        def batches(eng, body):
            with eng.Fori(0, BATCH // 2 - 1) as g:
                for u in range(2):
                    body(g * 2 + u, u, False)
            for b in range(BATCH - 2, BATCH):
                body(b, b % 2, b == BATCH - 1)

        @block.sync
        def _(sp):
            def load(b, u):
                sp.dma_start(context[:, u, :, :].unsqueeze(1),
                             a["context_T"][pieces(b), :, :].rearrange("b (k p) s -> p b k s", p=CP))\
                  .then_inc(ctx_loaded[u], 16)

            load(0, 0)
            load(1, 1)
            for dst, src, p in ((wq, "Wq", P), (wk, "Wk", CP), (wv, "Wv", CP)):
                sp.dma_start(dst[:, :, :], a["L0_xattn_" + src].rearrange("(k p) n -> p k n", p=p)).then_inc(w_loaded, 16)
            for n, way in enumerate(("in", "out")):
                sp.dma_start(wf[:, n, :, :], a["L0_xattn_W_film_" + way].rearrange("(k p) n -> p k n", p=P))\
                  .then_inc(w_loaded, 16)
                sp.dma_start(bf[:, n, :], spread(a["L0_xattn_b_film_" + way])).then_inc(w_loaded, 16)
            sp.dma_start(mod[:, :], spread(a["L0_xattn_mod_gate"])).then_inc(w_loaded, 16)
            sp.dma_start(mask8[:, :], a["mask_BxS_bf1"]).then_inc(w_loaded, 16)
            sp.dma_start(key_mask8[:, :, :], a["mask_BxS2_bf1"].partition_broadcast(P)).then_inc(w_loaded, 16)
            with sp.Fori(1, BATCH // 2) as g:
                for u in range(2):
                    sp.wait_ge(qkv_ready, g * 2 + (u - 1))
                    load(g * 2 + u, u)

        @block.tensor
        def _(pe):
            def project(b, u):
                pe.wait_ge(q_done, b + 1)
                pe.wait_ge(kv_done, b + 1)
                for kk in range(DK):
                    nc.tensor.matmul(Q[:, :], wq[:, kk, :], c.XT[:, kk, pieces(b * SEQ, SEQ)], start=kk == 0,
                                     stop=kk == DK - 1)
                pe.wait_ge(ctx_loaded[u], (b // 2 + 1) * 16 if isinstance(b, int) else b * 8 + (16 - 8 * u))
                for kk in range(CK):
                    nc.tensor.matmul(KV[:, 0:KEYS], wk[:, kk, :], context[:, u, kk, :], start=kk == 0,
                                     stop=kk == CK - 1)
                for kk in range(CK):
                    last = nc.tensor.matmul(KV[0:KEYS, DIM:2 * DIM], context[:, u, kk, :], wv[:, kk, :],
                                            start=kk == 0, stop=kk == CK - 1)
                last.then_inc(qkv_ready, 1)

            def body(b, u, final):
                pe.wait_ge(q_done, b + 2)
                pe.wait_ge(kv_done, b + 2)
                pe.wait_ge(scores_read, b + 1)
                for i in range(TPB):
                    last = nc.tensor.matmul(S[i][:, :], q[:, i * P:(i + 1) * P],
                                            k_wide[:, :, :].rearrange("p h s -> p (h s)"), start=True, stop=True)
                last.then_inc(scores_ready, 1)
                if not final:
                    project(b + 1, 1 - u)
                pe.wait_ge(mean_ready, b + 1)
                for i in range(TPB):
                    last = nc.tensor.transpose(T[:, i * P:(i + 1) * P], mean[:, i, :], c.ident[:, :])
                last.then_inc(turned, 1)
                pe.wait_ge(turned_done, b + 1)
                for m in range(DK):
                    last = nc.tensor.matmul(CT[:, m, :], v[:, u, m * P:(m + 1) * P], mean_t[:, :], start=True,
                                            stop=True)
                last.then_inc(ct_ready, 1)
                pe.wait_ge(ct_done, b + 1)
                for i in range(TPB):
                    for way in range(2):
                        pe.wait_ge(film_done, b * (2 * TPB) + (2 * i + way + 1))
                        for m in range(DK):
                            last = nc.tensor.matmul(F[way][:, :], ct[:, m, i * P:(i + 1) * P], wf[:, way, m, :],
                                                    start=m == 0, stop=m == DK - 1)
                        last.then_inc(film_ready, 1)

            pe.wait_ge(w_loaded, LOADS)
            project(0, 0)
            batches(pe, body)

        @block.scalar
        def _(act):
            act.sem_inc(q_done, 1)

            def evacuate(b, u):
                act.wait_ge(qkv_ready, b + 1)
                nc.scalar.activation(q[:, :], Q[:, :], ACT.Copy).then_inc(q_done, 1)

            def body(b, u, final):
                if not final:
                    act.wait_ge(scores_ready, b + 1)
                    evacuate(b + 1, 1 - u)
                act.wait_ge(shifted, b + 1)
                nc.scalar.activation(score[:, :, :, :], score[:, :, :, :], ACT.Exp).then_inc(exp_done, 1)
                act.wait_ge(turned, b + 1)
                nc.scalar.activation(mean_t[:, :], T[:, :], ACT.Copy).then_inc(turned_done, 1)
                act.wait_ge(ct_ready, b + 1)
                nc.scalar.activation(ct[:, :, :], CT[:, :, :], ACT.Copy).then_inc(ct_done, 1)

            evacuate(0, 0)
            batches(act, body)

        @block.vector
        def _(dve):
            vv = nc.vector
            dve.sem_inc(kv_done, 1)
            dve.sem_inc(scores_read, 1)
            dve.sem_inc(film_done, 2)
            dve.wait_ge(w_loaded, LOADS)
            vv.tensor_copy(share[:, :], mask8[:, :])
            vv.tensor_copy(key_fill[:, :, :], key_mask8[:, :, :])
            for way in range(2):
                vv.tensor_scalar(bf[:, way, :], bf[:, way, :], mod[:, 0:1], None, ALU.mult)
            dve.drain()
            vv.tensor_scalar(share[:, :], share[:, :], 1.0 / HEADS, None, ALU.mult)
            vv.tensor_scalar(key_fill[:, :, :], key_fill[:, :, :], 1.0, 1.0e30, ALU.subtract, ALU.mult)
            for way in range(2):
                vv.tensor_scalar(bf[:, way, 0:DIM], bf[:, way, 0:DIM], 1.0, None, ALU.add)
            dve.drain()

            def widen(b, u):
                wide = [P, HEADS, KEYS]
                dve.wait_ge(qkv_ready, b + 1)
                vv.tensor_tensor(k_wide[:, :, :], KV[:, 0:KEYS].unsqueeze(1).to_broadcast(wide),
                                 c.headmask[:, 0:HEADS].unsqueeze(2).to_broadcast(wide), ALU.mult)
                vv.tensor_copy(v[:, u, :], KV[0:KEYS, DIM:2 * DIM]).then_inc(kv_done, 1)

            def body(b, u, final):
                dve.wait_ge(scores_ready, b + 1)
                fill = key_fill[:, pieces(b), :].to_broadcast([P, HEADS, KEYS])
                for i in range(TPB):
                    last = vv.scalar_tensor_tensor(score[:, i, :, :], S[i][:, :].rearrange("p (h s) -> p h s", s=KEYS),
                                                   SCALE, fill, ALU.mult, ALU.add)
                last.then_inc(scores_read, 1)
                if not final:
                    widen(b + 1, 1 - u)
                dve.drain()
                for r in range(TOP // 8):
                    src, t8 = (score, top) if r == 0 else (rest, top_n)
                    for i in range(TPB):
                        for h in range(HEADS):
                            vv.max(t8[:, i, h, :], src[:, i, h, :])
                    dve.drain()
                    for i in range(TPB):
                        for h in range(HEADS):
                            vv.match_replace(rest[:, i, h, :], t8[:, i, h, :], src[:, i, h, :], NEG)
                    dve.drain()
                rows = [P, TPB * HEADS, KEYS]
                s3 = score[:, :, :, :].rearrange("p i h s -> p (i h) s")
                st = stat[:, :, :].rearrange("p i h -> p (i h)")
                vv.tensor_tensor(s3, s3, top[:, :, :, 0].rearrange("p i h -> p (i h)").unsqueeze(2).to_broadcast(rows),
                                 ALU.subtract).then_inc(shifted, 1)
                dve.wait_ge(exp_done, b + 1)
                flat = "p i h s -> p (i h s)"
                vv.scalar_tensor_tensor(score[:, :, :, :].rearrange(flat), rest[:, :, :, :].rearrange(flat), NEG,
                                        score[:, :, :, :].rearrange(flat), ALU.is_equal, ALU.mult)
                dve.drain()
                vv.tensor_reduce(st, s3, AX.X, ALU.add)
                dve.drain()
                vv.reciprocal(st, st)
                dve.drain()
                for i in range(TPB):
                    vv.tensor_scalar(stat[:, i, :], stat[:, i, :], share[:, pieces(b * TPB + i)], None, ALU.mult)
                dve.drain()
                vv.tensor_tensor(s3, s3, st.unsqueeze(2).to_broadcast(rows), ALU.mult)
                dve.drain()
                for i in range(TPB):
                    last = vv.tensor_reduce(mean[:, i, :], score[:, i, :, :].rearrange("p h s -> p s h"), AX.X, ALU.add)
                last.then_inc(mean_ready, 1)
                for i in range(TPB):
                    t = b * TPB + i
                    dve.wait_ge(film_ready, b * (2 * TPB) + (2 * i + 1))
                    vv.scalar_tensor_tensor(film[:, i, :], F[0][:, :], mod[:, 0:1], bf[:, 0, :], ALU.mult, ALU.add)\
                      .then_inc(film_done, 1)
                    dve.wait_ge(film_ready, b * (2 * TPB) + (2 * i + 2))
                    vv.scalar_tensor_tensor(FO[:, pieces(t), :].rearrange("p a n -> p (a n)"), F[1][:, :], mod[:, 0:1],
                                            bf[:, 1, :], ALU.mult, ALU.add).then_inc(film_done, 1)
                dve.drain()
                x = X2[:, pieces(b * TPB, TPB), :]
                vv.tensor_tensor(x, x, film[:, :, 0:DIM], ALU.mult)
                dve.drain()
                vv.tensor_tensor(x, x, film[:, :, DIM:2 * DIM], ALU.add)

            widen(0, 0)
            batches(dve, body)
            dve.drain()


def convolve(nc, c, a, X2, FO, KA, KB, KC):
    PAIRS = BATCH // 2
    TPP = 2 * TPB
    with ExitStack() as ctx:
        sb, ps, sem = sub_memory(nc, ctx, "cv_")
        fwd = sb("fwd", [P, TPB, 2 * SEQ])
        back = sb("back", [P, 4, SEQ])
        prod = sb("prod", [P, 2, 4, 2 * DIM])
        spec = sb("spec", [P, 2, 2, 2 * DIM])
        y = sb("y", [P, TPP, DIM])
        f_ps = [[ps(f"f{part}{h}", [P, 2, DIM]) for h in range(2)] for part in range(2)]
        y_ps = [ps(f"y{i}", [P, 2, DIM]) for i in range(TPB)]
        loaded, f_ready, f_done = sem("loaded"), sem("f_ready"), sem("f_done")
        prod_ready, spec_ready = sem("prod_ready"), sem("spec_ready")
        y_ready, y_done = sem("y_ready"), sem("y_done")
        block = ctx.enter_context(nc.Block())

        @block.sync
        def _(sp):
            sp.dma_start(fwd[:, :, :], a["fwd"].rearrange("(i p) f -> p i f", p=P)).then_inc(loaded, 16)
            sp.dma_start(back[:, :, :], a["back"].rearrange("(i p) l -> p i l", p=P)).then_inc(loaded, 16)

        @block.tensor
        def _(pe):
            pe.wait_ge(loaded, 32)
            with pe.Fori(0, PAIRS) as g:
                for h in range(2):
                    pe.wait_ge(f_done, g * 2 + h + 1)
                    for part in range(2):
                        for i in range(TPB):
                            col = part * SEQ + h * P
                            last = nc.tensor.matmul(f_ps[part][h][:, :, :], fwd[:, i, col:col + P],
                                                    X2[:, bass.ds(g * TPP + i, 2, TPB), :],
                                                    start=i == 0, stop=i == TPB - 1)
                    last.then_inc(f_ready, 1)
                pe.wait_ge(spec_ready, g * 2 + 2)
                for i in range(TPB):
                    pe.wait_ge(y_done, g * TPB + (i + 1))
                    for n in range(4):
                        last = nc.tensor.matmul(y_ps[i][:, :, :].rearrange("p b d -> p (b d)"),
                                                back[:, n, i * P:(i + 1) * P], spec[:, n // 2, n % 2, :],
                                                start=n == 0, stop=n == 3)
                    last.then_inc(y_ready, 1)

        @block.vector
        def _(dve):
            v = nc.vector
            dve.sem_inc(f_done, 2)
            dve.sem_inc(y_done, 2)
            with dve.Fori(0, PAIRS) as g:
                for h in range(2):
                    dve.wait_ge(f_ready, g * 2 + h + 1)
                    for n, (part, kern) in enumerate(((0, KA), (1, KB), (0, KB), (1, KC))):
                        last = v.tensor_tensor(prod[:, h, n, :].rearrange("p (b d) -> p b d", b=2), f_ps[part][h][:, :, :],
                                               kern[:, h, :].unsqueeze(1).to_broadcast([P, 2, DIM]), ALU.mult)
                    last.then_inc(f_done, 1)
                for i in range(TPB):
                    dve.wait_ge(y_ready, g * TPB + i + 1)
                    for b in range(2):
                        t = g * TPP + (b * TPB + i)
                        v.tensor_tensor(y[:, b * TPB + i, :].unsqueeze(1), y_ps[i][:, b, :].unsqueeze(1), FO[:, pieces(t), 0:DIM], ALU.mult)
                    dve.drain()
                    dve.sem_inc(y_done, 1)
                tiles = pieces(g * TPP, TPP)
                v.tensor_tensor(y[:, :, :], y[:, :, :], FO[:, tiles, DIM:2 * DIM], ALU.add)
                dve.drain()
                v.tensor_tensor(X2[:, tiles, :], y[:, :, :], c.XN[:, tiles, :], ALU.add)
            dve.drain()

        @block.gpsimd
        def _(pool):
            with pool.Fori(0, PAIRS) as g:
                for h in range(2):
                    pool.wait_ge(f_done, g * 2 + h + 3)
                    nc.gpsimd.tensor_tensor(spec[:, 0, h, :], prod[:, h, 0, :], prod[:, h, 1, :], ALU.subtract)
                    nc.gpsimd.tensor_tensor(spec[:, 1, h, :], prod[:, h, 2, :], prod[:, h, 3, :], ALU.add)\
                      .then_inc(spec_ready, 1)


def add_branch(nc, c, X2):
    with nc.Block() as block:
        @block.vector
        def _(dve):
            nc.vector.tensor_tensor(X2[:, :, :], X2[:, :, :], c.ACC[:, :, :], ALU.add)


def layer0_attention(nc, c, a):
    pre = "L0_xattn_"
    with ExitStack() as ctx:
        sb, ps, sem = sub_memory(nc, ctx, "l0i_")
        KA, KB, KC = (sb(f"kernel{n}", [P, 2, DIM]) for n in range(3))
        state_space_kernel(nc, c, a, KA, KB, KC)
        X2 = sb("x2", [P, TILES, DIM])
        normalise(nc, c, c.X, natural=c.XN)
        normalise(nc, c, c.XN, natural=X2, transposed=False, gain=a[pre + "g_norm_in"], shift=a[pre + "b_norm_in"])
        with ExitStack() as inner:
            FO = inner.enter_context(nc.sbuf_tensor("film_out", [P, TILES, 2 * DIM], F32))
            film_attention(nc, c, a, X2, FO)
            convolve(nc, c, a, X2, FO, KA, KB, KC)
        normalise(nc, c, X2, gain=a[pre + "g_ffn"], shift=a[pre + "b_ffn"])
        experts(nc, c, "l0x", 1, 1024, a["L0_W1"], a["L0_W2"], func=ACT.Gelu, up_bias=a["L0_b1"],
                down_bias=a["L0_b2"])
        add_branch(nc, c, X2)
        normalise(nc, c, X2, natural=c.ACC, transposed=False, gain=a[pre + "g_norm_out"],
                  shift=a[pre + "b_norm_out"])


def build(nc, a, out, stop=99, start=0):
    with ExitStack() as ctx:
        sb, ps, sem = sub_memory(nc, ctx)
        c = Core()
        c.X = sb("residual", [P, TILES, DIM])
        c.XN = sb("normal", [P, TILES, DIM])
        c.XT = sb("normal_turned", [P, DK, TOKENS])
        c.ACC = sb("branch", [P, TILES, DIM])
        c.ident = sb("identity", [P, P])
        c.gate = sb("tanh_gates", [P, 8])
        c.headmask = sb("head_masks", [P, 16])
        c.iota8 = sb("iota", [P, 24])
        c.W = sb("expert_weights", [P, 16, TILES])
        load_inputs(nc, c, a)
        c.last = None
        if start <= 0 and stop >= 0:
            layer0_attention(nc, c, a)
            c.last = 0
        if start <= 1 and stop >= 1:
            W = c.W[:, 0:8, :]
            normalise(nc, c, c.X, natural=c.XN, add=c.last)
            hash_router(nc, c, W)
            experts(nc, c, "l0", 8, 1024, a["L0_ffn_W1"], a["L0_ffn_W2"], func=ACT.Relu, up_bias=a["L0_ffn_b1"],
                    down_bias=a["L0_ffn_b2"], weights=W)
            c.last = 4
        if start <= 2 and stop >= 2:
            normalise(nc, c, c.X, add=c.last)
            layer1_attention(nc, c, a)
            c.last = 1
        if start <= 3 and stop >= 3:
            W = c.W[:, 0:8, :]
            normalise(nc, c, c.X, natural=c.XN, transposed=False, add=c.last)
            normalise(nc, c, c.XN, gain=a["L1_ffn_ln_scale"], shift=a["L1_ffn_ln_bias"])
            softmax_router(nc, c, "l1_router", a["L1_gate_T"], 8, W, eps=1e-5)
            normalise(nc, c, c.X)
            experts(nc, c, "l1s", 1, 512, a["L1_sWu"], a["L1_sWd"], gate=a["L1_sWg"])
            experts(nc, c, "l1", 8, 512, a["L1_ffn_Wu"], a["L1_ffn_Wd"], gate=a["L1_ffn_Wg"], weights=W, fresh=False)
            c.last = 5
        if start <= 4 and stop >= 4:
            normalise(nc, c, c.X, add=c.last)
            narrow_attention(nc, c, a, 2)
            c.last = 2
        if start <= 5 and stop >= 5:
            normalise(nc, c, c.X, add=c.last)
            adapter_layer(nc, c, a)
            c.last = 6
        if start <= 6 and stop >= 6:
            normalise(nc, c, c.X, add=c.last)
            narrow_attention(nc, c, a, 3)
            c.last = 3
        if start <= 7 and stop >= 7:
            normalise(nc, c, c.X, add=c.last)
            softmax_router(nc, c, "l3_router", a["L3_ffn_Wr"], 16, c.W)
            experts(nc, c, "l3s", 1, 256, a["L3_Su"], a["L3_Sd"], gate=a["L3_Sg"])
            experts(nc, c, "l3", 16, 128, a["L3_ffn_Wu"], a["L3_ffn_Wd"], gate=a["L3_ffn_Wg"], weights=c.W, fresh=False)
            c.last = 7
        store_output(nc, c, out)


def constants():
    ident = np.eye(P, dtype=np.float32)
    p = np.arange(P)
    headmask = np.zeros((P, 16), np.float32)
    for h in range(4):
        headmask[:, h] = p // 32 == h
    for h in range(8):
        headmask[:, 4 + h] = p // 16 == h
    iota8 = np.tile(np.concatenate([np.arange(16), (np.arange(8) - 1) % 8]).astype(np.float32), (P, 1))
    N = 2 * SEQ
    l = np.arange(SEQ)[:, None]
    k = np.arange(SEQ)[None, :]
    turn = 2 * np.pi * ((l * k) % N) / N
    re, im = np.cos(turn), -np.sin(turn)
    im[:, 0] = (-1.0) ** np.arange(SEQ)
    fwd = np.concatenate([re, im], 1)
    scale = np.full(SEQ, 2.0 / N)
    scale[0] = 1.0 / N
    back = np.concatenate([re * scale, im * scale], 1).T
    fwd, back = fwd.astype(np.float32), np.ascontiguousarray(back.astype(np.float32))
    steps = np.tile(np.concatenate([np.arange(16), 16 * np.arange(16)]).astype(np.float32), (P, 1))
    return {"ident": ident, "headmask": headmask, "iota8": iota8, "fwd": fwd, "back": back, "steps": steps}


def layout(inputs):
    a = {k: np.asarray(v) for k, v in inputs.items()}
    d = {k: np.ascontiguousarray(v) for k, v in a.items()}
    d["L0_xattn_mod_gate"] = d["L0_xattn_mod_gate"].reshape(1)
    d["context_T"] = np.ascontiguousarray(a["ctx_768"].transpose(0, 2, 1))
    d["L1_gate_T"] = np.ascontiguousarray(a["L1_ffn_gate_w"].T)
    for n, k in (("L1_sWg", "L1_ffn_sWg"), ("L1_sWu", "L1_ffn_sWu"), ("L1_sWd", "L1_ffn_sWd"),
                 ("L3_Sg", "L3_ffn_Sg"), ("L3_Su", "L3_ffn_Su"), ("L3_Sd", "L3_ffn_Sd"),
                 ("L0_W1", "L0_xattn_W1"), ("L0_W2", "L0_xattn_W2"), ("L0_b2", "L0_xattn_b2")):
        d[n] = a[k][None]
        del d[k]
    d["L0_ffn_b1"] = np.ascontiguousarray(a["L0_ffn_b1"].reshape(8, 8, P).transpose(0, 2, 1))
    d["L0_b1"] = np.ascontiguousarray(a["L0_xattn_b1"].reshape(1, 8, P).transpose(0, 2, 1))
    del d["L0_xattn_b1"]
    for n in ("bq", "bk"):
        d["L2_" + n] = np.ascontiguousarray(a["L2_xattn_" + n].reshape(DK, P).T)
        del d["L2_xattn_" + n]
    for n in ("bd1", "ba_down"):
        d["L2_" + n] = np.ascontiguousarray(a["L2_ffn_" + n].reshape(4, P).T)
        del d["L2_ffn_" + n]
    d["L2_bd2"] = np.ascontiguousarray(a["L2_ffn_bd2"].reshape(8, DK, P).transpose(2, 0, 1))
    del d["L2_ffn_bd2"]
    d["mask_BxS_bk0"] = np.ascontiguousarray(d["mask_BxS_bk0"].reshape(TILES, P).T)
    d["mask_BxS_bf1"] = np.ascontiguousarray(d["mask_BxS_bf1"].reshape(TILES, P).T)
    d["L3_Wq_T"] = np.ascontiguousarray(a["L3_xattn_Wq"].T)
    d["L3_Wkv_T"] = np.ascontiguousarray(a["L3_xattn_Wkv"].T)
    for k in ("A_re", "A_im", "C_re", "C_im"):
        v = a["L0_xattn_" + k]
        d["S_" + k] = np.ascontiguousarray(v.reshape(2, 128, 64).transpose(0, 2, 1).reshape(128, 128))
        del d["L0_xattn_" + k]
    for k in ("ctx_768", "L1_ffn_gate_w", "L3_xattn_Wq", "L3_xattn_Wkv"):
        del d[k]
    d.update(constants())
    return d


def kernel(**inputs):
    import concourse.bacc as bacc
    from concourse.bass_utils import run_bass_kernel_spmd

    nc = bacc.Bacc("TRN2", target_bir_lowering=False, num_devices=1)
    arrays = layout(inputs)
    args = {k: nc.dram_tensor("in_" + k, v.shape, mybir.dt.from_np(v.dtype), kind="ExternalInput").ap()
            for k, v in arrays.items()}
    out = nc.dram_tensor("out_0", (BATCH, SEQ, DIM), F32, kind="ExternalOutput").ap()
    build(nc, args, out)
    r = run_bass_kernel_spmd(nc, [{"in_" + k: v for k, v in arrays.items()}], core_ids=[0])
    return r.results[0]["out_0"]
```

```python
from contextlib import ExitStack

import numpy as np

import concourse.bass as bass
from concourse import mybir

F32 = mybir.dt.float32
I32 = mybir.dt.int32
U32 = mybir.dt.uint32
U8 = mybir.dt.uint8
ACT = mybir.ActivationFunctionType
ALU = mybir.AluOpType
AX = mybir.AxisListType

P = 128
BATCH, SEQ, DIM = 8, 256, 256
KEYS, CTX = 77, 192
CP = 96
CK = CTX // CP
DK = DIM // P
TILES = BATCH * SEQ // P
TOKENS = BATCH * SEQ
TPB = SEQ // P
EPS = 1e-5
BLOCK = 512
BLOCKS = TOKENS // BLOCK
TPK = BLOCK // P
MAGIC = 12582912.0
NEG = -3.0e38


def pieces(i, n=1):
    return bass.ds(i, n)


class Core:

    stages = 0

    def count(self):
        self.stages += 1
        return self.stages


class Transfers:

    def __init__(self, nc, ctx, name):
        self.sem = ctx.enter_context(nc.semaphore("transfers_" + name))
        self.count = 0

    def expect(self, n):
        self.count += 16 * n
        return self.count


def sub_memory(nc, ctx, prefix=""):
    def sb(name, shape, dt=F32):
        return ctx.enter_context(nc.sbuf_tensor(prefix + name, shape, dt))

    def ps(name, shape, dt=F32):
        return ctx.enter_context(nc.psum_tensor(prefix + name, shape, dt))

    def sem(name):
        handle = ctx.enter_context(nc.semaphore(prefix + name))
        ctx.callback(nc.sync.sem_clear, handle)
        return handle

    return sb, ps, sem


def row(ap):
    return ap.rearrange("(a n) -> a n", a=1)


def spread(ap):
    return ap.partition_broadcast(P)


def load_inputs(nc, c, a):
    with ExitStack() as ctx:
        sb, ps, sem = sub_memory(nc, ctx)
        gates = sb("gates", [P, 8])
        loaded, gates_done = sem("setup_loaded"), sem("setup_gates")
        block = ctx.enter_context(nc.Block())

        @block.sync
        def _(sp):
            sp.dma_start(gates[:, 0:4], spread(a["g_xattn"])).then_inc(loaded, 16)
            sp.dma_start(gates[:, 4:8], spread(a["g_ffn"])).then_inc(loaded, 16)
            sp.dma_start(c.X[:, :, :], a["x"].rearrange("b (i p) d -> p (b i) d", p=P)).then_inc(loaded, 16)
            sp.dma_start(c.ident[:, :], a["ident"]).then_inc(loaded, 16)
            sp.dma_start(c.headmask[:, :], a["headmask"]).then_inc(loaded, 16)
            sp.dma_start(c.iota[:, :], a["iota"]).then_inc(loaded, 16)
            sp.dma_start(c.above[:, :], a["above"]).then_inc(loaded, 16)
            sp.dma_start(c.ones[:, :], a["ones"]).then_inc(loaded, 16)

        @block.scalar
        def _(act):
            act.wait_ge(loaded, 8 * 16)
            nc.scalar.activation(c.gate[:, :], gates[:, :], ACT.Tanh).then_inc(gates_done, 1)
            act.wait_ge(gates_done, 1)


def token_statistics(nc, dve, source, stats, mean, diff, var, var_ready):
    v = nc.vector
    with dve.Fori(0, TILES) as t:
        v.bn_stats(stats[:, pieces(t), :].rearrange("p a s -> p (a s)"),
                   source[:, pieces(t), :].rearrange("p a s -> p (a s)"))
    dve.drain()
    v.tensor_tensor(mean[:, :], stats[:, :, 1], stats[:, :, 4], ALU.add)
    v.tensor_tensor(diff[:, :], stats[:, :, 1], stats[:, :, 4], ALU.subtract)
    v.tensor_tensor(var[:, :], stats[:, :, 2], stats[:, :, 5], ALU.add)
    dve.drain()
    v.tensor_scalar(mean[:, :], mean[:, :], 0.5, None, ALU.mult)
    v.tensor_tensor(diff[:, :], diff[:, :], diff[:, :], ALU.mult)
    v.tensor_scalar(var[:, :], var[:, :], 1.0 / DIM, EPS, ALU.mult, ALU.add)
    dve.drain()
    v.scalar_tensor_tensor(var[:, :], diff[:, :], 0.25, var[:, :], ALU.mult, ALU.add).then_inc(var_ready, 1)


def reciprocal_root(nc, dve, var, dev, rstd):
    v = nc.vector
    v.reciprocal(rstd[:, :], dev[:, :])
    dve.drain()
    v.tensor_tensor(dev[:, :], rstd[:, :], rstd[:, :], ALU.mult)
    dve.drain()
    v.tensor_tensor(dev[:, :], dev[:, :], var[:, :], ALU.mult)
    dve.drain()
    v.tensor_scalar(dev[:, :], dev[:, :], -0.5, 1.5, ALU.mult, ALU.add)
    dve.drain()
    v.tensor_tensor(rstd[:, :], rstd[:, :], dev[:, :], ALU.mult)
    dve.drain()


def normalise(nc, c, source, natural=None, transposed=True, gain=None, shift=None, add=None, store=None):
    with ExitStack() as ctx:
        sb, ps, sem = sub_memory(nc, ctx, f"n{c.count()}_")
        stats = sb("ln_stats", [P, TILES, 6])
        mean = sb("ln_mean", [P, TILES])
        diff = sb("ln_diff", [P, TILES])
        var = sb("ln_var", [P, TILES])
        dev = sb("ln_dev", [P, TILES])
        rstd = sb("ln_rstd", [P, TILES])
        scratch = sb("ln_scratch", [P, 2, TPB, DIM])
        affine = sb("ln_affine", [P, 2, DIM])
        turned = [ps(f"ln_turned{u}", [P, DK, SEQ]) for u in range(2)]
        affine_loaded = sem("ln_affine_loaded")
        var_ready, dev_ready = sem("ln_var_ready"), sem("ln_dev_ready")
        scratch_ready = sem("ln_scratch_ready")
        scratch_turned, scratch_copied = sem("ln_scratch_turned"), sem("ln_scratch_copied")
        turned_free = sem("ln_turned_free")
        block = ctx.enter_context(nc.Block())

        if gain is not None:
            @block.sync
            def _(sp):
                sp.dma_start(affine[:, 0, :], spread(gain)).then_inc(affine_loaded, 16)
                sp.dma_start(affine[:, 1, :], spread(shift)).then_inc(affine_loaded, 16)

        @block.vector
        def _(dve):
            v = nc.vector
            if add is not None:
                for h in range(2):
                    t = slice(h * TILES // 2, (h + 1) * TILES // 2)
                    v.scalar_tensor_tensor(c.X[:, t, :], c.ACC[:, t, :], c.gate[:, add:add + 1], c.X[:, t, :],
                                           ALU.mult, ALU.add)
                dve.drain()
            token_statistics(nc, dve, source, stats, mean, diff, var, var_ready)
            dve.wait_ge(dev_ready, 1)
            reciprocal_root(nc, dve, var, dev, rstd)
            if transposed:
                dve.sem_inc(scratch_turned, 2)
            if natural is not None:
                dve.sem_inc(scratch_copied, 2)
            if gain is not None:
                dve.wait_ge(affine_loaded, 32)
            with dve.Fori(0, BATCH // 2) as g:
                for u in range(2):
                    if transposed:
                        dve.wait_ge(scratch_turned, g * 2 + u + 1)
                    if natural is not None:
                        dve.wait_ge(scratch_copied, g * 2 + u + 1)
                    for i in range(TPB):
                        t = g * 4 + (2 * u + i)
                        last = v.tensor_scalar(scratch[:, u, i, :].unsqueeze(1), source[:, pieces(t), :],
                                               mean[:, pieces(t)], rstd[:, pieces(t)], ALU.subtract, ALU.mult)
                    if gain is not None:
                        for k, op in ((0, ALU.mult), (1, ALU.add)):
                            dve.drain()
                            last = v.tensor_tensor(scratch[:, u, :, :], scratch[:, u, :, :],
                                                   affine[:, k, :].unsqueeze(1).to_broadcast([P, TPB, DIM]), op)
                    last.then_inc(scratch_ready, 1)

        if natural is not None:
            @block.gpsimd
            def _(pool):
                with pool.Fori(0, BATCH // 2) as g:
                    for u in range(2):
                        pool.wait_ge(scratch_ready, g * 2 + u + 1)
                        nc.gpsimd.tensor_copy(natural[:, pieces(g * 4 + 2 * u, TPB), :],
                                              scratch[:, u, :, :]).then_inc(scratch_copied, 1)

        if transposed:
            @block.tensor
            def _(pe):
                with pe.Fori(0, BATCH // 2) as g:
                    for u in range(2):
                        pe.wait_ge(scratch_ready, g * 2 + u + 1)
                        pe.wait_ge(turned_free, g * 2 + u + 1)
                        for i in range(TPB):
                            for k in range(DK):
                                last = nc.tensor.transpose(turned[u][:, k, i * P:(i + 1) * P],
                                                           scratch[:, u, i, k * P:(k + 1) * P], c.ident[:, :])
                        last.then_inc(scratch_turned, 1)

        @block.scalar
        def _(act):
            act.wait_ge(var_ready, 1)
            nc.scalar.activation(dev[:, :], var[:, :], ACT.Sqrt).then_inc(dev_ready, 1)
            if transposed:
                act.sem_inc(turned_free, 2)
                with act.Fori(0, BATCH // 2) as g:
                    for u in range(2):
                        act.wait_ge(scratch_turned, g * 2 + u + 3)
                        nc.scalar.activation(c.XT[:, :, pieces(g * 2 * SEQ + u * SEQ, SEQ)], turned[u][:, :, :],
                                             ACT.Copy).then_inc(turned_free, 1)


def dense_layer(nc, c, name, width, up, down, gate=None, func=ACT.Silu, up_bias=None, down_bias=None,
                blocks=range(BLOCKS), send=None):
    NF = width // P
    NB = len(blocks)
    gated = gate is not None
    ring = 2 if gated else 4
    with ExitStack() as ctx:
        sb, ps, sem = sub_memory(nc, ctx, f"{name}{c.count()}_")
        w_up = sb("w_up", [P, DK, width])
        w_gate = sb("w_gate", [P, DK, width]) if gated else None
        w_down = sb("w_down", [P, NF, DIM])
        hidden = sb("hidden", [P, 2, NF, BLOCK])
        b_down = sb("b_down", [P, DIM]) if down_bias is not None else None
        b_up = sb("b_up", [P, NF]) if up_bias is not None else None
        silu = sb("silu", [P, 2, BLOCK]) if gated else None
        up_ps = [ps(f"up{i}", [P, BLOCK]) for i in range(ring)]
        gate_ps = [ps(f"gate{i}", [P, BLOCK]) for i in range(ring)] if gated else None
        out_ps = [ps(f"out{i}", [P, BLOCK]) for i in range(4)]
        up_loaded, down_loaded = sem("up_loaded"), sem("down_loaded")
        up_ready, gate_done = sem("up_ready"), sem("gate_done")
        hidden_done = sem("hidden_done")
        out_ready, out_free = sem("out_ready"), sem("out_free")
        sent = c.transfers["sent"]
        block = ctx.enter_context(nc.Block())
        up_loads, down_loads = 32 if gated or up_bias is not None else 16, 16 if down_bias is None else 32

        @block.sync
        def _(sp):
            for w, src in ((w_up, up), (w_gate, gate)):
                if src is not None:
                    sp.dma_start(w[:, :, :], src.rearrange("(k p) n -> p k n", p=P)).then_inc(up_loaded, 16)
            if up_bias is not None:
                sp.dma_start(b_up[:, :], up_bias).then_inc(up_loaded, 16)
            sp.dma_start(w_down[:, :, :], down.rearrange("(k p) n -> p k n", p=P)).then_inc(down_loaded, 16)
            if down_bias is not None:
                sp.dma_start(b_down[:, :], spread(down_bias)).then_inc(down_loaded, 16)

        if send is not None:
            @block.gpsimd
            def _(pool):
                send_tokens(nc, c, send, pool, sent)

        @block.tensor
        def _(pe):
            def up_block(n, k):
                for f in range(NF):
                    pe.wait_ge(hidden_done, n * NF + f + 1)
                    slot = (n * NF + f) % ring
                    for wt, tile in ((w_up, up_ps), (w_gate, gate_ps)):
                        if wt is not None:
                            for kk in range(DK):
                                last = nc.tensor.matmul(tile[slot][:, :], wt[:, kk, f * P:(f + 1) * P],
                                                        c.XT[:, kk, k * BLOCK:(k + 1) * BLOCK],
                                                        start=kk == 0, stop=kk == DK - 1)
                    last.then_inc(up_ready, 1)

            def down_block(n):
                pe.wait_ge(hidden_done, (n + 1) * NF + ring)
                for i in range(TPK):
                    pe.wait_ge(out_free, n * TPK + i + 1)
                    for f in range(NF):
                        last = nc.tensor.matmul(out_ps[i][:, 0:DIM], hidden[:, n % 2, f, i * P:(i + 1) * P],
                                                w_down[:, f, :], start=f == 0, stop=f == NF - 1)
                    last.then_inc(out_ready, 1)

            pe.wait_ge(up_loaded, up_loads)
            for n, k in enumerate(blocks):
                up_block(n, k)
                if n == 0:
                    pe.wait_ge(down_loaded, down_loads)
                else:
                    down_block(n - 1)
            down_block(NB - 1)

        @block.scalar
        def _(act):
            if not gated:
                act.sem_inc(hidden_done, ring)
            if up_bias is not None:
                act.wait_ge(up_loaded, up_loads)
            for n in range(NB):
                if not gated and n >= 2:
                    act.wait_ge(out_ready, TPK * (n - 1))
                for f in range(NF):
                    slot = (n * NF + f) % ring
                    act.wait_ge(up_ready, n * NF + f + 1)
                    if gated:
                        nc.scalar.activation(silu[:, slot, :], gate_ps[slot][:, :], func).then_inc(gate_done, 1)
                    else:
                        nc.scalar.activation(hidden[:, n % 2, f, :], up_ps[slot][:, :], func,
                                             bias=b_up[:, f:f + 1]).then_inc(hidden_done, 1)

        @block.vector
        def _(dve):
            v = nc.vector
            if gated:
                dve.sem_inc(hidden_done, ring)
            dve.sem_inc(out_free, 4)
            if down_bias is not None:
                dve.wait_ge(down_loaded, down_loads)

            def hidden_block(n):
                if n >= 2:
                    dve.wait_ge(out_ready, TPK * (n - 1))
                for f in range(NF):
                    slot = (n * NF + f) % ring
                    dve.wait_ge(gate_done, n * NF + f + 1)
                    v.tensor_tensor(hidden[:, n % 2, f, :], up_ps[slot][:, :], silu[:, slot, :], ALU.mult)\
                     .then_inc(hidden_done, 1)

            def out_block(n, k):
                for i in range(TPK):
                    dve.wait_ge(out_ready, n * TPK + i + 1)
                    acc, value = c.ACC[:, k * TPK + i, :], out_ps[i][:, 0:DIM]
                    if down_bias is not None:
                        v.tensor_tensor(acc, value, b_down[:, :], ALU.add).then_inc(out_free, 1)
                    else:
                        v.tensor_copy(acc, value).then_inc(out_free, 1)

            for n, k in enumerate(blocks):
                if gated:
                    hidden_block(n)
                if n:
                    out_block(n - 1, k - 1)
            out_block(NB - 1, blocks[-1])
            dve.drain()


CHOICES = 2
KT = CHOICES * TILES
SLOT_TILE = 256
SPT = SLOT_TILE // P


def slot_tiles(E):
    return CHOICES * TOKENS // SLOT_TILE + E - 1


def plan_slots(nc, c, E, S):
    NT = slot_tiles(E)
    with ExitStack() as ctx:
        sb, ps, sem = sub_memory(nc, ctx, f"plan{c.count()}_")
        chosen = c.chosen[:, 0:E, :]
        running = [sb(f"running{u}", [P, E, KT]) for u in range(2)]
        before = sb("before", [P, E, KT])
        count = sb("count", [P, E])
        tiles = sb("tiles", [P, E])
        end = [sb(f"end{u}", [P, E]) for u in range(2)]
        first = sb("first", [P, E])
        past = sb("past", [P, NT, E])
        owner = sb("owner_value", [P, NT])
        where = sb("where", [P, KT])
        rank_ps = ps("rank", [P, E, KT])
        count_ps = ps("count_ps", [P, E])
        summed, ranked = sem("summed"), sem("ranked")
        block = ctx.enter_context(nc.Block())

        @block.vector
        def _(dve):
            v = nc.vector

            def running_sum(x, y, n):
                step = 1
                while step < n:
                    v.tensor_copy(y[..., 0:step], x[..., 0:step])
                    v.tensor_tensor(y[..., step:n], x[..., step:n], x[..., 0:n - step], ALU.add)
                    dve.drain()
                    x, y = y, x
                    step *= 2
                return x

            v.tensor_copy(running[0][:, :, :], chosen)
            dve.drain()
            total = running_sum(running[0][:, :, :], running[1][:, :, :], KT)
            v.tensor_tensor(before[:, :, :], total, chosen, ALU.subtract)
            v.tensor_copy(count[:, :], total[:, :, KT - 1]).then_inc(summed, 1)
            dve.wait_ge(ranked, 1)
            v.tensor_scalar(tiles[:, :], count_ps[:, :], 1.0 / SLOT_TILE, 0.498, ALU.mult, ALU.add)
            dve.drain()
            v.tensor_scalar(tiles[:, :], tiles[:, :], MAGIC, None, ALU.add)
            dve.drain()
            v.tensor_scalar(tiles[:, :], tiles[:, :], MAGIC, None, ALU.subtract)
            dve.drain()
            v.tensor_copy(end[0][:, :], tiles[:, :])
            dve.drain()
            last = running_sum(end[0][:, :], end[1][:, :], E)
            v.tensor_tensor(first[:, :], last, tiles[:, :], ALU.subtract)
            iota = c.iota[:, 0:NT].unsqueeze(2).to_broadcast([P, NT, E])
            v.tensor_tensor(past[:, :, :], iota, last.unsqueeze(1).to_broadcast([P, NT, E]), ALU.is_ge)
            dve.drain()
            v.tensor_scalar(first[:, :], first[:, :], float(SLOT_TILE), None, ALU.mult)
            v.tensor_reduce(owner[:, :], past[:, :, :], AX.X, ALU.add)
            dve.drain()
            v.tensor_scalar(owner[:, :], owner[:, :], float(E - 1), None, ALU.min)
            v.tensor_tensor(before[:, :, :], rank_ps[:, :, :], first[:, :].unsqueeze(2).to_broadcast([P, E, KT]),
                            ALU.add)
            dve.drain()
            v.tensor_copy(S.owner[:, 0:NT], owner[:, :])
            v.tensor_tensor(before[:, :, :], before[:, :, :], chosen, ALU.mult)
            dve.drain()
            v.tensor_reduce(where[:, :], before[:, :, :].rearrange("p e k -> p k e"), AX.X, ALU.add)
            dve.drain()
            v.tensor_copy(S.slot[:, :], where[:, :])
            dve.drain()

        @block.tensor
        def _(pe):
            pe.wait_ge(summed, 1)
            nc.tensor.matmul(count_ps[:, :], c.ones[:, :], count[:, :], start=True, stop=True)
            nc.tensor.matmul(rank_ps[:, :, :], c.above[:, :], chosen, start=True, stop=False)
            nc.tensor.matmul(rank_ps[:, :, :], c.ones[:, :], before[:, :, :], start=False, stop=True)\
              .then_inc(ranked, 1)


def send_tokens(nc, c, S, pool, sent):
    for kt in range(KT):
        nc.gpsimd.indirect_dma_start(S.table, bass.IndirectOffsetOnAxis(ap=S.slot[:, kt:kt + 1], axis=0),
                                     c.XN[:, kt % TILES, :], None).then_inc(sent.sem, 16)
    pool.wait_ge(sent.sem, sent.expect(KT))


def routed_experts(nc, c, name, E, width, S, up, down, gate=None, up_bias=None, down_bias=None):
    NF = width // P
    GW = min(2, NF)
    NG = NF // GW
    NT = slot_tiles(E)
    assert NT % 2 == 1
    gated = gate is not None
    ring = 2 if gated else 4
    lanes = 1 if gated else 2
    share = NG // lanes
    with ExitStack() as ctx:
        sb, ps, sem = sub_memory(nc, ctx, name + "_")
        w_up = sb("w_up", [P, 2, DK, width])
        w_gate = sb("w_gate", [P, 2, DK, width]) if gated else None
        w_down = sb("w_down", [P, 2, NF, DIM])
        b_up = None if gated else sb("b_up", [P, 2, NF])
        b_down = None if gated else sb("b_down", [P, 2, DIM])
        rows = sb("rows", [P, 2, SPT, DIM])
        x_t = sb("x_t", [P, 2, DK, SLOT_TILE])
        silu = sb("silu", [P, 2, GW * SLOT_TILE]) if gated else None
        hidden = sb("hidden", [P, 2, NF, SLOT_TILE])
        result = sb("result", [P, 2, SPT, DIM])
        x_ps = ps("x_ps", [P, DK, SLOT_TILE])
        up_ps = [ps(f"up{i}", [P, GW, SLOT_TILE]) for i in range(ring)]
        gate_ps = [ps(f"gate{i}", [P, GW, SLOT_TILE]) for i in range(ring)] if gated else None
        out_ps = [ps(f"out{i}", [P, SPT, DIM]) for i in range(2)]
        rows_loaded = [sem(f"rows_loaded{u}") for u in range(2)]
        up_loaded = [sem(f"up_loaded{u}") for u in range(2)]
        down_loaded = [sem(f"down_loaded{u}") for u in range(2)]
        turned, x_ready = sem("turned"), sem("x_ready")
        up_ready, gate_done = sem("up_ready"), sem("gate_done")
        hidden_done = [sem(f"hidden_done{i}") for i in range(lanes)]
        out_ready, out_done = sem("out_ready"), sem("out_done")
        stored, result_free = c.transfers["stored"], sem("result_free")
        block = ctx.enter_context(nc.Block())
        credit = ring // lanes

        def over_tiles(eng, body):
            with eng.Fori(0, NT // 2) as g:
                for u in range(2):
                    body(g * 2 + u, g, u)
            body(NT - 1, NT // 2, 0)

        @block.sync
        def _(sp):
            def load(j, g, u, again):
                e = pieces(sp.value_load(S.owner[0:1, pieces(j)], min_val=0, max_val=E - 1))
                if again:
                    sp.wait_ge(turned, j - 1)
                sp.dma_start(rows[:, u, :, :].unsqueeze(1),
                             S.table.rearrange("(j i p) d -> p j i d", i=SPT, p=P)[:, pieces(j), :, :])\
                  .then_inc(rows_loaded[u], 16)
                if again:
                    sp.wait_ge(up_ready, (j - 1) * NG)
                for w, src in ((w_up, up), (w_gate, gate)):
                    if src is not None:
                        sp.dma_start(w[:, u, :, :].unsqueeze(1), src[e, :, :].rearrange("a (k p) n -> p a k n", p=P))\
                          .then_inc(up_loaded[u], 16)
                if again and not gated:
                    for n in range(lanes):
                        sp.wait_ge(hidden_done[n], (j - 1) * share + credit)
                if not gated:
                    sp.dma_start(b_up[:, u, :].unsqueeze(1), up_bias[e, :, :].rearrange("a p f -> p a f"))\
                      .then_inc(up_loaded[u], 16)
                if again:
                    sp.wait_ge(out_ready, j - 1)
                sp.dma_start(w_down[:, u, :, :].unsqueeze(1), down[e, :, :].rearrange("a (k p) n -> p a k n", p=P))\
                  .then_inc(down_loaded[u], 16)
                if not gated:
                    if again:
                        sp.wait_ge(out_done, j + 1)
                    sp.dma_start(b_down[:, u, :].unsqueeze(1), down_bias[e, :].partition_broadcast(P))\
                      .then_inc(down_loaded[u], 16)

            for u in range(2):
                load(u, 0, u, False)
            with sp.Fori(1, NT // 2) as g:
                for u in range(2):
                    load(g * 2 + u, g, u, True)
            load(NT - 1, NT // 2, 0, True)

        @block.tensor
        def _(pe):
            def transposes(g, u):
                pe.wait_ge(rows_loaded[u], (g + 1) * 16)
                for i in range(SPT):
                    for k in range(DK):
                        last = nc.tensor.transpose(x_ps[:, k, i * P:(i + 1) * P], rows[:, u, i, k * P:(k + 1) * P],
                                                   c.ident[:, :])
                last.then_inc(turned, 1)

            def tile(j, g, u, ahead):
                pe.wait_ge(up_loaded[u], (g + 1) * 32)
                pe.wait_ge(x_ready, j + 1)
                for q in range(NG):
                    bank = (u * NG + q) % ring
                    lane = q % lanes
                    pe.wait_ge(hidden_done[lane], j * share + (q // lanes + 1))
                    for w, tiles in ((w_up, up_ps), (w_gate, gate_ps)):
                        if w is not None:
                            for i in range(GW):
                                f = q * GW + i
                                for k in range(DK):
                                    last = nc.tensor.matmul(tiles[bank][:, i, :], w[:, u, k, f * P:(f + 1) * P],
                                                            x_t[:, u, k, :], start=k == 0, stop=k == DK - 1)
                    last.then_inc(up_ready, 1)
                if ahead:
                    transposes(g + u, 1 - u)
                pe.wait_ge(down_loaded[u], (g + 1) * (16 if gated else 32))
                for lane in range(lanes):
                    pe.wait_ge(hidden_done[lane], j * share + (share + credit))
                pe.wait_ge(out_done, j + 1)
                for i in range(SPT):
                    for f in range(NF):
                        last = nc.tensor.matmul(out_ps[u][:, i, :], hidden[:, u, f, i * P:(i + 1) * P],
                                                w_down[:, u, f, :], start=f == 0, stop=f == NF - 1)
                last.then_inc(out_ready, 1)

            transposes(0, 0)
            with pe.Fori(0, NT // 2) as g:
                for u in range(2):
                    tile(g * 2 + u, g, u, ahead=True)
            tile(NT - 1, NT // 2, 0, ahead=False)

        def finish_group(eng, j, u, q):
            n = q % 2
            eng.wait_ge(up_ready, j * NG + (q + 1))
            for i in range(GW):
                f = q * GW + i
                src, dst, bias = up_ps[q][:, i, :], hidden[:, u, f, :], b_up[:, u, f:f + 1]
                if n:
                    last = nc.scalar.activation(dst, src, ACT.Relu, bias=bias)
                else:
                    last = nc.vector.tensor_scalar(dst, src, bias, 0.0, ALU.add, ALU.max)
            last.then_inc(hidden_done[n], 1)

        @block.scalar
        def _(act):
            if not gated:
                act.sem_inc(hidden_done[1], credit)

            def body(j, g, u):
                if not gated:
                    act.wait_ge(up_loaded[u], (g + 1) * 32)
                act.wait_ge(turned, j + 1)
                nc.scalar.activation(x_t[:, u, :, :], x_ps[:, :, :], ACT.Copy).then_inc(x_ready, 1)
                for q in range(NG):
                    if gated:
                        bank = (u * NG + q) % ring
                        act.wait_ge(up_ready, j * NG + (q + 1))
                        nc.scalar.activation(silu[:, bank, :].rearrange("p (f n) -> p f n", f=GW),
                                             gate_ps[bank][:, :, :], ACT.Silu).then_inc(gate_done, 1)
                    elif q % 2:
                        finish_group(act, j, u, q)

            over_tiles(act, body)

        @block.vector
        def _(dve):
            v = nc.vector
            dve.sem_inc(hidden_done[0], credit)
            dve.sem_inc(out_done, 2)
            dve.sem_inc(result_free, 2)

            def body(j, g, u):
                if not gated:
                    dve.wait_ge(up_loaded[u], (g + 1) * 32)
                for q in range(NG):
                    bank = (u * NG + q) % ring
                    if gated:
                        dve.wait_ge(gate_done, j * NG + (q + 1))
                        v.tensor_tensor(hidden[:, u, q * GW:(q + 1) * GW, :], up_ps[bank][:, :, :],
                                        silu[:, bank, :].rearrange("p (f n) -> p f n", f=GW), ALU.mult)\
                         .then_inc(hidden_done[0], 1)
                    elif q % 2 == 0:
                        finish_group(dve, j, u, q)
                dve.wait_ge(result_free, j + 1)
                dve.wait_ge(out_ready, j + 1)
                if gated:
                    v.tensor_copy(result[:, u, :, :], out_ps[u][:, :, :]).then_inc(out_done, 1)
                else:
                    dve.wait_ge(down_loaded[u], (g + 1) * 32)
                    v.tensor_tensor(result[:, u, :, :], out_ps[u][:, :, :],
                                    b_down[:, u, :].unsqueeze(1).to_broadcast([P, SPT, DIM]), ALU.add)\
                     .then_inc(out_done, 1)

            over_tiles(dve, body)

        @block.gpsimd
        def _(pool):
            before = stored.count
            stored.expect(NT)

            def body(j, g, u):
                pool.wait_ge(out_done, j + 3)
                pool.dma_start(S.results.rearrange("(j i p) d -> p j i d", i=SPT, p=P)[:, pieces(j), :, :],
                               result[:, u, :, :].unsqueeze(1)).then_inc(stored.sem, 16)
                pool.wait_ge(stored.sem, (j + 1) * 16 + before)
                pool.sem_inc(result_free, 1)

            over_tiles(pool, body)


def collect(nc, c, E, S, fresh):
    GROUPS = 8
    PER = KT // GROUPS
    with ExitStack() as ctx:
        sb, ps, sem = sub_memory(nc, ctx, f"collect{c.count()}_")
        got = sb("got", [P, KT, DIM])
        arrived = [c.transfers[f"arrived{n}"] for n in range(GROUPS)]
        block = ctx.enter_context(nc.Block())

        @block.gpsimd
        def _(pool):
            for n in range(GROUPS):
                for kt in range(n * PER, (n + 1) * PER):
                    nc.gpsimd.indirect_dma_start(got[:, kt, :], None, S.results[0:slot_tiles(E) * SLOT_TILE, :],
                                                 bass.IndirectOffsetOnAxis(ap=S.slot[:, kt:kt + 1], axis=0))\
                      .then_inc(arrived[n].sem, 16)

        @block.vector
        def _(dve):
            v = nc.vector
            for n in range(GROUPS):
                dve.wait_ge(arrived[n].sem, arrived[n].expect(PER))
                for kt in range(n * PER, (n + 1) * PER):
                    acc, part = c.ACC[:, kt % TILES, :], c.share[:, kt:kt + 1]
                    if fresh and kt < TILES:
                        v.tensor_scalar(acc, got[:, kt, :], part, None, ALU.mult)
                    else:
                        v.scalar_tensor_tensor(acc, got[:, kt, :], part, acc, ALU.mult, ALU.add)
                if n == GROUPS // 2 - 1:
                    dve.drain()
            dve.drain()


def send_block(nc, c, S):
    with ExitStack() as ctx:
        sb, ps, sem = sub_memory(nc, ctx, f"send{c.count()}_")
        sent = c.transfers["sent"]
        block = ctx.enter_context(nc.Block())

        @block.gpsimd
        def _(pool):
            send_tokens(nc, c, S, pool, sent)


def hash_router(nc, c):
    with ExitStack() as ctx:
        sb, ps, sem = sub_memory(nc, ctx)
        s, a, k, g, h = (sb(f"hash_{n}", [P, TILES]) for n in ("sum", "abs", "whole", "over", "bucket"))
        block = ctx.enter_context(nc.Block())

        @block.vector
        def _(dve):
            v = nc.vector

            def ts(*args):
                v.tensor_scalar(*args)
                dve.drain()

            def tt(*args):
                v.tensor_tensor(*args)
                dve.drain()

            S, A, K, G, H = (x[:, :] for x in (s, a, k, g, h))
            v.memset(c.share[:, :], 0.5)
            tt(S, c.XN[:, :, 0], c.XN[:, :, 1], ALU.add)
            ts(A, S, -1.0, None, ALU.mult)
            tt(A, A, S, ALU.max)
            ts(K, A, MAGIC, None, ALU.add)
            ts(K, K, MAGIC, None, ALU.subtract)
            tt(G, K, A, ALU.is_gt)
            tt(K, K, G, ALU.subtract)
            ts(G, S, 0.0, -2.0, ALU.is_lt, ALU.mult)
            ts(G, G, 1.0, None, ALU.add)
            tt(K, K, G, ALU.mult)
            ts(G, K, 0.125, -0.4375, ALU.mult, ALU.add)
            ts(G, G, MAGIC, None, ALU.add)
            ts(G, G, MAGIC, -8.0, ALU.subtract, ALU.mult)
            tt(H, K, G, ALU.add)
            by_expert = [P, 8, TILES]
            iota = c.iota[:, 0:8].unsqueeze(2).to_broadcast(by_expert)
            previous = c.iota[:, 32:40].unsqueeze(2).to_broadcast(by_expert)
            bucket = H.unsqueeze(1).to_broadcast(by_expert)
            tt(c.chosen[:, 0:8, 0:TILES], iota, bucket, ALU.is_equal)
            tt(c.chosen[:, 0:8, TILES:KT], previous, bucket, ALU.is_equal)


def softmax_router(nc, c, name, router, E, eps=None, gain=None, shift=None):
    again = gain is not None
    with ExitStack() as ctx:
        sb, ps, sem = sub_memory(nc, ctx, name + "_")
        w = sb("w", [P, DK, E])
        affine = sb("affine", [P, 2, DK])
        w_shift = sb("w_shift", [P, DK, E])
        stats = sb("stats", [P, TILES, 6])
        mean, diff, var, dev, rstd = (sb(n, [P, TILES]) for n in ("mean", "diff", "var", "dev", "rstd"))
        sums = sb("sums", [P, 2, E])
        p = sb("probs", [P, TILES, E])
        one = sb("stat", [P, TILES])
        top = sb("top", [P, TILES, 8])
        at = sb("at", [P, TILES, 8], U32)
        atf = sb("atf", [P, TILES, 8])
        logits = ps("logits", [P, TILES, E])
        sums_ps = ps("sums_ps", [P, 2, E])
        loaded, weights_ready, logits_ready = sem("loaded"), sem("weights_ready"), sem("logits_ready")
        var_ready, dev_ready = sem("var_ready"), sem("dev_ready")
        shifted, exp_ready = sem("shifted"), sem("exp_ready")
        block = ctx.enter_context(nc.Block())

        @block.sync
        def _(sp):
            sp.dma_start(w[:, :, :], router.rearrange("(k p) e -> p k e", p=P)).then_inc(loaded, 16)
            if again:
                sp.dma_start(affine[:, 0, :], gain).then_inc(loaded, 16)
                sp.dma_start(affine[:, 1, :], shift).then_inc(loaded, 16)

        @block.tensor
        def _(pe):
            if again:
                pe.wait_ge(weights_ready, 1)
                for n, x in enumerate((w, w_shift)):
                    for k in range(DK):
                        nc.tensor.matmul(sums_ps[:, n, :], c.ones[:, :], x[:, k, :], start=k == 0, stop=k == DK - 1)
            else:
                pe.wait_ge(loaded, 16)
            for t in range(TILES):
                for k in range(DK):
                    last = nc.tensor.matmul(logits[:, t, :], c.XT[:, k, t * P:(t + 1) * P], w[:, k, :],
                                            start=k == 0, stop=k == DK - 1)
            last.then_inc(logits_ready, 1)

        @block.scalar
        def _(act):
            if again:
                act.wait_ge(var_ready, 1)
                nc.scalar.activation(dev[:, :], var[:, :], ACT.Sqrt).then_inc(dev_ready, 1)
            act.wait_ge(shifted, 1)
            nc.scalar.activation(p[:, :, :], p[:, :, :], ACT.Exp).then_inc(exp_ready, 1)

        @block.vector
        def _(dve):
            v = nc.vector
            wide = [P, TILES, E]

            def by_token(x):
                return x[:, :].unsqueeze(2).to_broadcast(wide)

            if again:
                dve.wait_ge(loaded, 48)
                for k in range(DK):
                    v.tensor_scalar(w_shift[:, k, :], w[:, k, :], affine[:, 1, k:k + 1], None, ALU.mult)
                dve.drain()
                for k in range(DK):
                    last = v.tensor_scalar(w[:, k, :], w[:, k, :], affine[:, 0, k:k + 1], None, ALU.mult)
                last.then_inc(weights_ready, 1)
                token_statistics(nc, dve, c.XN, stats, mean, diff, var, var_ready)
                dve.wait_ge(dev_ready, 1)
                reciprocal_root(nc, dve, var, dev, rstd)
                dve.wait_ge(logits_ready, 1)
                v.tensor_copy(sums[:, :, :], sums_ps[:, :, :])
                dve.drain()
                v.tensor_tensor(p[:, :, :], by_token(mean), sums[:, 0, :].unsqueeze(1).to_broadcast(wide), ALU.mult)
                dve.drain()
                v.tensor_tensor(p[:, :, :], logits[:, :, :], p[:, :, :], ALU.subtract)
                dve.drain()
                v.tensor_tensor(p[:, :, :], p[:, :, :], by_token(rstd), ALU.mult)
                dve.drain()
                v.tensor_tensor(p[:, :, :], p[:, :, :], sums[:, 1, :].unsqueeze(1).to_broadcast(wide), ALU.add)
                dve.drain()
                value = p
            else:
                dve.wait_ge(logits_ready, 1)
                value = logits
            v.tensor_reduce(one[:, :], value[:, :, :], AX.X, ALU.max)
            dve.drain()
            v.tensor_tensor(p[:, :, :], value[:, :, :], by_token(one), ALU.subtract).then_inc(shifted, 1)
            dve.wait_ge(exp_ready, 1)
            v.tensor_reduce(one[:, :], p[:, :, :], AX.X, ALU.add)
            dve.drain()
            v.reciprocal(one[:, :], one[:, :])
            dve.drain()
            v.tensor_tensor(p[:, :, :], p[:, :, :], by_token(one), ALU.mult)
            dve.drain()
            for t in range(TILES):
                v.max(top[:, t, :], p[:, t, :])
            dve.drain()
            for t in range(TILES):
                v.max_index(at[:, t, :], top[:, t, :], p[:, t, :])
            dve.drain()
            v.tensor_copy(atf[:, :, :], at[:, :, :])
            if eps is not None:
                v.tensor_tensor(one[:, :], top[:, :, 0], top[:, :, 1], ALU.add)
                dve.drain()
                v.tensor_scalar(one[:, :], one[:, :], eps, None, ALU.add)
                dve.drain()
                v.reciprocal(one[:, :], one[:, :])
                dve.drain()
                v.tensor_tensor(top[:, :, 0:CHOICES], top[:, :, 0:CHOICES],
                                one[:, :].unsqueeze(2).to_broadcast([P, TILES, CHOICES]), ALU.mult)
            dve.drain()
            by_expert = [P, E, TILES]
            iota = c.iota[:, 0:E].unsqueeze(2).to_broadcast(by_expert)
            for rank in range(CHOICES):
                kt = slice(rank * TILES, (rank + 1) * TILES)
                v.tensor_tensor(c.chosen[:, 0:E, kt], iota, atf[:, :, rank].unsqueeze(1).to_broadcast(by_expert),
                                ALU.is_equal)
                v.tensor_copy(c.share[:, kt], top[:, :, rank])
            dve.drain()


def store_output(nc, c, out):
    with ExitStack() as ctx:
        sb, ps, sem = sub_memory(nc, ctx)
        final, stored = sem("final"), sem("stored")
        block = ctx.enter_context(nc.Block())
        HALF = TILES // 2

        @block.vector
        def _(dve):
            for h in range(2):
                t = slice(h * HALF, (h + 1) * HALF)
                nc.vector.scalar_tensor_tensor(c.X[:, t, :], c.ACC[:, t, :], c.gate[:, c.last:c.last + 1], c.X[:, t, :],
                                               ALU.mult, ALU.add).then_inc(final, 1)

        @block.sync
        def _(sp):
            y = out.rearrange("b (i p) d -> p (b i) d", p=P)
            for h in range(2):
                t = slice(h * HALF, (h + 1) * HALF)
                sp.wait_ge(final, h + 1)
                sp.dma_start(y[:, t, :], c.X[:, t, :]).then_inc(stored, 16)
            sp.wait_ge(stored, 32)


def layer1_attention(nc, c, a):
    HEADS, DH = 8, 128
    INNER = HEADS * DH
    HALF = HEADS // 2
    SCALE = float(DH) ** -0.25
    ROWS = TPB * HEADS
    with ExitStack() as ctx:
        sb, ps, sem = sub_memory(nc, ctx, "a1_")
        wq = sb("wq", [P, DK, INNER])
        wk = sb("wk", [CP, CK, INNER])
        wv = sb("wv", [CP, CK, INNER])
        wo = sb("wo", [P, HEADS, DIM])
        bo = sb("bo", [P, DIM])
        context = sb("context", [CP, 2, CK, KEYS])
        q = sb("q", [P, HEADS, SEQ])
        k = sb("k", [P, HEADS, KEYS])
        v = sb("v", [KEYS, 2, INNER])
        probs = sb("probs", [P, TPB * 2, HALF * KEYS])
        stat = sb("stat", [P, ROWS])
        probs_t = sb("probs_t", [KEYS, ROWS, P])
        mixed = sb("mixed", [P, HEADS, SEQ])
        A = ps("A", [P, 4, 512])
        B = ps("B", [P, 4, 512])
        w_loaded = sem("w_loaded")
        ctx_loaded = [sem(f"ctx_loaded{u}") for u in range(2)]
        q_ready, kv_ready, kv_done = sem("q_ready"), sem("kv_ready"), sem("kv_done")
        q_done = sem("q_done")
        scores_ready, scores_read = sem("scores_ready"), sem("scores_read")
        shifted, exp_done, probs_ready = sem("shifted"), sem("exp_done"), sem("probs_ready")
        turned, turned_done = sem("turned"), sem("turned_done")
        mixed_ready, mixed_done = sem("mixed_ready"), sem("mixed_done")
        out_ready, out_done = sem("out_ready"), sem("out_done")
        block = ctx.enter_context(nc.Block())

        def batches(eng, body):
            with eng.Fori(0, BATCH // 2 - 1) as g:
                for u in range(2):
                    body(g * 2 + u, u, False)
            for b in range(BATCH - 2, BATCH):
                body(b, b % 2, b == BATCH - 1)

        @block.sync
        def _(sp):
            def load(b, u):
                sp.dma_start(context[:, u, :, :].unsqueeze(1),
                             a["context_T"][pieces(b), :, :].rearrange("b (k p) s -> p b k s", p=CP))\
                  .then_inc(ctx_loaded[u], 16)

            load(0, 0)
            load(1, 1)
            sp.dma_start(wq[:, :, :], a["L1_xattn_Wq"].rearrange("(k p) n -> p k n", p=P)).then_inc(w_loaded, 16)
            sp.dma_start(wk[:, :, :], a["L1_xattn_Wk"].rearrange("(k p) n -> p k n", p=CP)).then_inc(w_loaded, 16)
            sp.dma_start(wv[:, :, :], a["L1_xattn_Wv"].rearrange("(k p) n -> p k n", p=CP)).then_inc(w_loaded, 16)
            sp.dma_start(wo[:, :, :], a["L1_xattn_Wo"].rearrange("(h p) n -> p h n", p=P)).then_inc(w_loaded, 16)
            sp.dma_start(bo[:, :], spread(a["L1_xattn_bo"])).then_inc(w_loaded, 16)
            with sp.Fori(1, BATCH // 2) as g:
                for u in range(2):
                    sp.wait_ge(kv_ready, g * 2 + (u - 1))
                    load(g * 2 + u, u)

        @block.tensor
        def _(pe):
            def project(b, u):
                pe.wait_ge(out_done, b + 1)
                for h in range(HEADS):
                    for kk in range(DK):
                        last = nc.tensor.matmul(B[:, h // 2, (h % 2) * SEQ:(h % 2 + 1) * SEQ],
                                                wq[:, kk, h * DH:(h + 1) * DH],
                                                c.XT[:, kk, pieces(b * SEQ, SEQ)], start=kk == 0, stop=kk == DK - 1)
                last.then_inc(q_ready, 1)
                pe.wait_ge(ctx_loaded[u], (b // 2 + 1) * 16 if isinstance(b, int) else b * 8 + (16 - 8 * u))
                pe.wait_ge(scores_read, b + 1)
                for h in range(HEADS):
                    for kk in range(CK):
                        nc.tensor.matmul(A[:, h // HALF, (h % HALF) * KEYS:(h % HALF + 1) * KEYS],
                                         wk[:, kk, h * DH:(h + 1) * DH], context[:, u, kk, :],
                                         start=kk == 0, stop=kk == CK - 1)
                for n in range(INNER // 512):
                    for kk in range(CK):
                        last = nc.tensor.matmul(A[0:KEYS, 2 + n, :], context[:, u, kk, :],
                                                wv[:, kk, n * 512:(n + 1) * 512], start=kk == 0, stop=kk == CK - 1)
                last.then_inc(kv_ready, 1)

            def body(b, u, final):
                pe.wait_ge(q_done, b + 1)
                pe.wait_ge(kv_done, b + 1)
                pe.wait_ge(mixed_done, b + 1)
                for i in range(TPB):
                    for h in range(HEADS):
                        last = nc.tensor.matmul(A[:, 2 * i + h // HALF, (h % HALF) * KEYS:(h % HALF + 1) * KEYS],
                                                q[:, h, i * P:(i + 1) * P], k[:, h, :], start=True, stop=True)
                last.then_inc(scores_ready, 1)
                if not final:
                    project(b + 1, 1 - u)
                pe.wait_ge(probs_ready, b + 1)
                if not final:
                    pe.wait_ge(q_done, b + 2)
                else:
                    pe.wait_ge(out_done, b + 2)
                for r in range(ROWS):
                    last = nc.tensor.transpose(B[0:KEYS, r // 4, (r % 4) * P:(r % 4 + 1) * P],
                                               probs[:, r // HALF, (r % HALF) * KEYS:(r % HALF + 1) * KEYS],
                                               c.ident[:, :])
                last.then_inc(turned, 1)
                pe.wait_ge(turned_done, b + 1)
                if not final:
                    pe.wait_ge(kv_done, b + 2)
                for h in range(HEADS):
                    last = nc.tensor.matmul(A[:, h // 2, (h % 2) * SEQ:(h % 2 + 1) * SEQ]
                                            .rearrange("p (i t) -> p i t", t=P),
                                            v[:, u, h * DH:(h + 1) * DH],
                                            probs_t[:, h:ROWS:HEADS, :], start=True, stop=True)
                last.then_inc(mixed_ready, 1)
                pe.wait_ge(mixed_done, b + 2)
                for i in range(TPB):
                    for h in range(HEADS):
                        last = nc.tensor.matmul(B[:, i, 0:DIM], mixed[:, h, i * P:(i + 1) * P], wo[:, h, :],
                                                start=h == 0, stop=h == HEADS - 1)
                last.then_inc(out_ready, 1)

            pe.wait_ge(w_loaded, 80)
            project(0, 0)
            batches(pe, body)

        @block.scalar
        def _(act):
            act.sem_inc(mixed_done, 1)

            def evacuate_qkv(b, u):
                act.wait_ge(q_ready, b + 1)
                nc.scalar.activation(q[:, :, :].rearrange("p (b h) s -> p b (h s)", b=4), B[:, :, :], ACT.Copy,
                                     scale=SCALE).then_inc(q_done, 1)
                act.wait_ge(kv_ready, b + 1)
                nc.scalar.activation(k[:, :, :].rearrange("p (b h) s -> p b (h s)", b=2),
                                     A[:, 0:2, 0:HALF * KEYS], ACT.Copy, scale=SCALE)
                nc.scalar.activation(v[:, u, :].rearrange("p (b n) -> p b n", b=2), A[0:KEYS, 2:4, :],
                                     ACT.Copy).then_inc(kv_done, 1)

            def body(b, u, final):
                if not final:
                    act.wait_ge(scores_ready, b + 1)
                    evacuate_qkv(b + 1, 1 - u)
                act.wait_ge(shifted, b + 1)
                nc.scalar.activation(probs[:, :, :], probs[:, :, :], ACT.Exp).then_inc(exp_done, 1)
                act.wait_ge(turned, b + 1)
                nc.scalar.activation(probs_t[:, :, :].rearrange("p (b r) t -> p b (r t)", b=4), B[0:KEYS, :, :],
                                     ACT.Copy).then_inc(turned_done, 1)
                act.wait_ge(mixed_ready, b + 1)
                nc.scalar.activation(mixed[:, :, :].rearrange("p (b h) s -> p b (h s)", b=4), A[:, :, :],
                                     ACT.Copy).then_inc(mixed_done, 1)

            evacuate_qkv(0, 0)
            batches(act, body)

        @block.vector
        def _(dve):
            vv = nc.vector
            grid = [P, ROWS, KEYS]
            probs_r = probs[:, :, :].rearrange("p a (h s) -> p (a h) s", s=KEYS)
            scores_r = A[:, :, 0:HALF * KEYS].rearrange("p a (h s) -> p a h s", s=KEYS)
            stat_r = stat[:, :].rearrange("p (a h) -> p a h", h=HALF)
            dve.sem_inc(scores_read, 1)
            dve.sem_inc(out_done, 2)
            dve.wait_ge(w_loaded, 80)

            def body(b, u, final):
                dve.wait_ge(scores_ready, b + 1)
                vv.tensor_reduce(stat_r, scores_r, AX.X, ALU.max)
                dve.drain()
                vv.tensor_tensor(probs[:, :, :].rearrange("p a (h s) -> p a h s", s=KEYS), scores_r,
                                 stat_r.unsqueeze(3).to_broadcast([P, 2 * TPB, HALF, KEYS]), ALU.subtract)
                dve.drain()
                dve.sem_inc(scores_read, 1)
                dve.sem_inc(shifted, 1)
                dve.wait_ge(exp_done, b + 1)
                vv.tensor_reduce(stat[:, :], probs_r, AX.X, ALU.add)
                dve.drain()
                vv.reciprocal(stat[:, :], stat[:, :])
                dve.drain()
                vv.tensor_tensor(probs_r, probs_r, stat[:, :].unsqueeze(2).to_broadcast(grid), ALU.mult)\
                  .then_inc(probs_ready, 1)
                dve.wait_ge(out_ready, b + 1)
                vv.tensor_tensor(c.ACC[:, pieces(b * TPB, TPB), :], B[:, 0:TPB, 0:DIM],
                                 bo[:, :].unsqueeze(1).to_broadcast([P, TPB, DIM]), ALU.add).then_inc(out_done, 1)

            batches(dve, body)


def narrow_attention(nc, c, a, layer):
    HEADS, DH = 16, 16
    HT = P // DH
    SCALE = float(DH) ** -0.5
    CLAMP = 10000.0
    final_layer = layer == 3
    with ExitStack() as ctx:
        sb, ps, sem = sub_memory(nc, ctx, f"a{layer}_")
        wq = sb("wq", [P, DK, DIM])
        wk = sb("wk", [CP, CK, DIM])
        wv = sb("wv", [CP, CK, DIM])
        context = sb("context", [CP, 2, CK, KEYS])
        q = sb("q", [P, DK, SEQ])
        k = sb("k", [P, 2, DK, KEYS])
        k_wide = sb("k_wide", [P, DK, HT, KEYS])
        v = sb("v", [KEYS, 2, DIM])
        probs = sb("probs", [P, TPB, HEADS, KEYS])
        stat = sb("stat", [P, TPB, HEADS])
        probs_t = sb("probs_t", [KEYS, 2, 8, P])
        if final_layer:
            mask8 = sb("mask8", [P, TILES], U8)
            keep = sb("keep", [P, TILES])
            fill = sb("fill", [P, TILES])
        else:
            wo = sb("wo", [P, DK, DIM])
            bqk = sb("bqk", [P, 2, DK])
            bo = sb("bo", [P, DIM])
            bv = sb("bv", [P, DIM])
            mixed = sb("mixed", [P, DIM])
            mixed_t = sb("mixed_t", [P, DK, P])
        S = ps("scores", [P, 4, 512])
        T = ps("turned", [P, 2, 512])
        Q = ps("q_ps", [P, DK, SEQ])
        KV = ps("kv_ps", [P, 512])
        w_loaded = sem("w_loaded")
        ctx_loaded = [sem(f"ctx_loaded{u}") for u in range(2)]
        setup_done = sem("setup_done")
        q_ready, kv_ready, q_done, kv_done = sem("q_ready"), sem("kv_ready"), sem("q_done"), sem("kv_done")
        k_wide_ready = sem("k_wide_ready")
        scores_ready, scores_read = sem("scores_ready"), sem("scores_read")
        shifted, exp_done = sem("shifted"), sem("exp_done")
        turned, turned_done = sem("turned"), sem("turned_done")
        mixed_ready, mixed_done = sem("mixed_ready"), sem("mixed_done")
        mt_ready, mt_done = sem("mt_ready"), sem("mt_done")
        out_ready, out_done = sem("out_ready"), sem("out_done")
        block = ctx.enter_context(nc.Block())
        LOADS = 48 + (16 if final_layer else 80)

        def batches(eng, body):
            with eng.Fori(0, BATCH // 2 - 1) as g:
                for u in range(2):
                    body(g * 2 + u, u, False)
            for b in range(BATCH - 2, BATCH):
                body(b, b % 2, b == BATCH - 1)

        @block.sync
        def _(sp):
            def load(b, u):
                sp.dma_start(context[:, u, :, :].unsqueeze(1),
                             a["context_T"][pieces(b), :, :].rearrange("b (k p) s -> p b k s", p=CP))\
                  .then_inc(ctx_loaded[u], 16)

            load(0, 0)
            load(1, 1)
            if final_layer:
                weights = [(wq, a["L3_Wq_T"], P), (wk, a["L3_Wkv_T"][:, 0:DIM], CP),
                           (wv, a["L3_Wkv_T"][:, DIM:2 * DIM], CP)]
            else:
                weights = [(wq, a["L2_xattn_Wq"], P), (wk, a["L2_xattn_Wk"], CP), (wv, a["L2_xattn_Wv"], CP),
                           (wo, a["L2_xattn_Wo"], P)]
            for dst, src, p in weights:
                sp.dma_start(dst[:, :, :], src.rearrange("(k p) n -> p k n", p=p)).then_inc(w_loaded, 16)
            if final_layer:
                sp.dma_start(mask8[:, :], a["mask_BxS_bk0"]).then_inc(w_loaded, 16)
            else:
                sp.dma_start(bqk[:, 0, :], a["L2_bq"]).then_inc(w_loaded, 16)
                sp.dma_start(bqk[:, 1, :], a["L2_bk"]).then_inc(w_loaded, 16)
                sp.dma_start(bo[:, :], spread(a["L2_xattn_bo"])).then_inc(w_loaded, 16)
                sp.dma_start(bv[:, :], spread(a["L2_xattn_bv"])).then_inc(w_loaded, 16)
            with sp.Fori(1, BATCH // 2) as g:
                for u in range(2):
                    sp.wait_ge(kv_ready, g * 2 + (u - 1))
                    load(g * 2 + u, u)

        @block.tensor
        def _(pe):
            def project(b, u):
                pe.wait_ge(out_done, b * TPB + 1)
                for m in range(DK):
                    for kk in range(DK):
                        last = nc.tensor.matmul(Q[:, m, :], wq[:, kk, m * P:(m + 1) * P],
                                                c.XT[:, kk, pieces(b * SEQ, SEQ)], start=kk == 0, stop=kk == DK - 1)
                last.then_inc(q_ready, 1)
                pe.wait_ge(ctx_loaded[u], (b // 2 + 1) * 16 if isinstance(b, int) else b * 8 + (16 - 8 * u))
                pe.wait_ge(kv_done, b + 1)
                for m in range(DK):
                    for kk in range(CK):
                        nc.tensor.matmul(KV[:, m * KEYS:(m + 1) * KEYS], wk[:, kk, m * P:(m + 1) * P],
                                         context[:, u, kk, :], start=kk == 0, stop=kk == CK - 1)
                for kk in range(CK):
                    last = nc.tensor.matmul(KV[0:KEYS, DIM:2 * DIM], context[:, u, kk, :], wv[:, kk, :],
                                            start=kk == 0, stop=kk == CK - 1)
                last.then_inc(kv_ready, 1)

            def scores(b, i):
                n = b * TPB + i
                pe.wait_ge(scores_read, n + 1)
                for h in range(0, HEADS, 4):
                    m = h // HT
                    last = nc.tensor.matmul(S[:, h // 4, 0:4 * KEYS], q[:, m, i * P:(i + 1) * P],
                                            k_wide[:, m, h % HT:h % HT + 4, :].rearrange("p h s -> p (h s)"),
                                            start=True, stop=True)
                last.then_inc(scores_ready, 1)

            def mix(b, i, u):
                n = b * TPB + i
                pe.wait_ge(exp_done, n + 1)
                for half in range(2):
                    pe.wait_ge(turned_done, n * 2 + half + 1)
                    for r in range(8):
                        last = nc.tensor.transpose(T[0:KEYS, r // 4, (r % 4) * P:(r % 4 + 1) * P],
                                                   probs[:, i, half * 8 + r, :], c.ident[:, :])
                    last.then_inc(turned, 1)
                    if half == 0:
                        pe.wait_ge(out_done, n + 3)
                        if i == 0:
                            pe.wait_ge(q_done, (b + 2) if not isinstance(b, int) or b + 1 < BATCH else b + 1)
                    pe.wait_ge(turned_done, n * 2 + half + 2)
                    for r in range(8):
                        h = half * 8 + r
                        last = nc.tensor.matmul(Q[:, 0, h * DH:(h + 1) * DH], probs_t[:, half, r, :],
                                                v[:, u, h * DH:(h + 1) * DH], start=True, stop=True)
                last.then_inc(mixed_ready, 1)
                if not final_layer:
                    pe.wait_ge(mixed_done, n + 1)
                    for m in range(DK):
                        last = nc.tensor.transpose(Q[:, 1, m * P:(m + 1) * P], mixed[:, m * P:(m + 1) * P],
                                                   c.ident[:, :])
                    last.then_inc(mt_ready, 1)
                    pe.wait_ge(mt_done, n + 1)
                    for m in range(DK):
                        last = nc.tensor.matmul(Q[:, 0, :], mixed_t[:, m, :], wo[:, m, :], start=m == 0,
                                                stop=m == DK - 1)
                    last.then_inc(out_ready, 1)

            def body(b, u, final):
                pe.wait_ge(q_done, b + 1)
                pe.wait_ge(k_wide_ready, b + 1)
                pe.wait_ge(kv_done, b + 2)
                scores(b, 0)
                scores(b, 1)
                if not final:
                    project(b + 1, 1 - u)
                mix(b, 0, u)
                mix(b, 1, u)

            pe.wait_ge(w_loaded, LOADS)
            project(0, 0)
            batches(pe, body)

        @block.scalar
        def _(act):
            act.sem_inc(kv_done, 1)
            act.sem_inc(turned_done, 1)
            act.wait_ge(setup_done, 1)

            def evacuate_qkv(b, u):
                act.wait_ge(q_ready, b + 1)
                for m in range(DK):
                    if final_layer:
                        last = nc.scalar.activation(q[:, m, :], Q[:, m, :], ACT.Copy, scale=SCALE)
                    else:
                        last = nc.scalar.activation(q[:, m, :], Q[:, m, :], ACT.Identity, bias=bqk[:, 0, m:m + 1])
                last.then_inc(q_done, 1)
                act.wait_ge(kv_ready, b + 1)
                for m in range(DK):
                    if final_layer:
                        nc.scalar.activation(k[:, u, m, :], KV[:, m * KEYS:(m + 1) * KEYS], ACT.Copy)
                    else:
                        nc.scalar.activation(k[:, u, m, :], KV[:, m * KEYS:(m + 1) * KEYS], ACT.Identity,
                                             bias=bqk[:, 1, m:m + 1])
                nc.scalar.activation(v[:, u, :], KV[0:KEYS, DIM:2 * DIM], ACT.Copy).then_inc(kv_done, 1)

            def body(b, u, final):
                if not final:
                    act.wait_ge(scores_ready, b * TPB + TPB)
                    evacuate_qkv(b + 1, 1 - u)
                for i in range(TPB):
                    n = b * TPB + i
                    act.wait_ge(shifted, n + 1)
                    nc.scalar.activation(probs[:, i, :, :], probs[:, i, :, :], ACT.Exp,
                                         scale=1.0 if final_layer else SCALE).then_inc(exp_done, 1)
                for i in range(TPB):
                    n = b * TPB + i
                    for half in range(2):
                        act.wait_ge(turned, n * 2 + half + 1)
                        nc.scalar.activation(probs_t[:, half, :, :].rearrange("p (b r) t -> p b (r t)", b=2),
                                             T[0:KEYS, :, :], ACT.Copy).then_inc(turned_done, 1)
                    if not final_layer:
                        act.wait_ge(mt_ready, n + 1)
                        nc.scalar.activation(mixed_t[:, :, :], Q[:, 1, :].rearrange("p (m t) -> p m t", t=P),
                                             ACT.Copy).then_inc(mt_done, 1)

            evacuate_qkv(0, 0)
            batches(act, body)

        @block.gpsimd
        def _(pool):
            pool.wait_ge(setup_done, 1)
            wide = [P, HT, KEYS]

            def body(b, u, final):
                pool.wait_ge(kv_done, b + 2)
                pool.wait_ge(scores_ready, b * TPB)
                for m in range(DK):
                    last = nc.gpsimd.tensor_tensor(k_wide[:, m, :, :], k[:, u, m, :].unsqueeze(1).to_broadcast(wide),
                                                   c.headmask[:, 4:4 + HT].unsqueeze(2).to_broadcast(wide), ALU.mult)
                last.then_inc(k_wide_ready, 1)

            pool.wait_ge(kv_done, 2)
            for m in range(DK):
                last = nc.gpsimd.tensor_tensor(k_wide[:, m, :, :], k[:, 0, m, :].unsqueeze(1).to_broadcast(wide),
                                               c.headmask[:, 4:4 + HT].unsqueeze(2).to_broadcast(wide), ALU.mult)
            last.then_inc(k_wide_ready, 1)
            with pool.Fori(0, BATCH // 2 - 1) as g:
                for u in range(2):
                    body(g * 2 + (u + 1), 1 - u, False)
            body(BATCH - 1, 1, True)

        @block.vector
        def _(dve):
            vv = nc.vector
            dve.sem_inc(scores_read, 1)
            dve.sem_inc(out_done, 3)
            dve.wait_ge(w_loaded, LOADS)
            if final_layer:
                vv.tensor_copy(keep[:, :], mask8[:, :])
                dve.drain()
                vv.tensor_scalar(fill[:, :], keep[:, :], 1.0, 1.0e9, ALU.subtract, ALU.mult)
                dve.drain()
            dve.sem_inc(setup_done, 1)
            scores_r = S[:, :, 0:4 * KEYS]

            def body(b, u, final):
                for i in range(TPB):
                    n = b * TPB + i
                    pr = probs[:, i, :, :]
                    st = stat[:, i, :]
                    dve.wait_ge(scores_ready, n + 1)
                    grouped = pr.rearrange("p (b h) s -> p b (h s)", b=4)
                    if final_layer:
                        vv.tensor_scalar(grouped, scores_r, keep[:, pieces(n)], fill[:, pieces(n)],
                                         ALU.mult, ALU.add).then_inc(scores_read, 1)
                    else:
                        vv.tensor_scalar(grouped, scores_r, CLAMP / SCALE, -CLAMP / SCALE,
                                         ALU.min, ALU.max).then_inc(scores_read, 1)
                    dve.drain()
                    vv.tensor_reduce(st, pr, AX.X, ALU.max)
                    dve.drain()
                    vv.tensor_tensor(pr, pr, st.unsqueeze(2).to_broadcast([P, HEADS, KEYS]), ALU.subtract)\
                      .then_inc(shifted, 1)
                for i in range(TPB):
                    n = b * TPB + i
                    st = stat[:, i, :]
                    dve.wait_ge(exp_done, n + 1)
                    vv.tensor_reduce(st, probs[:, i, :, :], AX.X, ALU.add)
                    dve.drain()
                    vv.reciprocal(st, st)
                    dve.drain()
                    dve.wait_ge(mixed_ready, n + 1)
                    split = [P, HEADS, DH]
                    mixed_ps = Q[:, 0, :].rearrange("p (h d) -> p h d", d=DH)
                    norm = st.unsqueeze(2).to_broadcast(split)
                    if final_layer:
                        vv.tensor_tensor(c.ACC[:, pieces(n), :].rearrange("p a (h d) -> p (a h) d", d=DH), mixed_ps,
                                         norm, ALU.mult).then_inc(out_done, 1)
                    else:
                        vv.tensor_tensor(mixed[:, :].rearrange("p (h d) -> p h d", d=DH), mixed_ps, norm, ALU.mult)
                        dve.drain()
                        vv.tensor_tensor(mixed[:, :], mixed[:, :], bv[:, :], ALU.add).then_inc(mixed_done, 1)
                        dve.wait_ge(out_ready, n + 1)
                        vv.tensor_tensor(c.ACC[:, pieces(n), :], Q[:, 0, :].unsqueeze(1), bo[:, :].unsqueeze(1),
                                         ALU.add).then_inc(out_done, 1)

            batches(dve, body)


def adapter_layer(nc, c, a):
    E, H = 8, 64
    PAIR = P // H
    M = E // PAIR
    with ExitStack() as ctx:
        sb, ps, sem = sub_memory(nc, ctx, "f2_")
        w_base = sb("w_base", [P, DK, DIM])
        w_in = sb("w_in", [P, 2, DK, E, H])
        w_out = sb("w_out", [P, 2, M, DIM])
        b_in = sb("b_in", [P, 2, M])
        b_recon = sb("b_recon", [P, E, DK])
        b_base = sb("b_base", [P, DIM])
        b_up = sb("b_up", [E, DIM])
        hidden = sb("hidden", [P, 2, M, BLOCK])
        diff = sb("diff", [P, 2, BLOCK])
        losses = sb("losses", [P, BATCH, E * DK])
        loss = sb("loss", [P, BATCH, E])
        least = sb("least", [P, BATCH])
        pick = sb("pick", [P, BATCH, E])
        pick_rows = sb("pick_rows", [E, BATCH])
        pick_wide = sb("pick_wide", [E, BATCH, P])
        scale = sb("scale", [P, M, BATCH])
        shift = sb("shift", [P, M, BATCH])
        ones = sb("ones", [P, P])
        hid_ps = [ps(f"hid{i}", [P, BLOCK]) for i in range(2)]
        rec_ps = [ps(f"rec{i}", [P, BLOCK]) for i in range(2)]
        out_ps = [ps(f"out{i}", [P, BLOCK]) for i in range(2)]
        loss_ps = ps("loss_ps", [P, BATCH, E * DK])
        loaded = sem("loaded")
        hid_ready, hid_done = sem("hid_ready"), sem("hid_done")
        rec_ready, rec_free = sem("rec_ready"), sem("rec_free")
        squared = sem("squared")
        ones_ready, loss_ready, picked = sem("ones_ready"), sem("loss_ready"), sem("picked")
        out_ready, out_done = sem("out_ready"), sem("out_done")
        block = ctx.enter_context(nc.Block())
        SB = BLOCK // SEQ
        RECS = E * DK

        @block.sync
        def _(sp):
            with nc.allow_non_contiguous_dma("small biases"):
                for n, w in enumerate(("L2_ffn_Wd1", "L2_ffn_Wa_down")):
                    for kk in range(DK):
                        sp.dma_start(w_in[:, n, kk, :, :],
                                     a[w][:, kk * P:(kk + 1) * P, :].rearrange("e p h -> p e h")).then_inc(loaded, 16)
                for n, w in enumerate(("L2_ffn_Wd2", "L2_ffn_Wa_up")):
                    sp.dma_start(w_out[:, n, :, :], a[w].rearrange("(m a) h d -> (a h) m d", a=PAIR))\
                      .then_inc(loaded, 16)
                sp.dma_start(b_in[:, 0, :], a["L2_bd1"]).then_inc(loaded, 16)
                sp.dma_start(b_in[:, 1, :], a["L2_ba_down"]).then_inc(loaded, 16)
                sp.dma_start(b_recon[:, :, :], a["L2_bd2"]).then_inc(loaded, 16)
                sp.dma_start(w_base[:, :, :], a["L2_ffn_W_base"].rearrange("(k p) n -> p k n", p=P)).then_inc(loaded, 16)
                sp.dma_start(b_base[:, :], spread(a["L2_ffn_b_base"])).then_inc(loaded, 16)
                sp.dma_start(b_up[:, :], a["L2_ffn_ba_up"]).then_inc(loaded, 16)
        LOADS = 12 * 16

        @block.tensor
        def _(pe):
            def hidden_block(g, u, which, columns):
                n = g * 2 + (u + which * BLOCKS)
                for m in range(M):
                    pe.wait_ge(hid_done, n * M + (m + 1))
                    for kk in range(DK):
                        last = nc.tensor.matmul(hid_ps[m % 2][:, :],
                                                w_in[:, which, kk, m * PAIR:(m + 1) * PAIR, :]
                                                .rearrange("p e h -> p (e h)"),
                                                c.XT[:, kk, columns], start=kk == 0, stop=kk == DK - 1)
                    last.then_inc(hid_ready, 1)

            pe.wait_ge(loaded, LOADS)
            with pe.Fori(0, BLOCKS // 2) as g:
                for u in range(2):
                    hidden_block(g, u, 0, pieces(g * (2 * BLOCK) + u * BLOCK, BLOCK))
                    pe.wait_ge(hid_done, g * (2 * M) + (u * M + M + 2))
                    for e in range(E):
                        rows = slice((e % PAIR) * H, (e % PAIR + 1) * H)
                        for m in range(DK):
                            r = e * DK + m
                            pe.wait_ge(rec_free, g * (2 * RECS) + (u * RECS + r + 1))
                            nc.tensor.matmul(rec_ps[r % 2][:, :], w_out[rows, 0, e // PAIR, m * P:(m + 1) * P],
                                             hidden[rows, u, e // PAIR, :], start=True, stop=True)\
                              .then_inc(rec_ready, 1)
            pe.wait_ge(squared, BLOCKS * RECS + 2)
            pe.wait_ge(ones_ready, 1)
            nc.tensor.matmul(loss_ps[:, :, :].rearrange("p b r -> p (b r)"), ones[:, :],
                             losses[:, :, :].rearrange("p b r -> p (b r)"), start=True, stop=True)\
              .then_inc(loss_ready, 1)
            pe.wait_ge(picked, 1)
            for blk in range(BLOCKS):
                hidden_block(blk // 2, blk % 2, 1, slice(blk * BLOCK, (blk + 1) * BLOCK))
                pe.wait_ge(hid_done, (BLOCKS + blk + 1) * M + 2)
                for i in range(TPK):
                    t = blk * TPK + i
                    pe.wait_ge(out_done, t + 1)
                    o = out_ps[t % 2][:, 0:DIM]
                    for kk in range(DK):
                        nc.tensor.matmul(o, c.XT[:, kk, t * P:(t + 1) * P], w_base[:, kk, :], start=kk == 0, stop=False)
                    for m in range(M):
                        nc.tensor.matmul(o, hidden[:, blk % 2, m, i * P:(i + 1) * P], w_out[:, 1, m, :], start=False,
                                         stop=False)
                    nc.tensor.matmul(o, pick_wide[:, t // TPB, :], b_up[:, :], start=False, stop=True)\
                      .then_inc(out_ready, 1)

        @block.scalar
        def _(act):
            act.sem_inc(hid_done, 2)
            act.sem_inc(squared, 2)
            act.wait_ge(loaded, LOADS)
            with act.Fori(0, BLOCKS // 2) as g:
                for u in range(2):
                    for m in range(M):
                        act.wait_ge(hid_ready, g * (2 * M) + (u * M + m + 1))
                        nc.scalar.activation(hidden[:, u, m, :], hid_ps[m % 2][:, :], ACT.Relu,
                                             bias=b_in[:, 0, m:m + 1]).then_inc(hid_done, 1)
                    for r in range(RECS):
                        act.wait_ge(rec_free, g * (2 * RECS) + (u * RECS + r + 3))
                        for s in range(SB):
                            b = g * (2 * SB) + (u * SB + s)
                            last = nc.scalar.activation(diff[:, r % 2, s * SEQ:(s + 1) * SEQ],
                                                        diff[:, r % 2, s * SEQ:(s + 1) * SEQ], ACT.Square,
                                                        accum_out=losses[:, pieces(b), r])
                        last.then_inc(squared, 1)
            act.wait_ge(picked, 1)
            for blk in range(BLOCKS):
                if blk >= 2:
                    act.wait_ge(out_ready, (blk - 1) * TPK)
                for m in range(M):
                    act.wait_ge(hid_ready, (BLOCKS + blk) * M + m + 1)
                    for s in range(SB):
                        b = blk * SB + s
                        cols = slice(s * SEQ, (s + 1) * SEQ)
                        last = nc.scalar.activation(hidden[:, blk % 2, m, cols], hid_ps[m % 2][:, cols], ACT.Relu,
                                                    bias=shift[:, m, b:b + 1], scale=scale[:, m, b:b + 1])
                    last.then_inc(hid_done, 1)

        @block.vector
        def _(dve):
            v = nc.vector
            dve.sem_inc(rec_free, 2)
            dve.sem_inc(out_done, 2)
            v.memset(ones[:, :], 1.0).then_inc(ones_ready, 1)
            dve.wait_ge(loaded, LOADS)
            with dve.Fori(0, BLOCKS // 2) as g:
                for u in range(2):
                    columns = pieces(g * (2 * BLOCK) + u * BLOCK, BLOCK)
                    for e in range(E):
                        for m in range(DK):
                            r = e * DK + m
                            dve.wait_ge(rec_ready, g * (2 * RECS) + (u * RECS + r + 1))
                            dve.wait_ge(squared, g * (2 * RECS) + (u * RECS + r + 1))
                            v.scalar_tensor_tensor(diff[:, r % 2, :], rec_ps[r % 2][:, :], b_recon[:, e, m:m + 1],
                                                   c.XT[:, m, columns], ALU.add, ALU.subtract).then_inc(rec_free, 1)
            dve.wait_ge(loss_ready, 1)
            wide = [P, BATCH, E]

            def tt(*args):
                v.tensor_tensor(*args)
                dve.drain()

            v.tensor_reduce(loss[:, :, :], loss_ps[:, :, :].rearrange("p b (e m) -> p b e m", m=DK), AX.X, ALU.add)
            dve.drain()
            v.tensor_reduce(least[:, :], loss[:, :, :], AX.X, ALU.min)
            dve.drain()
            iota = c.iota[:, 0:E].unsqueeze(1).to_broadcast(wide)
            tt(pick[:, :, :], loss[:, :, :], least[:, :].unsqueeze(2).to_broadcast(wide), ALU.is_gt)
            v.scalar_tensor_tensor(pick[:, :, :], pick[:, :, :], float(E), iota, ALU.mult, ALU.add)
            dve.drain()
            v.tensor_reduce(least[:, :], pick[:, :, :], AX.X, ALU.min)
            dve.drain()
            tt(pick[:, :, :], iota, least[:, :].unsqueeze(2).to_broadcast(wide), ALU.is_equal)
            for half in range(PAIR):
                rows = slice(half * H, (half + 1) * H)
                v.tensor_copy(scale[rows, :, :], pick[rows, :, half:E:PAIR].rearrange("p b m -> p m b"))
            dve.drain()
            tt(shift[:, :, :], scale[:, :, :], b_in[:, 1, :].unsqueeze(2).to_broadcast([P, M, BATCH]), ALU.mult)
            tt(loss[0:E, :, :], pick[0:E, :, :], c.ident[0:E, 0:E].unsqueeze(1).to_broadcast([E, BATCH, E]), ALU.mult)
            v.tensor_reduce(pick_rows[:, :], loss[0:E, :, :], AX.X, ALU.add)
            dve.drain()
            v.tensor_copy(pick_wide[:, :, :], pick_rows[:, :].unsqueeze(2).to_broadcast([E, BATCH, P]))
            dve.drain()
            dve.sem_inc(picked, 1)
            for t in range(TILES):
                dve.wait_ge(out_ready, t + 1)
                v.tensor_tensor(c.ACC[:, t, :], out_ps[t % 2][:, 0:DIM], b_base[:, :], ALU.add).then_inc(out_done, 1)
            dve.drain()


def state_space_kernel(nc, c, a, KA, KB, KC):
    N, J, S = 64, 128, 16
    CH = 16
    CHUNKS = J // CH
    TWO_PI = 2 * np.pi
    C1 = 6.28125
    C2 = float(np.float32(TWO_PI - C1) .view(np.int32).__and__(-4096).view(np.float32))
    C3 = float(TWO_PI - C1 - C2)
    LN2_HI = 0.693359375
    LN2_LO = float(np.log(2.0) - LN2_HI)
    with ExitStack() as ctx:
        sb, ps, sem = sub_memory(nc, ctx, "ss_")
        small = {n: sb(n, [P, J]) for n in ("are", "aim", "cre", "cim", "ldt", "dt", "theta", "rho", "er", "ei",
                                            "t0", "t1", "t2", "dcr", "dci", "cos0", "sin0")}
        bits = sb("bits", [P, J], I32)
        steps = sb("steps", [P, 2 * S])
        big = {n: sb(n, [P, J, S]) for n in ("qr", "qi", "w")}
        halves = [t[:, :, :].rearrange("p t d -> p (t d)")[:, h * J * S:(h + 1) * J * S]
                  for t in (c.XN, c.XT, c.ACC) for h in range(2)]
        for n, part in zip(("phase", "turns", "mag", "pr", "pi", "u"), halves):
            big[n] = part.rearrange("p (j s) -> p j s", s=S)
        slot = sb("slot", [P, 2, 4, CH, S])
        d_skip = sb("d_skip", [1, DIM])
        k_sb = sb("k_sb", [S, S, DIM])
        fwd = sb("fwd", [S, S, 2 * SEQ])
        k_ps = [[ps(f"k{u}{h}", [S, CH, S]) for h in range(2)] for u in range(2)]
        f_ps = [ps(f"f{i}", [P, DIM]) for i in range(4)]
        loaded, asked, answered = sem("loaded"), sem("asked"), sem("answered")
        slot_ready, k_ready, k_free = sem("slot_ready"), sem("k_ready"), sem("k_free")
        k_whole, f_ready, begun = sem("k_whole"), sem("f_ready"), sem("begun")
        block = ctx.enter_context(nc.Block())

        @block.sync
        def _(sp):
            for n, k in (("are", "A_re"), ("aim", "A_im"), ("cre", "C_re"), ("cim", "C_im")):
                sp.dma_start(small[n][:, :], a["S_" + k]).then_inc(loaded, 16)
            for h in range(2):
                sp.dma_start(small["ldt"][h * N:(h + 1) * N, :],
                             a["L0_xattn_log_dt"][h * J:(h + 1) * J].partition_broadcast(N)).then_inc(loaded, 16)
            sp.dma_start(steps[:, :], a["steps"]).then_inc(loaded, 16)
            sp.dma_start(d_skip[:, :], row(a["L0_xattn_D_skip"])).then_inc(loaded, 16)
            sp.dma_start(fwd[:, :, :], a["fwd"].rearrange("(a b) f -> b a f", b=S)).then_inc(loaded, 16)

        @block.vector
        def _(dve):
            v = nc.vector

            def tt(*args):
                v.tensor_tensor(*args)
                dve.drain()

            def ts(*args):
                v.tensor_scalar(*args)
                dve.drain()

            def stt(*args):
                v.scalar_tensor_tensor(*args)
                dve.drain()

            def ask(n, done):
                dve.sem_inc(asked, 1)
                dve.wait_ge(answered, done)

            def reduce_angle(x, k):
                ts(k, x, 1.0 / TWO_PI, MAGIC, ALU.mult, ALU.add)
                ts(k, k, MAGIC, None, ALU.subtract)
                for part in (C1, C2, C3):
                    stt(x, k, -part, x, ALU.mult, ALU.add)
                ts(x, x, 3.1415925, -3.1415925, ALU.min, ALU.max)

            m = {n: t[:, :] for n, t in small.items()}
            dve.wait_ge(loaded, 9 * 16)
            ts(m["t0"], m["ldt"], float(1 / np.log(2.0)), MAGIC, ALU.mult, ALU.add)
            ts(m["t0"], m["t0"], MAGIC, -126.0, ALU.subtract, ALU.max)
            stt(m["t1"], m["t0"], -LN2_HI, m["ldt"], ALU.mult, ALU.add)
            stt(m["t1"], m["t0"], -LN2_LO, m["t1"], ALU.mult, ALU.add)
            coefs = [1.0 / 5040, 1.0 / 720, 1.0 / 120, 1.0 / 24, 1.0 / 6, 0.5, 1.0]
            ts(m["t2"], m["t1"], coefs[0], None, ALU.mult)
            for co in coefs[1:]:
                stt(m["t2"], m["t2"], co, m["t1"], ALU.add, ALU.mult)
            ts(bits[:, :], m["t0"], 127.0, 8388608.0, ALU.add, ALU.mult)
            stt(m["dt"], m["t2"], 1.0, bits[:, :].bitcast(F32), ALU.add, ALU.mult)
            tt(m["theta"], m["dt"], m["aim"], ALU.mult)
            tt(m["rho"], m["dt"], m["are"], ALU.mult)
            v.tensor_copy(m["t0"], m["theta"])
            dve.drain()
            reduce_angle(m["t0"], m["t1"])
            ask(1, 3)
            tt(m["cos0"], m["cos0"], m["cos0"], ALU.mult)
            ts(m["t1"], m["t0"], -1.0, 1.0, ALU.mult, ALU.add)
            v.reciprocal(m["t1"], m["t1"])
            dve.drain()
            stt(m["t0"], m["t0"], 2.0, m["t1"], ALU.mult, ALU.mult)
            ts(m["t1"], m["cos0"], -2.0, None, ALU.mult)
            stt(m["er"], m["t1"], 1.0, m["t0"], ALU.add, ALU.mult)
            tt(m["er"], m["er"], m["t1"], ALU.add)
            stt(m["ei"], m["t0"], 1.0, m["sin0"], ALU.add, ALU.mult)
            tt(m["t0"], m["cre"], m["er"], ALU.mult)
            tt(m["t1"], m["cim"], m["ei"], ALU.mult)
            tt(m["t0"], m["t0"], m["t1"], ALU.subtract)
            tt(m["t1"], m["cre"], m["ei"], ALU.mult)
            tt(m["t2"], m["cim"], m["er"], ALU.mult)
            tt(m["t1"], m["t1"], m["t2"], ALU.add)
            tt(m["er"], m["are"], m["are"], ALU.mult)
            tt(m["ei"], m["aim"], m["aim"], ALU.mult)
            tt(m["er"], m["er"], m["ei"], ALU.add)
            v.reciprocal(m["er"], m["er"])
            dve.drain()
            for out, x, y, op in (("dcr", "t0", "t1", ALU.add), ("dci", "t1", "t0", ALU.subtract)):
                tt(m[out], m[x], m["are"], ALU.mult)
                tt(m["t2"], m[y], m["aim"], ALU.mult)
                tt(m[out], m[out], m["t2"], op)
                stt(m[out], m[out], 2.0, m["er"], ALU.mult, ALU.mult)
            b = {n: t[:, :, :] for n, t in big.items()}
            wide = [P, J, S]
            for f, re, im in ((0, "qr", "qi"), (1, "pr", "pi")):
                at = steps[:, f * S:(f + 1) * S].unsqueeze(1).to_broadcast(wide)
                tt(b["phase"], m["theta"].unsqueeze(2).to_broadcast(wide), at, ALU.mult)
                tt(b["mag"], m["rho"].unsqueeze(2).to_broadcast(wide), at, ALU.mult)
                reduce_angle(b["phase"], b["turns"])
                ask(2 + f, 6 + 3 * f)
                tt(b[re], b[re], b[re], ALU.mult)
                ts(b[re], b[re], -2.0, 1.0, ALU.mult, ALU.add)
                tt(b[re], b[re], b["mag"], ALU.mult)
                tt(b[im], b[im], b["mag"], ALU.mult)
            dcr, dci = (m[n].unsqueeze(2).to_broadcast(wide) for n in ("dcr", "dci"))
            tt(b["u"], b["pr"], dcr, ALU.mult)
            tt(b["w"], b["pi"], dci, ALU.mult)
            tt(b["u"], b["u"], b["w"], ALU.subtract)
            tt(b["pr"], b["pr"], dci, ALU.mult)
            tt(b["pi"], b["pi"], dcr, ALU.mult)
            stt(b["w"], b["pr"], -1.0, b["pi"], ALU.mult, ALU.subtract)
            with dve.Fori(0, CHUNKS // 2) as g:
                for u in range(2):
                    dve.wait_ge(k_ready, g * 2 + u + 1)
                    for n, x in enumerate(("qr", "qi", "u", "w")):
                        last = v.tensor_copy(slot[:, u, n, :, :], big[x][:, pieces(g * (2 * CH) + u * CH, CH), :])
                    last.then_inc(slot_ready, 1)
            dve.wait_ge(k_free, CHUNKS + 2)
            v.tensor_tensor(k_sb[0:1, 0, :], k_sb[0:1, 0, :], d_skip[:, :], ALU.add).then_inc(k_whole, 1)
            dve.wait_ge(f_ready, 4)
            for h in range(2):
                v.tensor_copy(KA[:, h, :], f_ps[h][:, :])
                v.tensor_copy(KC[:, h, :], f_ps[h][:, :])
                v.tensor_copy(KB[:, h, :], f_ps[2 + h][:, :])
            dve.drain()
            v.tensor_copy(KC[0:1, 0, :], f_ps[2][0:1, :])
            v.memset(KB[0:1, 0, :], 0.0)
            dve.drain()

        @block.scalar
        def _(act):
            act.sem_inc(k_free, 2)
            act.wait_ge(loaded, 9 * 16)
            act.wait_ge(asked, 1)
            s = {n: t[:, :] for n, t in small.items()}
            nc.scalar.activation(s["sin0"], s["t0"], ACT.Sin).then_inc(answered, 1)
            nc.scalar.activation(s["cos0"], s["t0"], ACT.Sin, scale=0.5).then_inc(answered, 1)
            act.wait_ge(answered, 2)
            nc.scalar.activation(s["t0"], s["rho"], ACT.Tanh, scale=0.5).then_inc(answered, 1)
            for f, re, im in ((0, "qr", "qi"), (1, "pr", "pi")):
                act.wait_ge(asked, 2 + f)
                nc.scalar.activation(big[im][:, :, :], big["phase"][:, :, :], ACT.Sin).then_inc(answered, 1)
                nc.scalar.activation(big[re][:, :, :], big["phase"][:, :, :], ACT.Sin, scale=0.5).then_inc(answered, 1)
                nc.scalar.activation(big["mag"][:, :, :], big["mag"][:, :, :], ACT.Exp).then_inc(answered, 1)
            with act.Fori(0, CHUNKS // 2) as g:
                for u in range(2):
                    act.wait_ge(k_ready, g * 2 + u + 3)
                    for h in range(2):
                        last = nc.scalar.activation(k_sb[:, :, pieces(g * (2 * CH) + (u * CH + h * J), CH)],
                                                    k_ps[u][h][:, :, :].rearrange("b j a -> b a j"), ACT.Copy)
                    last.then_inc(k_free, 1)

        @block.tensor
        def _(pe):
            pe.sem_inc(k_ready, 2)
            with pe.Fori(0, CHUNKS // 2) as g:
                for u in range(2):
                    pe.wait_ge(slot_ready, g * 2 + u + 1)
                    pe.wait_ge(k_free, g * 2 + u + 1)
                    pe.sem_inc(begun, 1)
                    for j in range(CH):
                        for h in range(2):
                            r = slice(h * N, (h + 1) * N)
                            nc.tensor.matmul(k_ps[u][h][:, j, :], slot[r, u, 0, j, :], slot[r, u, 2, j, :],
                                             start=True, stop=False)
                            last = nc.tensor.matmul(k_ps[u][h][:, j, :], slot[r, u, 1, j, :], slot[r, u, 3, j, :],
                                                    start=False, stop=True)
                    last.then_inc(k_ready, 1)
            pe.wait_ge(k_whole, 1)
            pe.wait_ge(loaded, 9 * 16)
            for f in range(4):
                for s in range(S):
                    last = nc.tensor.matmul(f_ps[f][:, :], fwd[:, s, f * P:(f + 1) * P], k_sb[:, s, :],
                                            start=s == 0, stop=s == S - 1)
                last.then_inc(f_ready, 1)


def film_attention(nc, c, a, X2, FO, table):
    HEADS, DH, TOP = 4, 32, 32
    SCALE = float(1.0 / np.sqrt(np.float32(DH)))
    with ExitStack() as ctx:
        sb, ps, sem = sub_memory(nc, ctx, "a0_")
        wq = sb("wq", [P, DK, P])
        wk = sb("wk", [CP, CK, P])
        wv = sb("wv", [CP, CK, DIM])
        wf = sb("wf", [P, 2, DK, 2 * DIM])
        bf = sb("bf", [P, 2, 2 * DIM])
        mod = sb("mod", [P, 1])
        context = sb("context", [CP, 2, CK, KEYS])
        mask8 = sb("mask8", [P, TILES], U8)
        share = sb("share", [P, TILES])
        key_mask8 = sb("key_mask8", [P, BATCH, KEYS], U8)
        key_fill = sb("key_fill", [P, BATCH, KEYS])
        q = sb("q", [P, SEQ])
        k_wide = sb("k_wide", [P, HEADS, KEYS])
        v = sb("v", [KEYS, 2, DIM])
        score = sb("score", [P, TPB, HEADS, KEYS])
        rest = sb("rest", [P, TPB, HEADS, KEYS])
        top = sb("top", [P, TPB, HEADS, 8])
        top_n = sb("top_n", [P, TPB, HEADS, 8])
        stat = sb("stat", [P, TPB, HEADS])
        mean = sb("mean", [P, TPB, KEYS])
        mean_t = sb("mean_t", [KEYS, SEQ])
        ct = sb("ct", [P, DK, SEQ])
        film = sb("film", [P, 2, 2 * DIM])
        Q = ps("q_ps", [P, SEQ])
        KV = ps("kv_ps", [P, 512])
        S = [ps(f"s{i}", [P, HEADS * KEYS]) for i in range(TPB)]
        T = ps("t", [KEYS, SEQ])
        CT = ps("ct_ps", [P, DK, SEQ])
        F = [ps(f"f{i}", [P, 2 * DIM]) for i in range(2)]
        w_loaded = sem("w_loaded")
        ctx_loaded = [sem(f"ctx_loaded{u}") for u in range(2)]
        setup_done = sem("setup_done")
        qkv_ready, q_done, kv_done = sem("qkv_ready"), sem("q_done"), sem("kv_done")
        scores_ready, scores_read = sem("scores_ready"), sem("scores_read")
        shifted, exp_done = sem("shifted"), sem("exp_done")
        mean_ready, turned, turned_done = sem("mean_ready"), sem("turned"), sem("turned_done")
        ct_ready, ct_done = sem("ct_ready"), sem("ct_done")
        film_ready, film_done = sem("film_ready"), sem("film_done")
        zero_ready, zero_stored = sem("zero_ready"), c.transfers["zeros"]
        block = ctx.enter_context(nc.Block())

        @block.gpsimd
        def _(pool):
            nc.gpsimd.memset(c.ACC[:, 0:8, :], 0.0).then_inc(zero_ready, 1)
            pool.wait_ge(zero_ready, 1)
            rows, step = table.shape[0], 8 * P
            for r in range(0, rows, step):
                n = min(step, rows - r) // P
                pool.dma_start(table[r:r + n * P, :].rearrange("(i p) d -> p i d", p=P), c.ACC[:, 0:n, :])\
                  .then_inc(zero_stored.sem, 16)
            pool.wait_ge(zero_stored.sem, zero_stored.expect(-(-rows // step)))
        LOADS = 16 * 10

        def batches(eng, body):
            with eng.Fori(0, BATCH // 2 - 1) as g:
                for u in range(2):
                    body(g * 2 + u, u, False)
            for b in range(BATCH - 2, BATCH):
                body(b, b % 2, b == BATCH - 1)

        @block.sync
        def _(sp):
            def load(b, u):
                sp.dma_start(context[:, u, :, :].unsqueeze(1),
                             a["context_T"][pieces(b), :, :].rearrange("b (k p) s -> p b k s", p=CP))\
                  .then_inc(ctx_loaded[u], 16)

            load(0, 0)
            load(1, 1)
            for dst, src, p in ((wq, "Wq", P), (wk, "Wk", CP), (wv, "Wv", CP)):
                sp.dma_start(dst[:, :, :], a["L0_xattn_" + src].rearrange("(k p) n -> p k n", p=p)).then_inc(w_loaded, 16)
            for n, way in enumerate(("in", "out")):
                sp.dma_start(wf[:, n, :, :], a["L0_xattn_W_film_" + way].rearrange("(k p) n -> p k n", p=P))\
                  .then_inc(w_loaded, 16)
                sp.dma_start(bf[:, n, :], spread(a["L0_xattn_b_film_" + way])).then_inc(w_loaded, 16)
            sp.dma_start(mod[:, :], spread(a["L0_xattn_mod_gate"])).then_inc(w_loaded, 16)
            sp.dma_start(mask8[:, :], a["mask_BxS_bf1"]).then_inc(w_loaded, 16)
            sp.dma_start(key_mask8[:, :, :], a["mask_BxS2_bf1"].partition_broadcast(P)).then_inc(w_loaded, 16)
            with sp.Fori(1, BATCH // 2) as g:
                for u in range(2):
                    sp.wait_ge(qkv_ready, g * 2 + (u - 1))
                    load(g * 2 + u, u)

        @block.tensor
        def _(pe):
            def project(b, u):
                pe.wait_ge(q_done, b + 1)
                pe.wait_ge(kv_done, b + 1)
                for kk in range(DK):
                    nc.tensor.matmul(Q[:, :], wq[:, kk, :], c.XT[:, kk, pieces(b * SEQ, SEQ)], start=kk == 0,
                                     stop=kk == DK - 1)
                pe.wait_ge(ctx_loaded[u], (b // 2 + 1) * 16 if isinstance(b, int) else b * 8 + (16 - 8 * u))
                for kk in range(CK):
                    nc.tensor.matmul(KV[:, 0:KEYS], wk[:, kk, :], context[:, u, kk, :], start=kk == 0,
                                     stop=kk == CK - 1)
                for kk in range(CK):
                    last = nc.tensor.matmul(KV[0:KEYS, DIM:2 * DIM], context[:, u, kk, :], wv[:, kk, :],
                                            start=kk == 0, stop=kk == CK - 1)
                last.then_inc(qkv_ready, 1)

            def body(b, u, final):
                pe.wait_ge(q_done, b + 2)
                pe.wait_ge(kv_done, b + 2)
                pe.wait_ge(scores_read, b + 1)
                for i in range(TPB):
                    last = nc.tensor.matmul(S[i][:, :], q[:, i * P:(i + 1) * P],
                                            k_wide[:, :, :].rearrange("p h s -> p (h s)"), start=True, stop=True)
                last.then_inc(scores_ready, 1)
                if not final:
                    project(b + 1, 1 - u)
                pe.wait_ge(mean_ready, b + 1)
                for i in range(TPB):
                    last = nc.tensor.transpose(T[:, i * P:(i + 1) * P], mean[:, i, :], c.ident[:, :])
                last.then_inc(turned, 1)
                pe.wait_ge(turned_done, b + 1)
                for m in range(DK):
                    last = nc.tensor.matmul(CT[:, m, :], v[:, u, m * P:(m + 1) * P], mean_t[:, :], start=True,
                                            stop=True)
                last.then_inc(ct_ready, 1)
                pe.wait_ge(ct_done, b + 1)
                for i in range(TPB):
                    for way in range(2):
                        pe.wait_ge(film_done, b * (2 * TPB) + (2 * i + way + 1))
                        for m in range(DK):
                            last = nc.tensor.matmul(F[way][:, :], ct[:, m, i * P:(i + 1) * P], wf[:, way, m, :],
                                                    start=m == 0, stop=m == DK - 1)
                        last.then_inc(film_ready, 1)

            pe.wait_ge(w_loaded, LOADS)
            project(0, 0)
            batches(pe, body)

        @block.scalar
        def _(act):
            act.sem_inc(q_done, 1)

            def evacuate(b, u):
                act.wait_ge(qkv_ready, b + 1)
                nc.scalar.activation(q[:, :], Q[:, :], ACT.Copy).then_inc(q_done, 1)

            def body(b, u, final):
                if not final:
                    act.wait_ge(scores_ready, b + 1)
                    evacuate(b + 1, 1 - u)
                act.wait_ge(shifted, b + 1)
                nc.scalar.activation(score[:, :, :, :], score[:, :, :, :], ACT.Exp).then_inc(exp_done, 1)
                act.wait_ge(turned, b + 1)
                nc.scalar.activation(mean_t[:, :], T[:, :], ACT.Copy).then_inc(turned_done, 1)
                act.wait_ge(ct_ready, b + 1)
                nc.scalar.activation(ct[:, :, :], CT[:, :, :], ACT.Copy).then_inc(ct_done, 1)

            evacuate(0, 0)
            batches(act, body)

        @block.vector
        def _(dve):
            vv = nc.vector
            dve.sem_inc(kv_done, 1)
            dve.sem_inc(scores_read, 1)
            dve.sem_inc(film_done, 2)
            dve.wait_ge(w_loaded, LOADS)
            vv.tensor_copy(share[:, :], mask8[:, :])
            vv.tensor_copy(key_fill[:, :, :], key_mask8[:, :, :])
            for way in range(2):
                vv.tensor_scalar(bf[:, way, :], bf[:, way, :], mod[:, 0:1], None, ALU.mult)
            dve.drain()
            vv.tensor_scalar(share[:, :], share[:, :], 1.0 / HEADS, None, ALU.mult)
            vv.tensor_scalar(key_fill[:, :, :], key_fill[:, :, :], 1.0, 1.0e30, ALU.subtract, ALU.mult)
            for way in range(2):
                vv.tensor_scalar(bf[:, way, 0:DIM], bf[:, way, 0:DIM], 1.0, None, ALU.add)
            dve.drain()

            def widen(b, u):
                wide = [P, HEADS, KEYS]
                dve.wait_ge(qkv_ready, b + 1)
                vv.tensor_tensor(k_wide[:, :, :], KV[:, 0:KEYS].unsqueeze(1).to_broadcast(wide),
                                 c.headmask[:, 0:HEADS].unsqueeze(2).to_broadcast(wide), ALU.mult)
                vv.tensor_copy(v[:, u, :], KV[0:KEYS, DIM:2 * DIM]).then_inc(kv_done, 1)

            def body(b, u, final):
                dve.wait_ge(scores_ready, b + 1)
                fill = key_fill[:, pieces(b), :].to_broadcast([P, HEADS, KEYS])
                for i in range(TPB):
                    last = vv.scalar_tensor_tensor(score[:, i, :, :], S[i][:, :].rearrange("p (h s) -> p h s", s=KEYS),
                                                   SCALE, fill, ALU.mult, ALU.add)
                last.then_inc(scores_read, 1)
                if not final:
                    widen(b + 1, 1 - u)
                dve.drain()
                for r in range(TOP // 8):
                    src, t8 = (score, top) if r == 0 else (rest, top_n)
                    for i in range(TPB):
                        for h in range(HEADS):
                            vv.max(t8[:, i, h, :], src[:, i, h, :])
                    dve.drain()
                    for i in range(TPB):
                        for h in range(HEADS):
                            vv.match_replace(rest[:, i, h, :], t8[:, i, h, :], src[:, i, h, :], NEG)
                    dve.drain()
                rows = [P, TPB * HEADS, KEYS]
                s3 = score[:, :, :, :].rearrange("p i h s -> p (i h) s")
                st = stat[:, :, :].rearrange("p i h -> p (i h)")
                vv.tensor_tensor(s3, s3, top[:, :, :, 0].rearrange("p i h -> p (i h)").unsqueeze(2).to_broadcast(rows),
                                 ALU.subtract).then_inc(shifted, 1)
                dve.wait_ge(exp_done, b + 1)
                flat = "p i h s -> p (i h s)"
                vv.scalar_tensor_tensor(score[:, :, :, :].rearrange(flat), rest[:, :, :, :].rearrange(flat), NEG,
                                        score[:, :, :, :].rearrange(flat), ALU.is_equal, ALU.mult)
                dve.drain()
                vv.tensor_reduce(st, s3, AX.X, ALU.add)
                dve.drain()
                vv.reciprocal(st, st)
                dve.drain()
                for i in range(TPB):
                    vv.tensor_scalar(stat[:, i, :], stat[:, i, :], share[:, pieces(b * TPB + i)], None, ALU.mult)
                dve.drain()
                vv.tensor_tensor(s3, s3, st.unsqueeze(2).to_broadcast(rows), ALU.mult)
                dve.drain()
                for i in range(TPB):
                    last = vv.tensor_reduce(mean[:, i, :], score[:, i, :, :].rearrange("p h s -> p s h"), AX.X, ALU.add)
                last.then_inc(mean_ready, 1)
                for i in range(TPB):
                    t = b * TPB + i
                    dve.wait_ge(film_ready, b * (2 * TPB) + (2 * i + 1))
                    vv.scalar_tensor_tensor(film[:, i, :], F[0][:, :], mod[:, 0:1], bf[:, 0, :], ALU.mult, ALU.add)\
                      .then_inc(film_done, 1)
                    dve.wait_ge(film_ready, b * (2 * TPB) + (2 * i + 2))
                    vv.scalar_tensor_tensor(FO[:, pieces(t), :].rearrange("p a n -> p (a n)"), F[1][:, :], mod[:, 0:1],
                                            bf[:, 1, :], ALU.mult, ALU.add).then_inc(film_done, 1)
                dve.drain()
                x = X2[:, pieces(b * TPB, TPB), :]
                vv.tensor_tensor(x, x, film[:, :, 0:DIM], ALU.mult)
                dve.drain()
                vv.tensor_tensor(x, x, film[:, :, DIM:2 * DIM], ALU.add)

            widen(0, 0)
            batches(dve, body)
            dve.drain()


def convolve(nc, c, a, X2, FO, KA, KB, KC):
    PAIRS = BATCH // 2
    TPP = 2 * TPB
    with ExitStack() as ctx:
        sb, ps, sem = sub_memory(nc, ctx, "cv_")
        fwd = sb("fwd", [P, TPB, 2 * SEQ])
        back = sb("back", [P, 4, SEQ])
        prod = sb("prod", [P, 2, 4, 2 * DIM])
        spec = sb("spec", [P, 2, 2, 2 * DIM])
        y = sb("y", [P, TPP, DIM])
        f_ps = [[ps(f"f{part}{h}", [P, 2, DIM]) for h in range(2)] for part in range(2)]
        y_ps = [ps(f"y{i}", [P, 2, DIM]) for i in range(TPB)]
        loaded, f_ready, f_done = sem("loaded"), sem("f_ready"), sem("f_done")
        prod_ready, spec_ready = sem("prod_ready"), sem("spec_ready")
        y_ready, y_done = sem("y_ready"), sem("y_done")
        block = ctx.enter_context(nc.Block())

        @block.sync
        def _(sp):
            sp.dma_start(fwd[:, :, :], a["fwd"].rearrange("(i p) f -> p i f", p=P)).then_inc(loaded, 16)
            sp.dma_start(back[:, :, :], a["back"].rearrange("(i p) l -> p i l", p=P)).then_inc(loaded, 16)

        @block.tensor
        def _(pe):
            pe.wait_ge(loaded, 32)
            with pe.Fori(0, PAIRS) as g:
                for h in range(2):
                    pe.wait_ge(f_done, g * 2 + h + 1)
                    for part in range(2):
                        for i in range(TPB):
                            col = part * SEQ + h * P
                            last = nc.tensor.matmul(f_ps[part][h][:, :, :], fwd[:, i, col:col + P],
                                                    X2[:, bass.ds(g * TPP + i, 2, TPB), :],
                                                    start=i == 0, stop=i == TPB - 1)
                    last.then_inc(f_ready, 1)
                pe.wait_ge(spec_ready, g * 2 + 2)
                for i in range(TPB):
                    pe.wait_ge(y_done, g * TPB + (i + 1))
                    for n in range(4):
                        last = nc.tensor.matmul(y_ps[i][:, :, :].rearrange("p b d -> p (b d)"),
                                                back[:, n, i * P:(i + 1) * P], spec[:, n // 2, n % 2, :],
                                                start=n == 0, stop=n == 3)
                    last.then_inc(y_ready, 1)

        @block.vector
        def _(dve):
            v = nc.vector
            dve.sem_inc(f_done, 2)
            dve.sem_inc(y_done, 2)
            with dve.Fori(0, PAIRS) as g:
                for h in range(2):
                    dve.wait_ge(f_ready, g * 2 + h + 1)
                    for n, (part, kern) in enumerate(((0, KA), (1, KB), (0, KB), (1, KC))):
                        last = v.tensor_tensor(prod[:, h, n, :].rearrange("p (b d) -> p b d", b=2), f_ps[part][h][:, :, :],
                                               kern[:, h, :].unsqueeze(1).to_broadcast([P, 2, DIM]), ALU.mult)
                    last.then_inc(f_done, 1)
                for i in range(TPB):
                    dve.wait_ge(y_ready, g * TPB + i + 1)
                    for b in range(2):
                        t = g * TPP + (b * TPB + i)
                        v.tensor_tensor(y[:, b * TPB + i, :].unsqueeze(1), y_ps[i][:, b, :].unsqueeze(1), FO[:, pieces(t), 0:DIM], ALU.mult)
                    dve.drain()
                    dve.sem_inc(y_done, 1)
                tiles = pieces(g * TPP, TPP)
                v.tensor_tensor(y[:, :, :], y[:, :, :], FO[:, tiles, DIM:2 * DIM], ALU.add)
                dve.drain()
                v.tensor_tensor(X2[:, tiles, :], y[:, :, :], c.XN[:, tiles, :], ALU.add)
            dve.drain()

        @block.gpsimd
        def _(pool):
            with pool.Fori(0, PAIRS) as g:
                for h in range(2):
                    pool.wait_ge(f_done, g * 2 + h + 3)
                    nc.gpsimd.tensor_tensor(spec[:, 0, h, :], prod[:, h, 0, :], prod[:, h, 1, :], ALU.subtract)
                    nc.gpsimd.tensor_tensor(spec[:, 1, h, :], prod[:, h, 2, :], prod[:, h, 3, :], ALU.add)\
                      .then_inc(spec_ready, 1)


def add_branch(nc, c, X2):
    with nc.Block() as block:
        @block.vector
        def _(dve):
            nc.vector.tensor_tensor(X2[:, :, :], X2[:, :, :], c.ACC[:, :, :], ALU.add)


def layer0_attention(nc, c, a, S):
    pre = "L0_xattn_"
    with ExitStack() as ctx:
        sb, ps, sem = sub_memory(nc, ctx, "l0i_")
        KA, KB, KC = (sb(f"kernel{n}", [P, 2, DIM]) for n in range(3))
        state_space_kernel(nc, c, a, KA, KB, KC)
        X2 = sb("x2", [P, TILES, DIM])
        normalise(nc, c, c.X, natural=c.XN)
        normalise(nc, c, c.XN, natural=X2, transposed=False, gain=a[pre + "g_norm_in"], shift=a[pre + "b_norm_in"])
        with ExitStack() as inner:
            FO = inner.enter_context(nc.sbuf_tensor("film_out", [P, TILES, 2 * DIM], F32))
            film_attention(nc, c, a, X2, FO, S.table)
            convolve(nc, c, a, X2, FO, KA, KB, KC)
        normalise(nc, c, X2, gain=a[pre + "g_ffn"], shift=a[pre + "b_ffn"])
        dense_layer(nc, c, "l0x", 1024, a[pre + "W1"], a[pre + "W2"], func=ACT.Gelu, up_bias=a["L0_b1"],
                    down_bias=a[pre + "b2"])
        add_branch(nc, c, X2)
        normalise(nc, c, X2, natural=c.ACC, transposed=False, gain=a[pre + "g_norm_out"],
                  shift=a[pre + "b_norm_out"])


def build(nc, a, out, stop=99, start=0):
    with ExitStack() as ctx:
        sb, ps, sem = sub_memory(nc, ctx)
        c = Core()
        c.transfers = {n: Transfers(nc, ctx, n) for n in ["zeros", "sent", "stored"] + [f"arrived{i}" for i in range(8)]}
        c.X = sb("residual", [P, TILES, DIM])
        c.XN = sb("normal", [P, TILES, DIM])
        c.XT = sb("normal_turned", [P, DK, TOKENS])
        c.ACC = sb("branch", [P, TILES, DIM])
        c.ident = sb("identity", [P, P])
        c.gate = sb("tanh_gates", [P, 8])
        c.headmask = sb("head_masks", [P, 16])
        c.above = sb("above", [P, P])
        c.ones = sb("ones", [P, P])
        c.iota = sb("iota", [P, 40])
        c.chosen = sb("chosen", [P, 16, KT])
        c.share = sb("choice_share", [P, KT])
        S = Core()
        S.slot = sb("choice_slot", [P, KT], U32)
        S.owner = sb("tile_owner", [P, 32], I32)
        rows = slot_tiles(16) * SLOT_TILE
        S.table = nc.dram_tensor("slot_tokens", (rows, DIM), F32, kind="Internal").ap()
        S.results = nc.dram_tensor("slot_results", (rows, DIM), F32, kind="Internal").ap()
        load_inputs(nc, c, a)
        c.last = None
        if start <= 0 and stop >= 0:
            layer0_attention(nc, c, a, S)
            c.last = 0
        if start <= 1 and stop >= 1:
            normalise(nc, c, c.X, natural=c.XN, transposed=False, add=c.last)
            hash_router(nc, c)
            plan_slots(nc, c, 8, S)
            send_block(nc, c, S)
            routed_experts(nc, c, "l0", 8, 1024, S, a["L0_ffn_W1"], a["L0_ffn_W2"], up_bias=a["L0_ffn_b1"],
                           down_bias=a["L0_ffn_b2"])
            collect(nc, c, 8, S, fresh=True)
            c.last = 4
        if start <= 2 and stop >= 2:
            normalise(nc, c, c.X, add=c.last)
            layer1_attention(nc, c, a)
            c.last = 1
        if start <= 3 and stop >= 3:
            normalise(nc, c, c.X, natural=c.XN, add=c.last)
            softmax_router(nc, c, "l1_router", a["L1_gate_T"], 8, eps=1e-5, gain=a["L1_gain"], shift=a["L1_shift"])
            plan_slots(nc, c, 8, S)
            dense_layer(nc, c, "l1s", 512, a["L1_ffn_sWu"], a["L1_ffn_sWd"], gate=a["L1_ffn_sWg"], send=S)
            routed_experts(nc, c, "l1", 8, 512, S, a["L1_ffn_Wu"], a["L1_ffn_Wd"], gate=a["L1_ffn_Wg"])
            collect(nc, c, 8, S, fresh=False)
            c.last = 5
        if start <= 4 and stop >= 4:
            normalise(nc, c, c.X, add=c.last)
            narrow_attention(nc, c, a, 2)
            c.last = 2
        if start <= 5 and stop >= 5:
            normalise(nc, c, c.X, add=c.last)
            adapter_layer(nc, c, a)
            c.last = 6
        if start <= 6 and stop >= 6:
            normalise(nc, c, c.X, add=c.last)
            narrow_attention(nc, c, a, 3)
            c.last = 3
        if start <= 7 and stop >= 7:
            normalise(nc, c, c.X, natural=c.XN, add=c.last)
            softmax_router(nc, c, "l3_router", a["L3_ffn_Wr"], 16)
            plan_slots(nc, c, 16, S)
            dense_layer(nc, c, "l3s", 256, a["L3_ffn_Su"], a["L3_ffn_Sd"], gate=a["L3_ffn_Sg"], send=S)
            routed_experts(nc, c, "l3", 16, 128, S, a["L3_ffn_Wu"], a["L3_ffn_Wd"], gate=a["L3_ffn_Wg"])
            collect(nc, c, 16, S, fresh=False)
            c.last = 7
        store_output(nc, c, out)


def constants():
    ident = np.eye(P, dtype=np.float32)
    p = np.arange(P)
    headmask = np.zeros((P, 16), np.float32)
    for h in range(4):
        headmask[:, h] = p // 32 == h
    for h in range(8):
        headmask[:, 4 + h] = p // 16 == h
    iota = np.tile(np.concatenate([np.arange(32), (np.arange(8) - 1) % 8]).astype(np.float32), (P, 1))
    above = np.triu(np.ones((P, P), np.float32), 1)
    ones = np.ones((P, P), np.float32)
    N = 2 * SEQ
    l = np.arange(SEQ)[:, None]
    k = np.arange(SEQ)[None, :]
    turn = 2 * np.pi * ((l * k) % N) / N
    re, im = np.cos(turn), -np.sin(turn)
    im[:, 0] = (-1.0) ** np.arange(SEQ)
    fwd = np.concatenate([re, im], 1)
    scale = np.full(SEQ, 2.0 / N)
    scale[0] = 1.0 / N
    back = np.concatenate([re * scale, im * scale], 1).T
    fwd, back = fwd.astype(np.float32), np.ascontiguousarray(back.astype(np.float32))
    steps = np.tile(np.concatenate([np.arange(16), 16 * np.arange(16)]).astype(np.float32), (P, 1))
    return {"ident": ident, "headmask": headmask, "iota": iota, "above": above, "ones": ones, "fwd": fwd, "back": back, "steps": steps}


def layout(inputs):
    a = {k: np.asarray(v) for k, v in inputs.items()}
    d = {k: np.ascontiguousarray(v) for k, v in a.items()}
    d["L0_xattn_mod_gate"] = d["L0_xattn_mod_gate"].reshape(1)
    d["context_T"] = np.ascontiguousarray(a["ctx_768"].transpose(0, 2, 1))
    d["L1_gate_T"] = np.ascontiguousarray(a["L1_ffn_gate_w"].T)
    d["L1_gain"] = np.ascontiguousarray(a["L1_ffn_ln_scale"].reshape(DK, P).T)
    d["L1_shift"] = np.ascontiguousarray(a["L1_ffn_ln_bias"].reshape(DK, P).T)
    for k in ("L1_ffn_ln_scale", "L1_ffn_ln_bias"):
        del d[k]
    d["L0_ffn_b1"] = np.ascontiguousarray(a["L0_ffn_b1"].reshape(8, 8, P).transpose(0, 2, 1))
    d["L0_b1"] = np.ascontiguousarray(a["L0_xattn_b1"].reshape(8, P).T)
    del d["L0_xattn_b1"]
    for n in ("bq", "bk"):
        d["L2_" + n] = np.ascontiguousarray(a["L2_xattn_" + n].reshape(DK, P).T)
        del d["L2_xattn_" + n]
    for n in ("bd1", "ba_down"):
        d["L2_" + n] = np.ascontiguousarray(a["L2_ffn_" + n].reshape(4, P).T)
        del d["L2_ffn_" + n]
    d["L2_bd2"] = np.ascontiguousarray(a["L2_ffn_bd2"].reshape(8, DK, P).transpose(2, 0, 1))
    del d["L2_ffn_bd2"]
    d["mask_BxS_bk0"] = np.ascontiguousarray(d["mask_BxS_bk0"].reshape(TILES, P).T)
    d["mask_BxS_bf1"] = np.ascontiguousarray(d["mask_BxS_bf1"].reshape(TILES, P).T)
    d["L3_Wq_T"] = np.ascontiguousarray(a["L3_xattn_Wq"].T)
    d["L3_Wkv_T"] = np.ascontiguousarray(a["L3_xattn_Wkv"].T)
    for k in ("A_re", "A_im", "C_re", "C_im"):
        v = a["L0_xattn_" + k]
        d["S_" + k] = np.ascontiguousarray(v.reshape(2, 128, 64).transpose(0, 2, 1).reshape(128, 128))
        del d["L0_xattn_" + k]
    for k in ("ctx_768", "L1_ffn_gate_w", "L3_xattn_Wq", "L3_xattn_Wkv"):
        del d[k]
    d.update(constants())
    return d


def kernel(**inputs):
    import concourse.bacc as bacc
    from concourse.bass_utils import run_bass_kernel_spmd

    nc = bacc.Bacc("TRN2", target_bir_lowering=False, num_devices=1)
    arrays = layout(inputs)
    args = {k: nc.dram_tensor("in_" + k, v.shape, mybir.dt.from_np(v.dtype), kind="ExternalInput").ap()
            for k, v in arrays.items()}
    out = nc.dram_tensor("out_0", (BATCH, SEQ, DIM), F32, kind="ExternalOutput").ap()
    build(nc, args, out)
    r = run_bass_kernel_spmd(nc, [{"in_" + k: v for k, v in arrays.items()}], core_ids=[0])
    return r.results[0]["out_0"]
```

```python
from contextlib import ExitStack

import numpy as np

import concourse.bass as bass
from concourse import mybir

F32 = mybir.dt.float32
I32 = mybir.dt.int32
U32 = mybir.dt.uint32
U8 = mybir.dt.uint8
ACT = mybir.ActivationFunctionType
ALU = mybir.AluOpType
AX = mybir.AxisListType

P = 128
BATCH, SEQ, DIM = 8, 256, 256
KEYS, CTX = 77, 192
CP = 96
CK = CTX // CP
DK = DIM // P
TILES = BATCH * SEQ // P
TOKENS = BATCH * SEQ
TPB = SEQ // P
EPS = 1e-5
BLOCK = 512
BLOCKS = TOKENS // BLOCK
TPK = BLOCK // P
MAGIC = 12582912.0
NEG = -3.0e38


def pieces(i, n=1):
    return bass.ds(i, n)


class Core:

    stages = 0

    def count(self):
        self.stages += 1
        return self.stages


class Transfers:

    def __init__(self, nc, ctx, name):
        self.sem = ctx.enter_context(nc.semaphore("transfers_" + name))
        self.count = 0

    def expect(self, n):
        self.count += 16 * n
        return self.count


def sub_memory(nc, ctx, prefix=""):
    def sb(name, shape, dt=F32):
        return ctx.enter_context(nc.sbuf_tensor(prefix + name, shape, dt))

    def ps(name, shape, dt=F32):
        return ctx.enter_context(nc.psum_tensor(prefix + name, shape, dt))

    def sem(name):
        handle = ctx.enter_context(nc.semaphore(prefix + name))
        ctx.callback(nc.sync.sem_clear, handle)
        return handle

    return sb, ps, sem


def row(ap):
    return ap.rearrange("(a n) -> a n", a=1)


def spread(ap):
    return ap.partition_broadcast(P)


def load_inputs(c, a, sp, gates, loaded):
    sp.dma_start(c.X[:, :, :], a["x"].rearrange("b (i p) d -> p (b i) d", p=P)).then_inc(loaded, 16)
    sp.dma_start(gates[:, 0:4], spread(a["g_xattn"])).then_inc(loaded, 16)
    sp.dma_start(gates[:, 4:8], spread(a["g_ffn"])).then_inc(loaded, 16)
    for name, tile in (("ident", c.ident), ("headmask", c.headmask), ("iota", c.iota), ("above", c.above),
                       ("ones", c.ones)):
        sp.dma_start(tile[:, :], a[name]).then_inc(loaded, 16)


def row_statistics(nc, dve, source, stats):
    with dve.Fori(0, TILES // 4) as g:
        for i in range(4):
            t = g * 4 + i
            nc.vector.bn_stats(stats[:, pieces(t), :].rearrange("p a s -> p (a s)"),
                               source[:, pieces(t), :].rearrange("p a s -> p (a s)"))
    dve.drain()


def mean_and_variance(nc, dve, stats, mean, diff, var, var_ready):
    v = nc.vector
    v.tensor_tensor(mean[:, :], stats[:, :, 1], stats[:, :, 4], ALU.add)
    v.tensor_tensor(diff[:, :], stats[:, :, 1], stats[:, :, 4], ALU.subtract)
    v.tensor_tensor(var[:, :], stats[:, :, 2], stats[:, :, 5], ALU.add)
    dve.drain()
    v.tensor_scalar(mean[:, :], mean[:, :], 0.5, None, ALU.mult)
    v.tensor_tensor(diff[:, :], diff[:, :], diff[:, :], ALU.mult)
    v.tensor_scalar(var[:, :], var[:, :], 1.0 / DIM, EPS, ALU.mult, ALU.add)
    dve.drain()
    v.scalar_tensor_tensor(var[:, :], diff[:, :], 0.25, var[:, :], ALU.mult, ALU.add).then_inc(var_ready, 1)


def reciprocal_root(nc, dve, var, dev, rstd):
    v = nc.vector
    v.reciprocal(rstd[:, :], dev[:, :])
    dve.drain()
    v.tensor_tensor(dev[:, :], rstd[:, :], rstd[:, :], ALU.mult)
    dve.drain()
    v.tensor_tensor(dev[:, :], dev[:, :], var[:, :], ALU.mult)
    dve.drain()
    v.tensor_scalar(dev[:, :], dev[:, :], -0.5, 1.5, ALU.mult, ALU.add)
    dve.drain()
    v.tensor_tensor(rstd[:, :], rstd[:, :], dev[:, :], ALU.mult)
    dve.drain()


def add_to_residual(nc, c, dve, value, tiles, gate, final=None):
    v = nc.vector
    n = len(tiles)
    x = c.X[:, pieces(tiles[0], n), :]
    dve.drain()
    last = v.scalar_tensor_tensor(x, value, c.gate[:, gate:gate + 1], x, ALU.mult, ALU.add)
    if final is not None:
        last.then_inc(final, 1)
        return
    dve.drain()
    for t in tiles:
        v.bn_stats(c.stats[:, pieces(t), :].rearrange("p a s -> p (a s)"),
                   c.X[:, pieces(t), :].rearrange("p a s -> p (a s)"))


def normalise(nc, c, source=None, natural=None, transposed=True, gain=None, shift=None, residual=None,
              stats=None):
    with ExitStack() as ctx:
        n = Normalisation(nc, c, ctx, source, natural, transposed, gain, shift, residual, stats)
        block = ctx.enter_context(nc.Block())

        if gain is not None:
            @block.sync
            def _(sp):
                n.load(sp)

        @block.vector
        def _(dve):
            n.statistics(dve)
            n.apply(dve)

        if n.copied:
            @block.gpsimd
            def _(pool):
                n.copy_first_tiles(pool)

        if transposed:
            @block.tensor
            def _(pe):
                n.turn(pe)

        @block.scalar
        def _(act):
            n.root(act)
            n.copy(act)


class Normalisation:

    def __init__(self, nc, c, ctx, source=None, natural=None, transposed=True, gain=None, shift=None, residual=None,
                 stats=None, turned=None):
        sb, ps, sem = sub_memory(nc, ctx, f"n{c.count()}_")
        self.nc, self.c, self.source, self.natural, self.transposed = nc, c, source, natural, transposed
        self.gain, self.shift, self.residual = gain, shift, residual
        self.x = c.X if source is None else source
        self.to_count = source is not None and stats is None
        self.stats = c.stats if source is None else sb("ln_stats", [P, TILES, 6]) if stats is None else stats
        self.mean, self.diff, self.var, self.dev, self.rstd = (
            sb("ln_" + n, [P, TILES]) for n in ("mean", "diff", "var", "dev", "rstd"))
        self.scratch = sb("ln_scratch", [P, 2, TPB, DIM])
        if gain is not None:
            self.affine = sb("ln_affine", [P, 2, DIM])
            self.affine_loaded = sem("ln_affine_loaded")
        if transposed:
            self.turned = [ps(f"ln_turned{u}", [P, DK, SEQ]) for u in range(2)] if turned is None else \
                [bank.rearrange("p (k s) -> p k s", k=DK) for bank in turned]
            self.scratch_turned, self.turned_free = sem("ln_scratch_turned"), sem("ln_turned_free")
        self.var_ready, self.dev_ready = sem("ln_var_ready"), sem("ln_dev_ready")
        self.scratch_ready = sem("ln_scratch_ready")
        self.direct = natural is not None and not transposed
        self.copied = [sem(f"ln_scratch_copied{i}") for i in range(2)] if natural is not None and transposed else []

    def load(self, sp):
        for k, src in enumerate((self.gain, self.shift)):
            sp.dma_start(self.affine[:, k, :], spread(src)).then_inc(self.affine_loaded, 16)

    def wait_natural(self, eng):
        for one in self.copied:
            eng.wait_ge(one, BATCH + 2)

    def wait_turned(self, pe):
        pe.wait_ge(self.turned_free, BATCH + 2)

    def statistics(self, dve):
        if self.to_count:
            row_statistics(self.nc, dve, self.source, self.stats)
        mean_and_variance(self.nc, dve, self.stats, self.mean, self.diff, self.var, self.var_ready)

    def root(self, act):
        act.wait_ge(self.var_ready, 1)
        self.nc.scalar.activation(self.dev[:, :], self.var[:, :], ACT.Sqrt).then_inc(self.dev_ready, 1)

    def apply(self, dve):
        v, scratch = self.nc.vector, self.scratch
        dve.wait_ge(self.dev_ready, 1)
        reciprocal_root(self.nc, dve, self.var, self.dev, self.rstd)
        if self.transposed:
            dve.sem_inc(self.scratch_turned, 2)
        for one in self.copied:
            dve.sem_inc(one, 2)
        if self.gain is not None:
            dve.wait_ge(self.affine_loaded, 32)
        with dve.Fori(0, BATCH // 2) as g:
            for u in range(2):
                if self.transposed:
                    dve.wait_ge(self.scratch_turned, g * 2 + u + 1)
                for one in self.copied:
                    dve.wait_ge(one, g * 2 + u + 1)
                tiles = [g * 4 + (2 * u + i) for i in range(TPB)]
                target = self.natural[:, pieces(tiles[0], TPB), :] if self.direct else scratch[:, u, :, :]
                for i, t in enumerate(tiles):
                    row = self.natural[:, pieces(t), :] if self.direct else scratch[:, u, i:i + 1, :]
                    last = v.tensor_scalar(row, self.x[:, pieces(t), :],
                                           self.mean[:, pieces(t)], self.rstd[:, pieces(t)], ALU.subtract, ALU.mult)
                if self.gain is not None:
                    for k, op in ((0, ALU.mult), (1, ALU.add)):
                        dve.drain()
                        last = v.tensor_tensor(target, target,
                                               self.affine[:, k, :].unsqueeze(1).to_broadcast([P, TPB, DIM]), op)
                if not self.direct:
                    last.then_inc(self.scratch_ready, 1)
                if self.residual is not None:
                    add_to_residual(self.nc, self.c, dve, scratch[:, u, :, :], tiles, self.residual)
        dve.drain()

    def copy_first_tiles(self, pool):
        with pool.Fori(0, BATCH // 2) as g:
            self.copy_first_pair(pool, g)

    def copy_first_pair(self, pool, g):
        for u in range(2):
            pool.wait_ge(self.scratch_ready, g * 2 + u + 1)
            self.nc.gpsimd.tensor_copy(self.natural[:, pieces(g * 4 + 2 * u), :],
                                       self.scratch[:, u, 0:1, :]).then_inc(self.copied[0], 1)

    def turn(self, pe):
        with pe.Fori(0, BATCH // 2) as g:
            self.turn_pair(pe, g)

    def turn_pair(self, pe, g):
        for u in range(2):
            pe.wait_ge(self.scratch_ready, g * 2 + u + 1)
            pe.wait_ge(self.turned_free, g * 2 + u + 1)
            for i in range(TPB):
                for k in range(DK):
                    last = self.nc.tensor.transpose(self.turned[u][:, k, i * P:(i + 1) * P],
                                                    self.scratch[:, u, i, k * P:(k + 1) * P], self.c.ident[:, :])
            last.then_inc(self.scratch_turned, 1)

    def copy(self, act):
        if not self.transposed:
            return
        act.sem_inc(self.turned_free, 2)
        with act.Fori(0, BATCH // 2) as g:
            self.copy_pair(act, g)

    def copy_pair(self, act, g):
        for u in range(2):
            if self.copied:
                act.wait_ge(self.scratch_ready, g * 2 + u + 1)
                self.nc.scalar.activation(self.natural[:, pieces(g * 4 + (2 * u + 1)), :],
                                          self.scratch[:, u, 1:2, :], ACT.Copy).then_inc(self.copied[1], 1)
            if self.transposed:
                act.wait_ge(self.scratch_turned, g * 2 + u + 3)
                self.nc.scalar.activation(self.c.XT[:, :, pieces(g * 2 * SEQ + u * SEQ, SEQ)],
                                          self.turned[u][:, :, :], ACT.Copy).then_inc(self.turned_free, 1)


def dense_layer(nc, c, name, width, up, down, gate=None, func=ACT.Silu, up_bias=None, down_bias=None,
                blocks=range(BLOCKS), send=None, collected=None,
                into=None, stats=None, out=None, normalised=None):
    NF = width // P
    NB = len(blocks)
    gated = gate is not None
    ring = 2 if gated else 4
    with ExitStack() as ctx:
        sb, ps, sem = sub_memory(nc, ctx, f"{name}{c.count()}_")
        w_up = sb("w_up", [P, DK, width])
        w_gate = sb("w_gate", [P, DK, width]) if gated else None
        w_down = sb("w_down", [P, NF, DIM])
        hidden = sb("hidden", [P, 2, NF, BLOCK])
        b_down = sb("b_down", [P, DIM]) if down_bias is not None else None
        b_up = sb("b_up", [P, NF]) if up_bias is not None else None
        silu = sb("silu", [P, 2, BLOCK]) if gated else None
        up_ps = [ps(f"up{i}", [P, BLOCK]) for i in range(ring)]
        gate_ps = [ps(f"gate{i}", [P, BLOCK]) for i in range(ring)] if gated else None
        out_ps = [ps(f"out{i}", [P, BLOCK]) for i in range(2)]
        norm = Normalisation(nc, c, ctx, **normalised) if normalised is not None else None
        up_loaded, down_loaded = sem("up_loaded"), sem("down_loaded")
        up_ready, gate_done = sem("up_ready"), sem("gate_done")
        hidden_done = sem("hidden_done")
        out_ready, out_free = sem("out_ready"), sem("out_free")
        sent = c.transfers["sent"]
        group_final, stored = sem("group_final"), sem("stored")
        results = Collection(nc, c, ctx, *collected, fresh=False) if collected is not None else None
        block = ctx.enter_context(nc.Block())
        up_loads, down_loads = 32 if gated or up_bias is not None else 16, 16 if down_bias is None else 32

        @block.sync
        def _(sp):
            if norm is not None:
                norm.load(sp)
            for w, src in ((w_up, up), (w_gate, gate)):
                if src is not None:
                    sp.dma_start(w[:, :, :], src.rearrange("(k p) n -> p k n", p=P)).then_inc(up_loaded, 16)
            if up_bias is not None:
                sp.dma_start(b_up[:, :], up_bias).then_inc(up_loaded, 16)
            sp.dma_start(w_down[:, :, :], down.rearrange("(k p) n -> p k n", p=P)).then_inc(down_loaded, 16)
            if down_bias is not None:
                sp.dma_start(b_down[:, :], spread(down_bias)).then_inc(down_loaded, 16)
            if out is not None:
                n = Collection.TPG
                for m in range(Collection.GROUPS):
                    sp.wait_ge(group_final, m + 1)
                    sp.dma_start(out.rearrange("b (i p) d -> p (b i) d", p=P)[:, m * n:(m + 1) * n, :],
                                 c.X[:, m * n:(m + 1) * n, :]).then_inc(stored, 16)
                sp.wait_ge(stored, Collection.GROUPS * 16)

        if send is not None:
            @block.gpsimd
            def _(pool):
                send_tokens(nc, c, send, pool, sent)

        if results is not None:
            @block.gpsimd
            def _(pool):
                for n in range(results.GROUPS):
                    results.gather(n)

        @block.tensor
        def _(pe):
            def up_block(n, k):
                for f in range(NF):
                    pe.wait_ge(hidden_done, n * NF + f + 1)
                    slot = (n * NF + f) % ring
                    for wt, tile in ((w_up, up_ps), (w_gate, gate_ps)):
                        if wt is not None:
                            for kk in range(DK):
                                last = nc.tensor.matmul(tile[slot][:, :], wt[:, kk, f * P:(f + 1) * P],
                                                        c.XT[:, kk, k * BLOCK:(k + 1) * BLOCK],
                                                        start=kk == 0, stop=kk == DK - 1)
                    last.then_inc(up_ready, 1)

            def down_block(n):
                pe.wait_ge(hidden_done, (n + 1) * NF + ring)
                for i in range(TPK):
                    pe.wait_ge(out_free, n * TPK + i + 1)
                    for f in range(NF):
                        last = nc.tensor.matmul(out_ps[i % 2][:, 0:DIM], hidden[:, n % 2, f, i * P:(i + 1) * P],
                                                w_down[:, f, :], start=f == 0, stop=f == NF - 1)
                    last.then_inc(out_ready, 1)

            for n, k in enumerate(blocks):
                if norm is not None:
                    if n == 0:
                        norm.turn_pair(pe, 0)
                    pe.wait_ge(norm.turned_free, 2 * n + 4)
                if n == 0:
                    pe.wait_ge(up_loaded, up_loads)
                up_block(n, k)
                if norm is not None and n + 1 < NB:
                    norm.turn_pair(pe, n + 1)
                if n == 0:
                    pe.wait_ge(down_loaded, down_loads)
                else:
                    down_block(n - 1)
            down_block(NB - 1)

        @block.scalar
        def _(act):
            if not gated:
                act.sem_inc(hidden_done, ring)
            if norm is not None:
                norm.root(act)
                act.sem_inc(norm.turned_free, 2)
            for n in range(NB):
                if norm is not None:
                    norm.copy_pair(act, n)
                if n == 0 and up_bias is not None:
                    act.wait_ge(up_loaded, up_loads)
                if not gated and n >= 2:
                    act.wait_ge(out_ready, TPK * (n - 1))
                for f in range(NF):
                    slot = (n * NF + f) % ring
                    act.wait_ge(up_ready, n * NF + f + 1)
                    if gated:
                        nc.scalar.activation(silu[:, slot, :], gate_ps[slot][:, :], func).then_inc(gate_done, 1)
                    else:
                        nc.scalar.activation(hidden[:, n % 2, f, :], up_ps[slot][:, :], func,
                                             bias=b_up[:, f:f + 1]).then_inc(hidden_done, 1)

        @block.vector
        def _(dve):
            v = nc.vector
            if norm is not None:
                norm.statistics(dve)
                norm.apply(dve)
            if gated:
                dve.sem_inc(hidden_done, ring)
            dve.sem_inc(out_free, 2)
            if down_bias is not None:
                dve.wait_ge(down_loaded, down_loads)

            def hidden_block(n):
                if n >= 2:
                    dve.wait_ge(out_ready, TPK * (n - 1))
                for f in range(NF):
                    slot = (n * NF + f) % ring
                    dve.wait_ge(gate_done, n * NF + f + 1)
                    v.tensor_tensor(hidden[:, n % 2, f, :], up_ps[slot][:, :], silu[:, slot, :], ALU.mult)\
                     .then_inc(hidden_done, 1)

            def out_block(n, k):
                for i in range(TPK):
                    dve.wait_ge(out_ready, n * TPK + i + 1)
                    acc, value = c.ACC[:, k * TPK + i, :], out_ps[i % 2][:, 0:DIM]
                    if down_bias is not None:
                        v.tensor_tensor(acc, value, b_down[:, :], ALU.add).then_inc(out_free, 1)
                    else:
                        v.tensor_copy(acc, value).then_inc(out_free, 1)
                    if into is not None:
                        t = k * TPK + i
                        dve.drain()
                        v.tensor_tensor(into[:, t, :], into[:, t, :], acc, ALU.add)
                        dve.drain()
                        v.bn_stats(stats[:, t, :], into[:, t, :])

            per_block = TPK * Collection.GROUPS // TILES

            def combine(groups):
                for m in groups:
                    results.combine(dve, m, group_final if out is not None else None)

            for n, k in enumerate(blocks):
                if gated:
                    hidden_block(n)
                if n:
                    out_block(n - 1, k - 1)
                if results is not None and n < 2:
                    combine(range(2) if n == 0 else range(2, k * per_block))
            out_block(NB - 1, blocks[-1])
            if results is not None:
                combine(range(blocks[-1] * per_block, Collection.GROUPS))
            dve.drain()


CHOICES = 2
KT = CHOICES * TILES
SLOT_TILE = 256
SPT = SLOT_TILE // P


def slot_tiles(E):
    return CHOICES * TOKENS // SLOT_TILE + E - 1


def plan_slots(nc, c, E, S):
    NT = slot_tiles(E)
    with ExitStack() as ctx:
        sb, ps, sem = sub_memory(nc, ctx, f"plan{c.count()}_")
        chosen = c.chosen[:, 0:E, :]
        running = [sb(f"running{u}", [P, E, KT]) for u in range(2)]
        before = sb("before", [P, E, KT])
        count = sb("count", [P, E])
        tiles = sb("tiles", [P, E])
        end = [sb(f"end{u}", [P, E]) for u in range(2)]
        first = sb("first", [P, E])
        past = sb("past", [P, NT, E])
        owner = sb("owner_value", [P, NT])
        where = sb("where", [P, KT])
        rank_ps = ps("rank", [P, E, KT])
        count_ps = ps("count_ps", [P, E])
        summed, ranked = sem("summed"), sem("ranked")
        block = ctx.enter_context(nc.Block())

        @block.vector
        def _(dve):
            v = nc.vector

            def running_sum(x, y, n):
                step = 1
                while step < n:
                    v.tensor_copy(y[..., 0:step], x[..., 0:step])
                    v.tensor_tensor(y[..., step:n], x[..., step:n], x[..., 0:n - step], ALU.add)
                    dve.drain()
                    x, y = y, x
                    step *= 2
                return x

            v.tensor_copy(running[0][:, :, :], chosen)
            dve.drain()
            total = running_sum(running[0][:, :, :], running[1][:, :, :], KT)
            v.tensor_tensor(before[:, :, :], total, chosen, ALU.subtract)
            v.tensor_copy(count[:, :], total[:, :, KT - 1]).then_inc(summed, 1)
            dve.wait_ge(ranked, 1)
            v.tensor_scalar(tiles[:, :], count_ps[:, :], 1.0 / SLOT_TILE, 0.498, ALU.mult, ALU.add)
            dve.drain()
            v.tensor_scalar(tiles[:, :], tiles[:, :], MAGIC, None, ALU.add)
            dve.drain()
            v.tensor_scalar(tiles[:, :], tiles[:, :], MAGIC, None, ALU.subtract)
            dve.drain()
            v.tensor_copy(end[0][:, :], tiles[:, :])
            dve.drain()
            last = running_sum(end[0][:, :], end[1][:, :], E)
            v.tensor_tensor(first[:, :], last, tiles[:, :], ALU.subtract)
            iota = c.iota[:, 0:NT].unsqueeze(2).to_broadcast([P, NT, E])
            v.tensor_tensor(past[:, :, :], iota, last.unsqueeze(1).to_broadcast([P, NT, E]), ALU.is_ge)
            dve.drain()
            v.tensor_scalar(first[:, :], first[:, :], float(SLOT_TILE), None, ALU.mult)
            v.tensor_reduce(owner[:, :], past[:, :, :], AX.X, ALU.add)
            dve.drain()
            v.tensor_scalar(owner[:, :], owner[:, :], float(E - 1), None, ALU.min)
            v.tensor_tensor(before[:, :, :], rank_ps[:, :, :], first[:, :].unsqueeze(2).to_broadcast([P, E, KT]),
                            ALU.add)
            dve.drain()
            v.tensor_copy(S.owner[:, 0:NT], owner[:, :])
            v.tensor_tensor(before[:, :, :], before[:, :, :], chosen, ALU.mult)
            dve.drain()
            v.tensor_reduce(where[:, :], before[:, :, :].rearrange("p e k -> p k e"), AX.X, ALU.add)
            dve.drain()
            v.tensor_copy(S.slot[:, :], where[:, :])
            dve.drain()

        @block.tensor
        def _(pe):
            pe.wait_ge(summed, 1)
            nc.tensor.matmul(count_ps[:, :], c.ones[:, :], count[:, :], start=True, stop=True)
            nc.tensor.matmul(rank_ps[:, :, :], c.above[:, :], chosen, start=True, stop=False)
            nc.tensor.matmul(rank_ps[:, :, :], c.ones[:, :], before[:, :, :], start=False, stop=True)\
              .then_inc(ranked, 1)


def send_tokens(nc, c, S, pool, sent):
    for kt in range(KT):
        nc.gpsimd.indirect_dma_start(S.table, bass.IndirectOffsetOnAxis(ap=S.slot[:, kt:kt + 1], axis=0),
                                     c.XN[:, kt % TILES, :], None).then_inc(sent.sem, 16)
    pool.wait_ge(sent.sem, sent.expect(KT))


def routed_experts(nc, c, name, E, width, S, up, down, gate=None, up_bias=None, down_bias=None, send=False):
    NF = width // P
    GW = min(2, NF)
    NG = NF // GW
    NT = slot_tiles(E)
    assert NT % 2 == 1
    gated = gate is not None
    ring = 2 if gated else 4
    lanes = 1 if gated else 2
    share = NG // lanes
    with ExitStack() as ctx:
        sb, ps, sem = sub_memory(nc, ctx, name + "_")
        w_up = sb("w_up", [P, 2, DK, width])
        w_gate = sb("w_gate", [P, 2, DK, width]) if gated else None
        w_down = sb("w_down", [P, 2, NF, DIM])
        b_up = None if gated else sb("b_up", [P, 2, NF])
        b_down = None if gated else sb("b_down", [P, 2, DIM])
        sent = c.transfers["sent"]
        rows = sb("rows", [P, 2, SPT, DIM])
        x_t = sb("x_t", [P, 2, DK, SLOT_TILE])
        silu = sb("silu", [P, 2, GW * SLOT_TILE]) if gated else None
        hidden = sb("hidden", [P, 2, NF, SLOT_TILE])
        result = sb("result", [P, 2, SPT, DIM])
        x_ps = ps("x_ps", [P, DK, SLOT_TILE])
        up_ps = [ps(f"up{i}", [P, GW, SLOT_TILE]) for i in range(ring)]
        gate_ps = [ps(f"gate{i}", [P, GW, SLOT_TILE]) for i in range(ring)] if gated else None
        out_ps = [ps(f"out{i}", [P, SPT, DIM]) for i in range(2)]
        rows_loaded = [sem(f"rows_loaded{u}") for u in range(2)]
        up_loaded = [sem(f"up_loaded{u}") for u in range(2)]
        down_loaded = [sem(f"down_loaded{u}") for u in range(2)]
        turned, x_ready = sem("turned"), sem("x_ready")
        up_ready, gate_done = sem("up_ready"), sem("gate_done")
        hidden_done = [sem(f"hidden_done{i}") for i in range(lanes)]
        out_ready, out_done = sem("out_ready"), sem("out_done")
        stored, result_free = c.transfers["stored"], sem("result_free")
        block = ctx.enter_context(nc.Block())
        credit = ring // lanes

        def over_tiles(eng, body):
            with eng.Fori(0, NT // 2) as g:
                for u in range(2):
                    body(g * 2 + u, g, u)
            body(NT - 1, NT // 2, 0)

        @block.sync
        def _(sp):
            def load_rows(j, u):
                sp.dma_start(rows[:, u, :, :].unsqueeze(1),
                             S.table.rearrange("(j i p) d -> p j i d", i=SPT, p=P)[:, pieces(j), :, :])\
                  .then_inc(rows_loaded[u], 16)

            def load(j, g, u, again):
                e = pieces(sp.value_load(S.owner[0:1, pieces(j)], min_val=0, max_val=E - 1))
                if again:
                    sp.wait_ge(turned, j - 1)
                    load_rows(j, u)
                if again:
                    sp.wait_ge(up_ready, (j - 1) * NG)
                for w, src in ((w_up, up), (w_gate, gate)):
                    if src is not None:
                        sp.dma_start(w[:, u, :, :].unsqueeze(1), src[e, :, :].rearrange("a (k p) n -> p a k n", p=P))\
                          .then_inc(up_loaded[u], 16)
                if again and not gated:
                    for n in range(lanes):
                        sp.wait_ge(hidden_done[n], (j - 1) * share + credit)
                if not gated:
                    sp.dma_start(b_up[:, u, :].unsqueeze(1), up_bias[e, :, :].rearrange("a p f -> p a f"))\
                      .then_inc(up_loaded[u], 16)
                if again:
                    sp.wait_ge(out_ready, j - 1)
                sp.dma_start(w_down[:, u, :, :].unsqueeze(1), down[e, :, :].rearrange("a (k p) n -> p a k n", p=P))\
                  .then_inc(down_loaded[u], 16)
                if not gated:
                    if again:
                        sp.wait_ge(out_done, j + 1)
                    sp.dma_start(b_down[:, u, :].unsqueeze(1), down_bias[e, :].partition_broadcast(P))\
                      .then_inc(down_loaded[u], 16)

            if not send:
                for u in range(2):
                    load_rows(u, u)
            for u in range(2):
                load(u, 0, u, False)
            if send:
                sp.wait_ge(sent.sem, sent.count + KT * 16)
                for u in range(2):
                    load_rows(u, u)
            with sp.Fori(1, NT // 2) as g:
                for u in range(2):
                    load(g * 2 + u, g, u, True)
            load(NT - 1, NT // 2, 0, True)

        @block.tensor
        def _(pe):
            def transposes(g, u):
                pe.wait_ge(rows_loaded[u], (g + 1) * 16)
                for i in range(SPT):
                    for k in range(DK):
                        last = nc.tensor.transpose(x_ps[:, k, i * P:(i + 1) * P], rows[:, u, i, k * P:(k + 1) * P],
                                                   c.ident[:, :])
                last.then_inc(turned, 1)

            def tile(j, g, u, ahead):
                pe.wait_ge(up_loaded[u], (g + 1) * 32)
                pe.wait_ge(x_ready, j + 1)
                for q in range(NG):
                    bank = (u * NG + q) % ring
                    for w, tiles in ((w_up, up_ps), (w_gate, gate_ps)):
                        if w is not None:
                            for i in range(GW):
                                f = q * GW + i
                                for k in range(DK):
                                    last = nc.tensor.matmul(tiles[bank][:, i, :], w[:, u, k, f * P:(f + 1) * P],
                                                            x_t[:, u, k, :], start=k == 0, stop=k == DK - 1)
                    last.then_inc(up_ready, 1)
                if ahead:
                    transposes(g + u, 1 - u)
                pe.wait_ge(down_loaded[u], (g + 1) * (16 if gated else 32))
                pe.wait_ge(out_done, j + 1)
                for lane in range(lanes):
                    early = share - (lane == (NG - 1) % lanes)
                    if early:
                        pe.wait_ge(hidden_done[lane], j * share + (early + credit))
                for i in range(SPT):
                    for f in range(NF):
                        if i == 0 and f == NF - GW:
                            pe.wait_ge(hidden_done[(NG - 1) % lanes], j * share + (share + credit))
                        last = nc.tensor.matmul(out_ps[u][:, i, :], hidden[:, u, f, i * P:(i + 1) * P],
                                                w_down[:, u, f, :], start=f == 0, stop=f == NF - 1)
                last.then_inc(out_ready, 1)

            transposes(0, 0)
            with pe.Fori(0, NT // 2) as g:
                for u in range(2):
                    tile(g * 2 + u, g, u, ahead=True)
            tile(NT - 1, NT // 2, 0, ahead=False)

        def finish_group(eng, j, u, q):
            n = q % 2
            eng.wait_ge(up_ready, j * NG + (q + 1))
            for i in range(GW):
                f = q * GW + i
                src, dst, bias = up_ps[q][:, i, :], hidden[:, u, f, :], b_up[:, u, f:f + 1]
                if n:
                    last = nc.scalar.activation(dst, src, ACT.Relu, bias=bias)
                else:
                    last = nc.vector.tensor_scalar(dst, src, bias, 0.0, ALU.add, ALU.max)
            last.then_inc(hidden_done[n], 1)

        @block.scalar
        def _(act):
            if not gated:
                act.sem_inc(hidden_done[1], credit)

            def body(j, g, u):
                if not gated:
                    act.wait_ge(up_loaded[u], (g + 1) * 32)
                act.wait_ge(turned, j + 1)
                nc.scalar.activation(x_t[:, u, :, :], x_ps[:, :, :], ACT.Copy).then_inc(x_ready, 1)
                for q in range(NG):
                    if gated:
                        bank = (u * NG + q) % ring
                        act.wait_ge(up_ready, j * NG + (q + 1))
                        nc.scalar.activation(silu[:, bank, :].rearrange("p (f n) -> p f n", f=GW),
                                             gate_ps[bank][:, :, :], ACT.Silu).then_inc(gate_done, 1)
                    elif q % 2:
                        finish_group(act, j, u, q)

            over_tiles(act, body)

        @block.vector
        def _(dve):
            v = nc.vector
            dve.sem_inc(hidden_done[0], credit)
            dve.sem_inc(out_done, 2)
            dve.sem_inc(result_free, 2)

            def body(j, g, u):
                if not gated:
                    dve.wait_ge(up_loaded[u], (g + 1) * 32)
                for q in range(NG):
                    bank = (u * NG + q) % ring
                    if gated:
                        dve.wait_ge(gate_done, j * NG + (q + 1))
                        v.tensor_tensor(hidden[:, u, q * GW:(q + 1) * GW, :], up_ps[bank][:, :, :],
                                        silu[:, bank, :].rearrange("p (f n) -> p f n", f=GW), ALU.mult)\
                         .then_inc(hidden_done[0], 1)
                    elif q % 2 == 0:
                        finish_group(dve, j, u, q)
                dve.wait_ge(result_free, j + 1)
                dve.wait_ge(out_ready, j + 1)
                if gated:
                    v.tensor_copy(result[:, u, :, :], out_ps[u][:, :, :]).then_inc(out_done, 1)
                else:
                    dve.wait_ge(down_loaded[u], (g + 1) * 32)
                    v.tensor_tensor(result[:, u, :, :], out_ps[u][:, :, :],
                                    b_down[:, u, :].unsqueeze(1).to_broadcast([P, SPT, DIM]), ALU.add)\
                     .then_inc(out_done, 1)

            over_tiles(dve, body)

        @block.gpsimd
        def _(pool):
            if send:
                send_tokens(nc, c, S, pool, sent)
            before = stored.count
            stored.expect(NT)

            def body(j, g, u):
                pool.wait_ge(out_done, j + 3)
                pool.dma_start(S.results.rearrange("(j i p) d -> p j i d", i=SPT, p=P)[:, pieces(j), :, :],
                               result[:, u, :, :].unsqueeze(1)).then_inc(stored.sem, 16)
                pool.wait_ge(stored.sem, (j + 1) * 16 + before)
                pool.sem_inc(result_free, 1)

            over_tiles(pool, body)


class Collection:

    GROUPS = 8
    TPG = TILES // GROUPS

    def __init__(self, nc, c, ctx, E, S, gate, fresh):
        self.nc, self.c, self.S, self.gate, self.fresh = nc, c, S, gate, fresh
        self.results = S.results[0:slot_tiles(E) * SLOT_TILE, :]
        self.got = ctx.enter_context(nc.sbuf_tensor(f"got{c.count()}", [P, CHOICES, TILES, DIM], F32))
        self.arrived = [c.transfers[f"arrived{n}"] for n in range(self.GROUPS)]

    def gather(self, n):
        for t in range(n * self.TPG, (n + 1) * self.TPG):
            for k in range(CHOICES):
                at = k * TILES + t
                self.nc.gpsimd.indirect_dma_start(
                    self.got[:, k, t, :], None, self.results,
                    bass.IndirectOffsetOnAxis(ap=self.S.slot[:, at:at + 1], axis=0)).then_inc(self.arrived[n].sem, 16)

    def combine(self, dve, n, final=None):
        v, c = self.nc.vector, self.c
        arrived = self.arrived[n]
        tiles = list(range(n * self.TPG, (n + 1) * self.TPG))
        dve.wait_ge(arrived.sem, arrived.expect(self.TPG * CHOICES))
        dve.drain()
        for k in range(CHOICES):
            for t in tiles:
                acc, part = c.ACC[:, t, :], c.share[:, k * TILES + t:k * TILES + t + 1]
                if self.fresh and k == 0:
                    v.tensor_scalar(acc, self.got[:, k, t, :], part, None, ALU.mult)
                else:
                    v.scalar_tensor_tensor(acc, self.got[:, k, t, :], part, acc, ALU.mult, ALU.add)
            if k == 0:
                dve.drain()
        add_to_residual(self.nc, c, dve, c.ACC[:, tiles[0]:tiles[0] + self.TPG, :], tiles, self.gate, final)


def collect(nc, c, E, S, gate):
    with ExitStack() as ctx:
        results = Collection(nc, c, ctx, E, S, gate, fresh=True)
        block = ctx.enter_context(nc.Block())

        @block.gpsimd
        def _(pool):
            for n in range(results.GROUPS):
                results.gather(n)

        @block.vector
        def _(dve):
            for n in range(results.GROUPS):
                results.combine(dve, n)
            dve.drain()



def hash_router(nc, c):
    with ExitStack() as ctx:
        sb, ps, sem = sub_memory(nc, ctx)
        s, a, k, g, h = (sb(f"hash_{n}", [P, TILES]) for n in ("sum", "abs", "whole", "over", "bucket"))
        block = ctx.enter_context(nc.Block())

        @block.vector
        def _(dve):
            v = nc.vector

            def ts(*args):
                v.tensor_scalar(*args)
                dve.drain()

            def tt(*args):
                v.tensor_tensor(*args)
                dve.drain()

            S, A, K, G, H = (x[:, :] for x in (s, a, k, g, h))
            v.memset(c.share[:, :], 0.5)
            tt(S, c.XN[:, :, 0], c.XN[:, :, 1], ALU.add)
            ts(A, S, -1.0, None, ALU.mult)
            tt(A, A, S, ALU.max)
            ts(K, A, MAGIC, None, ALU.add)
            ts(K, K, MAGIC, None, ALU.subtract)
            tt(G, K, A, ALU.is_gt)
            tt(K, K, G, ALU.subtract)
            ts(G, S, 0.0, -2.0, ALU.is_lt, ALU.mult)
            ts(G, G, 1.0, None, ALU.add)
            tt(K, K, G, ALU.mult)
            ts(G, K, 0.125, -0.4375, ALU.mult, ALU.add)
            ts(G, G, MAGIC, None, ALU.add)
            ts(G, G, MAGIC, -8.0, ALU.subtract, ALU.mult)
            tt(H, K, G, ALU.add)
            by_expert = [P, 8, TILES]
            iota = c.iota[:, 0:8].unsqueeze(2).to_broadcast(by_expert)
            previous = c.iota[:, 32:40].unsqueeze(2).to_broadcast(by_expert)
            bucket = H.unsqueeze(1).to_broadcast(by_expert)
            tt(c.chosen[:, 0:8, 0:TILES], iota, bucket, ALU.is_equal)
            tt(c.chosen[:, 0:8, TILES:KT], previous, bucket, ALU.is_equal)


def softmax_router(nc, c, name, router, E, eps=None, gain=None, shift=None):
    again = gain is not None
    with ExitStack() as ctx:
        sb, ps, sem = sub_memory(nc, ctx, name + "_")
        w = sb("w", [P, DK, E])
        affine = sb("affine", [P, 2, DK])
        w_shift = sb("w_shift", [P, DK, E])
        stats = sb("stats", [P, TILES, 6])
        mean, diff, var, dev, rstd = (sb(n, [P, TILES]) for n in ("mean", "diff", "var", "dev", "rstd"))
        sums = sb("sums", [P, 2, E])
        p = sb("probs", [P, TILES, E])
        one = sb("stat", [P, TILES])
        top = sb("top", [P, TILES, 8])
        at = sb("at", [P, TILES, 8], U32)
        atf = sb("atf", [P, TILES, 8])
        logits = ps("logits", [P, TILES, E])
        sums_ps = ps("sums_ps", [P, 2, E])
        loaded, weights_ready, logits_ready = sem("loaded"), sem("weights_ready"), sem("logits_ready")
        var_ready, dev_ready = sem("var_ready"), sem("dev_ready")
        shifted, exp_ready = sem("shifted"), sem("exp_ready")
        block = ctx.enter_context(nc.Block())

        @block.sync
        def _(sp):
            sp.dma_start(w[:, :, :], router.rearrange("(k p) e -> p k e", p=P)).then_inc(loaded, 16)
            if again:
                sp.dma_start(affine[:, 0, :], gain).then_inc(loaded, 16)
                sp.dma_start(affine[:, 1, :], shift).then_inc(loaded, 16)

        @block.tensor
        def _(pe):
            if again:
                pe.wait_ge(weights_ready, 1)
                for n, x in enumerate((w, w_shift)):
                    for k in range(DK):
                        nc.tensor.matmul(sums_ps[:, n, :], c.ones[:, :], x[:, k, :], start=k == 0, stop=k == DK - 1)
            else:
                pe.wait_ge(loaded, 16)
            for t in range(TILES):
                for k in range(DK):
                    last = nc.tensor.matmul(logits[:, t, :], c.XT[:, k, t * P:(t + 1) * P], w[:, k, :],
                                            start=k == 0, stop=k == DK - 1)
            last.then_inc(logits_ready, 1)

        @block.scalar
        def _(act):
            if again:
                act.wait_ge(var_ready, 1)
                nc.scalar.activation(dev[:, :], var[:, :], ACT.Sqrt).then_inc(dev_ready, 1)
            act.wait_ge(shifted, 1)
            nc.scalar.activation(p[:, :, :], p[:, :, :], ACT.Exp).then_inc(exp_ready, 1)

        @block.vector
        def _(dve):
            v = nc.vector
            wide = [P, TILES, E]

            def by_token(x):
                return x[:, :].unsqueeze(2).to_broadcast(wide)

            if again:
                dve.wait_ge(loaded, 48)
                for k in range(DK):
                    v.tensor_scalar(w_shift[:, k, :], w[:, k, :], affine[:, 1, k:k + 1], None, ALU.mult)
                dve.drain()
                for k in range(DK):
                    last = v.tensor_scalar(w[:, k, :], w[:, k, :], affine[:, 0, k:k + 1], None, ALU.mult)
                last.then_inc(weights_ready, 1)
                row_statistics(nc, dve, c.XN, stats)
                mean_and_variance(nc, dve, stats, mean, diff, var, var_ready)
                dve.wait_ge(dev_ready, 1)
                reciprocal_root(nc, dve, var, dev, rstd)
                dve.wait_ge(logits_ready, 1)
                v.tensor_copy(sums[:, :, :], sums_ps[:, :, :])
                dve.drain()
                v.tensor_tensor(p[:, :, :], by_token(mean), sums[:, 0, :].unsqueeze(1).to_broadcast(wide), ALU.mult)
                dve.drain()
                v.tensor_tensor(p[:, :, :], logits[:, :, :], p[:, :, :], ALU.subtract)
                dve.drain()
                v.tensor_tensor(p[:, :, :], p[:, :, :], by_token(rstd), ALU.mult)
                dve.drain()
                v.tensor_tensor(p[:, :, :], p[:, :, :], sums[:, 1, :].unsqueeze(1).to_broadcast(wide), ALU.add)
                dve.drain()
                value = p
            else:
                dve.wait_ge(logits_ready, 1)
                value = logits
            v.tensor_reduce(one[:, :], value[:, :, :], AX.X, ALU.max)
            dve.drain()
            v.tensor_tensor(p[:, :, :], value[:, :, :], by_token(one), ALU.subtract).then_inc(shifted, 1)
            dve.wait_ge(exp_ready, 1)
            v.tensor_reduce(one[:, :], p[:, :, :], AX.X, ALU.add)
            dve.drain()
            v.reciprocal(one[:, :], one[:, :])
            dve.drain()
            v.tensor_tensor(p[:, :, :], p[:, :, :], by_token(one), ALU.mult)
            dve.drain()
            for t in range(TILES):
                v.max(top[:, t, :], p[:, t, :])
            dve.drain()
            for t in range(TILES):
                v.max_index(at[:, t, :], top[:, t, :], p[:, t, :])
            dve.drain()
            v.tensor_copy(atf[:, :, :], at[:, :, :])
            if eps is not None:
                v.tensor_tensor(one[:, :], top[:, :, 0], top[:, :, 1], ALU.add)
                dve.drain()
                v.tensor_scalar(one[:, :], one[:, :], eps, None, ALU.add)
                dve.drain()
                v.reciprocal(one[:, :], one[:, :])
                dve.drain()
                v.tensor_tensor(top[:, :, 0:CHOICES], top[:, :, 0:CHOICES],
                                one[:, :].unsqueeze(2).to_broadcast([P, TILES, CHOICES]), ALU.mult)
            dve.drain()
            by_expert = [P, E, TILES]
            iota = c.iota[:, 0:E].unsqueeze(2).to_broadcast(by_expert)
            for rank in range(CHOICES):
                kt = slice(rank * TILES, (rank + 1) * TILES)
                v.tensor_tensor(c.chosen[:, 0:E, kt], iota, atf[:, :, rank].unsqueeze(1).to_broadcast(by_expert),
                                ALU.is_equal)
                v.tensor_copy(c.share[:, kt], top[:, :, rank])
            dve.drain()


def layer1_attention(nc, c, a):
    HEADS, DH = 8, 128
    INNER = HEADS * DH
    HALF = HEADS // 2
    SCALE = float(DH) ** -0.25
    CHUNKS = 8
    with ExitStack() as ctx:
        sb, ps, sem = sub_memory(nc, ctx, "a1_")
        wq = sb("wq", [P, DK, INNER])
        wk = sb("wk", [CP, CK, INNER])
        wv = sb("wv", [CP, CK, INNER])
        wo = sb("wo", [P, HEADS, DIM])
        bo = sb("bo", [P, DIM])
        context = sb("context", [CP, 2, CK, KEYS])
        q = sb("q", [P, HEADS, SEQ])
        k = sb("k", [P, HEADS, KEYS])
        v = sb("v", [KEYS, 2, INNER])
        probs = sb("probs", [P, TPB, HEADS, KEYS])
        stat = sb("stat", [P, TPB, HEADS])
        probs_t = sb("probs_t", [KEYS, HEADS, P])
        mixed = sb("mixed", [P, HEADS, P])
        branch = sb("branch", [P, DIM])
        S = ps("scores", [P, 2, 512])
        T = ps("turned_ps", [KEYS, 2, 512])
        M = ps("mixed_ps", [P, 2, 512])
        G = ps("projected", [P, 2, 512])
        norm = Normalisation(nc, c, ctx, turned=[G[:, u, :] for u in range(2)])
        w_loaded = sem("w_loaded")
        ctx_loaded = [sem(f"ctx_loaded{u}") for u in range(2)]
        chunk_ready, chunk_done = sem("chunk_ready"), sem("chunk_done")
        scores_ready, scores_read = sem("scores_ready"), sem("scores_read")
        shifted, exp_done, probs_ready = sem("shifted"), sem("exp_done"), sem("probs_ready")
        turned, turned_done = sem("turned"), sem("turned_done")
        mixed_ready, mixed_done = sem("mixed_ready"), sem("mixed_done")
        out_ready, out_done = sem("out_ready"), sem("out_done")
        block = ctx.enter_context(nc.Block())


        def batches(eng, body):
            body(0, 0, True, False)
            with eng.Fori(0, BATCH // 2 - 1) as g:
                for u in (1, 0):
                    body(g * 2 + (2 - u), u, False, False)
            body(BATCH - 1, 1, False, True)

        @block.sync
        def _(sp):
            def load(b, u):
                sp.dma_start(context[:, u, :, :].unsqueeze(1),
                             a["context_T"][pieces(b), :, :].rearrange("b (k p) s -> p b k s", p=CP))\
                  .then_inc(ctx_loaded[u], 16)

            load(0, 0)
            load(1, 1)
            sp.dma_start(wq[:, :, :], a["L1_xattn_Wq"].rearrange("(k p) n -> p k n", p=P)).then_inc(w_loaded, 16)
            sp.dma_start(wk[:, :, :], a["L1_xattn_Wk"].rearrange("(k p) n -> p k n", p=CP)).then_inc(w_loaded, 16)
            sp.dma_start(wv[:, :, :], a["L1_xattn_Wv"].rearrange("(k p) n -> p k n", p=CP)).then_inc(w_loaded, 16)
            sp.dma_start(wo[:, :, :], a["L1_xattn_Wo"].rearrange("(h p) n -> p h n", p=P)).then_inc(w_loaded, 16)
            sp.dma_start(bo[:, :], spread(a["L1_xattn_bo"])).then_inc(w_loaded, 16)
            with sp.Fori(1, BATCH // 2) as g:
                for u in range(2):
                    sp.wait_ge(chunk_ready, g * (2 * CHUNKS) + (u - 1) * CHUNKS)
                    load(g * 2 + u, u)

        @block.tensor
        def _(pe):
            def project(b, u, begin=False):
                for n in range(CHUNKS):
                    if not begin or n >= 2:
                        pe.wait_ge(chunk_done, b * CHUNKS + (n - 1))
                    bank = n % 2
                    if n < 4:
                        for h in range(2 * n, 2 * n + 2):
                            for kk in range(DK):
                                last = nc.tensor.matmul(G[:, bank, (h % 2) * SEQ:(h % 2 + 1) * SEQ],
                                                        wq[:, kk, h * DH:(h + 1) * DH],
                                                        c.XT[:, kk, pieces(b * SEQ, SEQ)],
                                                        start=kk == 0, stop=kk == DK - 1)
                    elif n < 6:
                        if n == 4:
                            pe.wait_ge(ctx_loaded[u], b * 8 + (16 - 8 * u))
                        for h in range(HALF):
                            w = slice((bank * HALF + h) * DH, (bank * HALF + h + 1) * DH)
                            for kk in range(CK):
                                last = nc.tensor.matmul(G[:, bank, h * KEYS:(h + 1) * KEYS], wk[:, kk, w],
                                                        context[:, u, kk, :], start=kk == 0, stop=kk == CK - 1)
                    else:
                        for kk in range(CK):
                            last = nc.tensor.matmul(G[0:KEYS, bank, :], context[:, u, kk, :],
                                                    wv[:, kk, bank * 512:(bank + 1) * 512],
                                                    start=kk == 0, stop=kk == CK - 1)
                    last.then_inc(chunk_ready, 1)

            def scores(b, i):
                if i == 0:
                    pe.wait_ge(chunk_done, (b + 1) * CHUNKS)
                pe.wait_ge(scores_read, b * TPB + (i + 1))
                for h in range(HEADS):
                    last = nc.tensor.matmul(S[:, h // HALF, (h % HALF) * KEYS:(h % HALF + 1) * KEYS],
                                            q[:, h, i * P:(i + 1) * P], k[:, h, :], start=True, stop=True)
                last.then_inc(scores_ready, 1)

            def project_values(t, bank):
                pe.wait_ge(mixed_done, t * 2 + 2)
                pe.wait_ge(out_done, t + 1)
                for h in range(HEADS):
                    last = nc.tensor.matmul(G[:, bank, 0:DIM], mixed[:, h, :], wo[:, h, :], start=h == 0,
                                            stop=h == HEADS - 1)
                last.then_inc(out_ready, 1)

            def attend(b, u, i, first, final):
                n = b * TPB + i
                pe.wait_ge(probs_ready, n + 1)
                for half in range(2):
                    for h in range(HALF):
                        last = nc.tensor.transpose(T[:, half, h * P:(h + 1) * P], probs[:, i, half * HALF + h, :],
                                                   c.ident[:, :])
                    last.then_inc(turned, 1)
                if not first:
                    if i == 0 and not final:
                        pe.wait_ge(chunk_done, (b + 2) * CHUNKS)
                    project_values(n - 1, i)
                for half in range(2):
                    pe.wait_ge(turned_done, n * 2 + (half + 1))
                    for h in range(HALF):
                        r = half * HALF + h
                        last = nc.tensor.matmul(M[:, half, h * P:(h + 1) * P], v[:, u, r * DH:(r + 1) * DH],
                                                probs_t[:, r, :], start=True, stop=True)
                    last.then_inc(mixed_ready, 1)

            def body(b, u, first, final):
                scores(b, 1)
                if not final:
                    pe.wait_ge(out_done, b * TPB + 1)
                    project(b + 1, 1 - u)
                attend(b, u, 0, first, final)
                if not final:
                    scores(b + 1, 0)
                attend(b, u, 1, False, final)

            norm.turn(pe)
            norm.wait_turned(pe)
            pe.wait_ge(w_loaded, 80)
            project(0, 0, begin=True)
            scores(0, 0)
            batches(pe, body)
            project_values(TILES - 1, 0)

        @block.scalar
        def _(act):
            def copy_chunk(b, u, n):
                act.wait_ge(chunk_ready, b * CHUNKS + (n + 1))
                bank = n % 2
                if n < 4:
                    last = nc.scalar.activation(q[:, 2 * n:2 * n + 2, :].rearrange("p h s -> p (h s)"), G[:, bank, :],
                                                ACT.Copy, scale=SCALE)
                elif n < 6:
                    last = nc.scalar.activation(k[:, bank * HALF:(bank + 1) * HALF, :].rearrange("p h s -> p (h s)"),
                                                G[:, bank, 0:HALF * KEYS], ACT.Copy, scale=SCALE)
                else:
                    last = nc.scalar.activation(v[:, u, bank * 512:(bank + 1) * 512], G[0:KEYS, bank, :], ACT.Copy)
                last.then_inc(chunk_done, 1)

            def exp(n, i):
                act.wait_ge(shifted, n + 1)
                nc.scalar.activation(probs[:, i, :, :], probs[:, i, :, :], ACT.Exp).then_inc(exp_done, 1)

            def body(b, u, first, final):
                for i in range(TPB):
                    n = b * TPB + i
                    if i == 0 and not final:
                        for m in range(CHUNKS):
                            if m == 2:
                                exp(n + 1, 1)
                            copy_chunk(b + 1, 1 - u, m)
                    for half in range(2):
                        act.wait_ge(turned, n * 2 + (half + 1))
                        nc.scalar.activation(probs_t[:, half * HALF:(half + 1) * HALF, :].rearrange("p h t -> p (h t)"),
                                             T[:, half, :], ACT.Copy).then_inc(turned_done, 1)
                    if i == 0 and final or i == 1 and not final:
                        exp(n + 1, 1 - i)
                    for half in range(2):
                        act.wait_ge(mixed_ready, n * 2 + (half + 1))
                        nc.scalar.activation(mixed[:, half * HALF:(half + 1) * HALF, :].rearrange("p h t -> p (h t)"),
                                             M[:, half, :], ACT.Copy).then_inc(mixed_done, 1)

            norm.root(act)
            norm.copy(act)
            for n in range(CHUNKS):
                copy_chunk(0, 0, n)
            exp(0, 0)
            batches(act, body)

        @block.vector
        def _(dve):
            vv = nc.vector
            norm.statistics(dve)
            norm.apply(dve)
            grid = [P, HEADS, KEYS]
            scores_r = S[:, :, 0:HALF * KEYS].rearrange("p a (h s) -> p a h s", s=KEYS)
            dve.sem_inc(scores_read, 1)
            dve.sem_inc(out_done, 2)
            dve.wait_ge(w_loaded, 80)

            def softmax(n, i):
                st = stat[:, i, :]
                by_bank = st.rearrange("p (a h) -> p a h", h=HALF)
                dve.wait_ge(scores_ready, n + 1)
                vv.tensor_reduce(by_bank, scores_r, AX.X, ALU.max)
                dve.drain()
                vv.tensor_tensor(probs[:, i, :, :].rearrange("p (a h) s -> p a h s", h=HALF), scores_r,
                                 by_bank.unsqueeze(3).to_broadcast([P, 2, HALF, KEYS]), ALU.subtract)
                dve.drain()
                dve.sem_inc(scores_read, 1)
                dve.sem_inc(shifted, 1)
                dve.wait_ge(exp_done, n + 1)
                vv.tensor_reduce(st, probs[:, i, :, :], AX.X, ALU.add)
                dve.drain()
                vv.reciprocal(st, st)
                dve.drain()
                vv.tensor_tensor(probs[:, i, :, :], probs[:, i, :, :], st.unsqueeze(2).to_broadcast(grid), ALU.mult)\
                  .then_inc(probs_ready, 1)

            def add_output(t, bank):
                dve.wait_ge(out_ready, t + 1)
                vv.tensor_tensor(branch[:, :], G[:, bank, 0:DIM], bo[:, :], ALU.add).then_inc(out_done, 1)
                add_to_residual(nc, c, dve, branch[:, :].unsqueeze(1), [t], 1)

            def body(b, u, first, final):
                for i in range(TPB):
                    n = b * TPB + i
                    if not (final and i == 1):
                        softmax(n + 1, 1 - i)
                    if not (first and i == 0):
                        add_output(n - 1, i)

            softmax(0, 0)
            batches(dve, body)
            add_output(TILES - 1, 0)


def narrow_attention(nc, c, a, layer):
    HEADS, DH = 16, 16
    HT = P // DH
    SCALE = float(DH) ** -0.5
    CLAMP = 10000.0
    final_layer = layer == 3
    with ExitStack() as ctx:
        sb, ps, sem = sub_memory(nc, ctx, f"a{layer}_")
        wq = sb("wq", [P, DK, DIM])
        wk = sb("wk", [CP, CK, DIM])
        wv = sb("wv", [CP, CK, DIM])
        context = sb("context", [CP, 2, CK, KEYS])
        q = sb("q", [P, DK, SEQ])
        k = sb("k", [P, 2, DK, KEYS])
        k_wide = sb("k_wide", [P, DK, HT, KEYS])
        v = sb("v", [KEYS, 2, HEADS, DH + 1])
        probs = sb("probs", [P, TPB, HEADS, KEYS])
        stat = sb("stat", [P, TPB, HEADS])
        probs_t = sb("probs_t", [KEYS, 4, 4, P])
        branch = sb("branch", [P, DIM])
        if final_layer:
            mask8 = sb("mask8", [P, TILES], U8)
            keep = sb("keep", [P, TILES])
            keep_now = sb("keep_now", [P, TPB])
        else:
            wo = sb("wo", [P, DK, DIM])
            bqk = sb("bqk", [P, 2, DK])
            bo = sb("bo", [P, DIM])
            bv = sb("bv", [P, DIM])
            mixed = sb("mixed", [P, DIM])
            mixed_t = sb("mixed_t", [P, DK, P])
        S = ps("scores", [P, 4, 512])
        T = ps("turned", [P, 2, 512])
        Q = ps("q_ps", [P, DK * SEQ])
        KV = ps("kv_ps", [P, 512])
        norm = Normalisation(nc, c, ctx, turned=[S[:, u, :] for u in range(2)])
        w_loaded = sem("w_loaded")
        ctx_loaded = [sem(f"ctx_loaded{u}") for u in range(2)]
        setup_done = sem("setup_done")
        q_ready, kv_ready, q_done, kv_done = sem("q_ready"), sem("kv_ready"), sem("q_done"), sem("kv_done")
        k_wide_ready = sem("k_wide_ready")
        scores_ready, scores_read = sem("scores_ready"), sem("scores_read")
        shifted, exp_done = sem("shifted"), sem("exp_done")
        turned, turned_done = sem("turned"), sem("turned_done")
        values_ready, values_read, mixed_done = sem("values_ready"), sem("values_read"), sem("mixed_done")
        mt_ready, mt_done = sem("mt_ready"), sem("mt_done")
        out_ready, out_done = sem("out_ready"), sem("out_done")
        block = ctx.enter_context(nc.Block())
        LOADS = 48 + (16 if final_layer else 80)

        def batches(eng, body):
            body(0, 0, True, False)
            with eng.Fori(0, BATCH // 2 - 1) as g:
                for u in (1, 0):
                    body(g * 2 + (2 - u), u, False, False)
            body(BATCH - 1, 1, False, True)

        @block.sync
        def _(sp):
            def load(b, u):
                sp.dma_start(context[:, u, :, :].unsqueeze(1),
                             a["context_T"][pieces(b), :, :].rearrange("b (k p) s -> p b k s", p=CP))\
                  .then_inc(ctx_loaded[u], 16)

            load(0, 0)
            load(1, 1)
            if final_layer:
                weights = [(wq, a["L3_Wq_T"], P), (wk, a["L3_Wkv_T"][:, 0:DIM], CP),
                           (wv, a["L3_Wkv_T"][:, DIM:2 * DIM], CP)]
            else:
                weights = [(wq, a["L2_xattn_Wq"], P), (wk, a["L2_xattn_Wk"], CP), (wv, a["L2_xattn_Wv"], CP),
                           (wo, a["L2_xattn_Wo"], P)]
            for dst, src, p in weights:
                sp.dma_start(dst[:, :, :], src.rearrange("(k p) n -> p k n", p=p)).then_inc(w_loaded, 16)
            if final_layer:
                sp.dma_start(mask8[:, :], a["mask_BxS_bk0"]).then_inc(w_loaded, 16)
            else:
                sp.dma_start(bqk[:, 0, :], a["L2_bq"]).then_inc(w_loaded, 16)
                sp.dma_start(bqk[:, 1, :], a["L2_bk"]).then_inc(w_loaded, 16)
                sp.dma_start(bo[:, :], spread(a["L2_xattn_bo"])).then_inc(w_loaded, 16)
                sp.dma_start(bv[:, :], spread(a["L2_xattn_bv"])).then_inc(w_loaded, 16)
            with sp.Fori(1, BATCH // 2) as g:
                for u in range(2):
                    sp.wait_ge(kv_ready, g * 2 + (u - 1))
                    load(g * 2 + u, u)

        @block.tensor
        def _(pe):
            def project(b, u, begin=False):
                for m in range(DK):
                    for kk in range(DK):
                        last = nc.tensor.matmul(Q[:, m * SEQ:(m + 1) * SEQ], wq[:, kk, m * P:(m + 1) * P],
                                                c.XT[:, kk, pieces(b * SEQ, SEQ)], start=kk == 0, stop=kk == DK - 1)
                last.then_inc(q_ready, 1)
                pe.wait_ge(ctx_loaded[u], b * 8 + (16 - 8 * u))
                if not (final_layer or begin):
                    pe.wait_ge(out_done, b * TPB - 1)
                for m in range(DK):
                    for kk in range(CK):
                        nc.tensor.matmul(KV[:, m * KEYS:(m + 1) * KEYS], wk[:, kk, m * P:(m + 1) * P],
                                         context[:, u, kk, :], start=kk == 0, stop=kk == CK - 1)
                for kk in range(CK):
                    last = nc.tensor.matmul(KV[0:KEYS, DIM:2 * DIM], context[:, u, kk, :], wv[:, kk, :],
                                            start=kk == 0, stop=kk == CK - 1)
                last.then_inc(kv_ready, 1)

            def scores(b, i):
                if i == 0:
                    pe.wait_ge(q_done, b + 1)
                    pe.wait_ge(k_wide_ready, b + 1)
                pe.wait_ge(scores_read, b * TPB + (i + 1))
                for h in range(0, HEADS, 4):
                    m = h // HT
                    last = nc.tensor.matmul(S[:, h // 4, 0:4 * KEYS], q[:, m, i * P:(i + 1) * P],
                                            k_wide[:, m, h % HT:h % HT + 4, :].rearrange("p h s -> p (h s)"),
                                            start=True, stop=True)
                last.then_inc(scores_ready, 1)

            def turn(n, i, r):
                pe.wait_ge(turned_done, n * 4 + (r + 1))
                for h in range(4):
                    last = nc.tensor.transpose(T[0:KEYS, r % 2, h * P:(h + 1) * P], probs[:, i, 4 * r + h, :],
                                               c.ident[:, :])
                last.then_inc(turned, 1)

            def mix(n, u, r):
                pe.wait_ge(turned_done, n * 4 + (r + 3))
                for h in range(4 * r, 4 * r + 4):
                    last = nc.tensor.matmul(Q[:, h * (DH + 1):(h + 1) * (DH + 1)], probs_t[:, r, h % 4, :],
                                            v[:, u, h, :], start=True, stop=True)
                return last

            def turn_values(t):
                pe.wait_ge(mixed_done, t + 1)
                pe.wait_ge(out_done, t + 2)
                for m in range(DK):
                    last = nc.tensor.transpose(KV[:, m * P:(m + 1) * P], mixed[:, m * P:(m + 1) * P], c.ident[:, :])
                last.then_inc(mt_ready, 1)

            def project_values(t):
                pe.wait_ge(mt_done, t + 1)
                for m in range(DK):
                    last = nc.tensor.matmul(KV[:, DIM:2 * DIM], mixed_t[:, m, :], wo[:, m, :], start=m == 0, stop=m == DK - 1)
                last.then_inc(out_ready, 1)

            def attend(b, u, i, first, final):
                n = b * TPB + i
                tail = not final_layer and not first
                pe.wait_ge(exp_done, n + 1)
                turn(n, i, 0)
                turn(n, i, 1)
                if i == 0 and not final:
                    pe.wait_ge(q_done, b + 2)
                    pe.wait_ge(kv_done, b + 2)
                if tail:
                    turn_values(n - 1)
                pe.wait_ge(values_read, n + 1)
                mix(n, u, 0)
                turn(n, i, 2)
                mix(n, u, 1)
                turn(n, i, 3)
                if tail:
                    project_values(n - 1)
                mix(n, u, 2)
                mix(n, u, 3).then_inc(values_ready, 1)

            def body(b, u, first, final):
                scores(b, 1)
                if not final:
                    pe.wait_ge(values_read, b * TPB + 1)
                    project(b + 1, 1 - u)
                attend(b, u, 0, first, final)
                if not final:
                    scores(b + 1, 0)
                attend(b, u, 1, False, final)

            norm.turn(pe)
            norm.wait_turned(pe)
            pe.wait_ge(w_loaded, LOADS)
            project(0, 0, begin=True)
            scores(0, 0)
            batches(pe, body)
            if not final_layer:
                turn_values(TILES - 1)
                project_values(TILES - 1)

        @block.scalar
        def _(act):
            act.sem_inc(turned_done, 2)
            norm.root(act)
            norm.copy(act)
            act.wait_ge(setup_done, 1)

            def evacuate_qkv(b, u):
                act.wait_ge(q_ready, b + 1)
                for m in range(DK):
                    if final_layer:
                        last = nc.scalar.activation(q[:, m, :], Q[:, m * SEQ:(m + 1) * SEQ], ACT.Copy, scale=SCALE)
                    else:
                        last = nc.scalar.activation(q[:, m, :], Q[:, m * SEQ:(m + 1) * SEQ], ACT.Identity, bias=bqk[:, 0, m:m + 1])
                last.then_inc(q_done, 1)
                act.wait_ge(kv_ready, b + 1)
                for m in range(DK):
                    if final_layer:
                        nc.scalar.activation(k[:, u, m, :], KV[:, m * KEYS:(m + 1) * KEYS], ACT.Copy)
                    else:
                        nc.scalar.activation(k[:, u, m, :], KV[:, m * KEYS:(m + 1) * KEYS], ACT.Identity,
                                             bias=bqk[:, 1, m:m + 1])
                nc.scalar.activation(v[:, u, :, 0:DH], KV[0:KEYS, DIM:2 * DIM].rearrange("s (h d) -> s h d", d=DH),
                                     ACT.Copy).then_inc(kv_done, 1)

            def exp(n, i):
                act.wait_ge(shifted, n + 1)
                nc.scalar.activation(probs[:, i, :, :], probs[:, i, :, :], ACT.Exp,
                                     scale=keep_now[:, i:i + 1] if final_layer else SCALE).then_inc(exp_done, 1)

            def copy_values(t):
                act.wait_ge(mt_ready, t + 1)
                nc.scalar.activation(mixed_t[:, :, :], KV[:, 0:DIM].rearrange("p (m t) -> p m t", t=P),
                                     ACT.Copy).then_inc(mt_done, 1)

            def body(b, u, first, final):
                if not final:
                    evacuate_qkv(b + 1, 1 - u)
                for i in range(TPB):
                    n = b * TPB + i
                    for r in range(4):
                        if r == 2 and not final_layer and not (first and i == 0):
                            copy_values(n - 1)
                        act.wait_ge(turned, n * 4 + (r + 1))
                        nc.scalar.activation(probs_t[:, r, :, :].rearrange("p r t -> p (r t)"), T[0:KEYS, r % 2, :],
                                             ACT.Copy).then_inc(turned_done, 1)
                    if not (final and i == 1):
                        exp(n + 1, 1 - i)

            evacuate_qkv(0, 0)
            exp(0, 0)
            batches(act, body)
            if not final_layer:
                copy_values(TILES - 1)

        @block.gpsimd
        def _(pool):
            pool.wait_ge(setup_done, 1)
            wide = [P, HT, KEYS]

            def body(b, u, first, final):
                pool.wait_ge(kv_done, b + 1)
                for m in range(DK):
                    last = nc.gpsimd.tensor_tensor(k_wide[:, m, :, :], k[:, u, m, :].unsqueeze(1).to_broadcast(wide),
                                                   c.headmask[:, 4:4 + HT].unsqueeze(2).to_broadcast(wide), ALU.mult)
                last.then_inc(k_wide_ready, 1)

            batches(pool, body)

        @block.vector
        def _(dve):
            vv = nc.vector
            norm.statistics(dve)
            norm.apply(dve)
            dve.sem_inc(scores_read, 1)
            dve.sem_inc(values_read, 1)
            dve.sem_inc(out_done, 2)
            dve.wait_ge(w_loaded, LOADS)
            vv.memset(v[:, :, :, :], 1.0)
            if final_layer:
                vv.tensor_copy(keep[:, :], mask8[:, :])
            dve.drain()
            dve.sem_inc(setup_done, 1)
            scores_r = S[:, :, 0:4 * KEYS]

            def shift(n, i):
                pr = probs[:, i, :, :]
                st = stat[:, i, :]
                dve.wait_ge(scores_ready, n + 1)
                grouped = pr.rearrange("p (b h) s -> p b h s", b=4)
                by_bank = st.rearrange("p (b h) -> p b h", b=4)
                if final_layer:
                    value = scores_r.rearrange("p b (h s) -> p b h s", s=KEYS)
                    vv.tensor_copy(keep_now[:, i:i + 1], keep[:, pieces(n)])
                else:
                    value = grouped
                    vv.tensor_scalar(pr.rearrange("p (b h) s -> p b (h s)", b=4), scores_r, CLAMP / SCALE,
                                     -CLAMP / SCALE, ALU.min, ALU.max).then_inc(scores_read, 1)
                    dve.drain()
                vv.tensor_reduce(by_bank, value, AX.X, ALU.max)
                dve.drain()
                last = vv.tensor_tensor(grouped, value, by_bank.unsqueeze(3).to_broadcast([P, 4, 4, KEYS]),
                                        ALU.subtract)
                last.then_inc(shifted, 1)
                if final_layer:
                    dve.wait_ge(shifted, n + 1)
                    dve.sem_inc(scores_read, 1)

            def add_projected(t):
                dve.wait_ge(out_ready, t + 1)
                vv.tensor_tensor(branch[:, :], KV[:, DIM:2 * DIM], bo[:, :], ALU.add).then_inc(out_done, 1)
                add_to_residual(nc, c, dve, branch[:, :].unsqueeze(1), [t], layer)

            def body(b, u, first, final):
                for i in range(TPB):
                    n = b * TPB + i
                    if not (final and i == 1):
                        shift(n + 1, 1 - i)
                    st = stat[:, i, :]
                    dve.wait_ge(values_ready, n + 1)
                    values = Q[:, 0:HEADS * (DH + 1)].rearrange("p (h d) -> p h d", d=DH + 1)
                    mixed_ps = values[:, :, 0:DH]
                    vv.reciprocal(st, values[:, :, DH])
                    dve.drain()
                    portion = st.unsqueeze(2).to_broadcast([P, HEADS, DH])
                    if final_layer:
                        vv.tensor_tensor(branch[:, :].rearrange("p (h d) -> p h d", d=DH), mixed_ps, portion,
                                         ALU.mult).then_inc(values_read, 1)
                        add_to_residual(nc, c, dve, branch[:, :].unsqueeze(1), [n], layer)
                    else:
                        vv.tensor_tensor(mixed[:, :].rearrange("p (h d) -> p h d", d=DH), mixed_ps, portion, ALU.mult)\
                          .then_inc(values_read, 1)
                        dve.drain()
                        vv.tensor_tensor(mixed[:, :], mixed[:, :], bv[:, :], ALU.add).then_inc(mixed_done, 1)
                        if not (first and i == 0):
                            add_projected(n - 1)

            shift(0, 0)
            batches(dve, body)
            if not final_layer:
                add_projected(TILES - 1)


def adapter_layer(nc, c, a):
    E, H = 8, 64
    PAIR = P // H
    M = E // PAIR
    with ExitStack() as ctx:
        sb, ps, sem = sub_memory(nc, ctx, "f2_")
        w_base = sb("w_base", [P, DK, DIM])
        w_in = sb("w_in", [P, 2, DK, E, H])
        w_out = sb("w_out", [P, 2, M, DIM])
        b_in = sb("b_in", [P, 2, M])
        b_recon = sb("b_recon", [P, E, DK])
        b_base = sb("b_base", [P, DIM])
        b_up = sb("b_up", [E, DIM])
        hidden = sb("hidden", [P, 2, M, BLOCK])
        diff = sb("diff", [P, 2, BLOCK])
        losses = sb("losses", [P, BATCH, E * DK])
        loss = sb("loss", [P, BATCH, E])
        least = sb("least", [P, BATCH])
        pick = sb("pick", [P, BATCH, E])
        pick_rows = sb("pick_rows", [E, BATCH])
        pick_wide = sb("pick_wide", [E, BATCH, P])
        scale = sb("scale", [P, M, BATCH])
        shift = sb("shift", [P, M, BATCH])
        ones = sb("ones", [P, P])
        hid_ps = [ps(f"hid{i}", [P, BLOCK]) for i in range(2)]
        rec_ps = [ps(f"rec{i}", [P, BLOCK]) for i in range(2)]
        out_ps = [ps(f"out{i}", [P, BLOCK]) for i in range(2)]
        branch = sb("branch", [P, DIM])
        loss_ps = ps("loss_ps", [P, BATCH, E * DK])
        norm = Normalisation(nc, c, ctx, turned=[out_ps[u][:, :] for u in range(2)])
        loaded = sem("loaded")
        hid_ready, hid_done = sem("hid_ready"), sem("hid_done")
        rec_ready, rec_free = sem("rec_ready"), sem("rec_free")
        squared = sem("squared")
        ones_ready, loss_ready, picked = sem("ones_ready"), sem("loss_ready"), sem("picked")
        out_ready, out_done = sem("out_ready"), sem("out_done")
        block = ctx.enter_context(nc.Block())
        SB = BLOCK // SEQ
        RECS = E * DK

        @block.sync
        def _(sp):
            with nc.allow_non_contiguous_dma("small biases"):
                for n, w in enumerate(("L2_ffn_Wd1", "L2_ffn_Wa_down")):
                    for kk in range(DK):
                        sp.dma_start(w_in[:, n, kk, :, :],
                                     a[w][:, kk * P:(kk + 1) * P, :].rearrange("e p h -> p e h")).then_inc(loaded, 16)
                for n, w in enumerate(("L2_ffn_Wd2", "L2_ffn_Wa_up")):
                    sp.dma_start(w_out[:, n, :, :], a[w].rearrange("(m a) h d -> (a h) m d", a=PAIR))\
                      .then_inc(loaded, 16)
                sp.dma_start(b_in[:, 0, :], a["L2_bd1"]).then_inc(loaded, 16)
                sp.dma_start(b_in[:, 1, :], a["L2_ba_down"]).then_inc(loaded, 16)
                sp.dma_start(b_recon[:, :, :], a["L2_bd2"]).then_inc(loaded, 16)
                sp.dma_start(w_base[:, :, :], a["L2_ffn_W_base"].rearrange("(k p) n -> p k n", p=P)).then_inc(loaded, 16)
                sp.dma_start(b_base[:, :], spread(a["L2_ffn_b_base"])).then_inc(loaded, 16)
                sp.dma_start(b_up[:, :], a["L2_ffn_ba_up"]).then_inc(loaded, 16)
        LOADS = 12 * 16

        @block.tensor
        def _(pe):
            def hidden_block(g, u, which, columns):
                n = g * 2 + (u + which * BLOCKS)
                for m in range(M):
                    pe.wait_ge(hid_done, n * M + (m + 1))
                    for kk in range(DK):
                        last = nc.tensor.matmul(hid_ps[m % 2][:, :],
                                                w_in[:, which, kk, m * PAIR:(m + 1) * PAIR, :]
                                                .rearrange("p e h -> p (e h)"),
                                                c.XT[:, kk, columns], start=kk == 0, stop=kk == DK - 1)
                    last.then_inc(hid_ready, 1)

            norm.turn(pe)
            norm.wait_turned(pe)
            pe.wait_ge(loaded, LOADS)
            with pe.Fori(0, BLOCKS // 2) as g:
                for u in range(2):
                    hidden_block(g, u, 0, pieces(g * (2 * BLOCK) + u * BLOCK, BLOCK))
                    pe.wait_ge(hid_done, g * (2 * M) + (u * M + M + 2))
                    for e in range(E):
                        rows = slice((e % PAIR) * H, (e % PAIR + 1) * H)
                        for m in range(DK):
                            r = e * DK + m
                            pe.wait_ge(rec_free, g * (2 * RECS) + (u * RECS + r + 1))
                            nc.tensor.matmul(rec_ps[r % 2][:, :], w_out[rows, 0, e // PAIR, m * P:(m + 1) * P],
                                             hidden[rows, u, e // PAIR, :], start=True, stop=True)\
                              .then_inc(rec_ready, 1)
            pe.wait_ge(squared, BLOCKS * RECS + 2)
            pe.wait_ge(ones_ready, 1)
            nc.tensor.matmul(loss_ps[:, :, :].rearrange("p b r -> p (b r)"), ones[:, :],
                             losses[:, :, :].rearrange("p b r -> p (b r)"), start=True, stop=True)\
              .then_inc(loss_ready, 1)
            pe.wait_ge(picked, 1)
            for blk in range(BLOCKS):
                hidden_block(blk // 2, blk % 2, 1, slice(blk * BLOCK, (blk + 1) * BLOCK))
                pe.wait_ge(hid_done, (BLOCKS + blk + 1) * M + 2)
                for i in range(TPK):
                    t = blk * TPK + i
                    pe.wait_ge(out_done, t + 1)
                    o = out_ps[t % 2][:, 0:DIM]
                    for kk in range(DK):
                        nc.tensor.matmul(o, c.XT[:, kk, t * P:(t + 1) * P], w_base[:, kk, :], start=kk == 0, stop=False)
                    for m in range(M):
                        nc.tensor.matmul(o, hidden[:, blk % 2, m, i * P:(i + 1) * P], w_out[:, 1, m, :], start=False,
                                         stop=False)
                    nc.tensor.matmul(o, pick_wide[:, t // TPB, :], b_up[:, :], start=False, stop=True)\
                      .then_inc(out_ready, 1)

        @block.scalar
        def _(act):
            act.sem_inc(hid_done, 2)
            act.sem_inc(squared, 2)
            norm.root(act)
            norm.copy(act)
            act.wait_ge(loaded, LOADS)
            with act.Fori(0, BLOCKS // 2) as g:
                for u in range(2):
                    for m in range(M):
                        act.wait_ge(hid_ready, g * (2 * M) + (u * M + m + 1))
                        nc.scalar.activation(hidden[:, u, m, :], hid_ps[m % 2][:, :], ACT.Relu,
                                             bias=b_in[:, 0, m:m + 1]).then_inc(hid_done, 1)
                    for r in range(RECS):
                        act.wait_ge(rec_free, g * (2 * RECS) + (u * RECS + r + 3))
                        for s in range(SB):
                            b = g * (2 * SB) + (u * SB + s)
                            last = nc.scalar.activation(diff[:, r % 2, s * SEQ:(s + 1) * SEQ],
                                                        diff[:, r % 2, s * SEQ:(s + 1) * SEQ], ACT.Square,
                                                        accum_out=losses[:, pieces(b), r])
                        last.then_inc(squared, 1)
            act.wait_ge(picked, 1)
            for blk in range(BLOCKS):
                if blk >= 2:
                    act.wait_ge(out_ready, (blk - 1) * TPK)
                for m in range(M):
                    act.wait_ge(hid_ready, (BLOCKS + blk) * M + m + 1)
                    for s in range(SB):
                        b = blk * SB + s
                        cols = slice(s * SEQ, (s + 1) * SEQ)
                        last = nc.scalar.activation(hidden[:, blk % 2, m, cols], hid_ps[m % 2][:, cols], ACT.Relu,
                                                    bias=shift[:, m, b:b + 1], scale=scale[:, m, b:b + 1])
                    last.then_inc(hid_done, 1)

        @block.vector
        def _(dve):
            v = nc.vector
            dve.sem_inc(rec_free, 2)
            dve.sem_inc(out_done, 2)
            v.memset(ones[:, :], 1.0).then_inc(ones_ready, 1)
            norm.statistics(dve)
            norm.apply(dve)
            dve.wait_ge(loaded, LOADS)
            with dve.Fori(0, BLOCKS // 2) as g:
                for u in range(2):
                    columns = pieces(g * (2 * BLOCK) + u * BLOCK, BLOCK)
                    for e in range(E):
                        for m in range(DK):
                            r = e * DK + m
                            dve.wait_ge(rec_ready, g * (2 * RECS) + (u * RECS + r + 1))
                            dve.wait_ge(squared, g * (2 * RECS) + (u * RECS + r + 1))
                            v.scalar_tensor_tensor(diff[:, r % 2, :], rec_ps[r % 2][:, :], b_recon[:, e, m:m + 1],
                                                   c.XT[:, m, columns], ALU.add, ALU.subtract).then_inc(rec_free, 1)
            dve.wait_ge(loss_ready, 1)
            wide = [P, BATCH, E]

            def tt(*args):
                v.tensor_tensor(*args)
                dve.drain()

            v.tensor_reduce(loss[:, :, :], loss_ps[:, :, :].rearrange("p b (e m) -> p b e m", m=DK), AX.X, ALU.add)
            dve.drain()
            v.tensor_reduce(least[:, :], loss[:, :, :], AX.X, ALU.min)
            dve.drain()
            iota = c.iota[:, 0:E].unsqueeze(1).to_broadcast(wide)
            tt(pick[:, :, :], loss[:, :, :], least[:, :].unsqueeze(2).to_broadcast(wide), ALU.is_gt)
            v.scalar_tensor_tensor(pick[:, :, :], pick[:, :, :], float(E), iota, ALU.mult, ALU.add)
            dve.drain()
            v.tensor_reduce(least[:, :], pick[:, :, :], AX.X, ALU.min)
            dve.drain()
            tt(pick[:, :, :], iota, least[:, :].unsqueeze(2).to_broadcast(wide), ALU.is_equal)
            for half in range(PAIR):
                rows = slice(half * H, (half + 1) * H)
                v.tensor_copy(scale[rows, :, :], pick[rows, :, half:E:PAIR].rearrange("p b m -> p m b"))
            dve.drain()
            tt(shift[:, :, :], scale[:, :, :], b_in[:, 1, :].unsqueeze(2).to_broadcast([P, M, BATCH]), ALU.mult)
            tt(loss[0:E, :, :], pick[0:E, :, :], c.ident[0:E, 0:E].unsqueeze(1).to_broadcast([E, BATCH, E]), ALU.mult)
            v.tensor_reduce(pick_rows[:, :], loss[0:E, :, :], AX.X, ALU.add)
            dve.drain()
            v.tensor_copy(pick_wide[:, :, :], pick_rows[:, :].unsqueeze(2).to_broadcast([E, BATCH, P]))
            dve.drain()
            dve.sem_inc(picked, 1)
            for t in range(TILES):
                dve.wait_ge(out_ready, t + 1)
                v.tensor_tensor(branch[:, :], out_ps[t % 2][:, 0:DIM], b_base[:, :], ALU.add).then_inc(out_done, 1)
                add_to_residual(nc, c, dve, branch[:, :].unsqueeze(1), [t], 6)
            dve.drain()


def state_space_kernel(nc, c, a, KA, KB, KC, X2):
    N, J, S = 64, 128, 16
    CH = 16
    CHUNKS = J // CH
    TWO_PI = 2 * np.pi
    C1 = 6.28125
    C2 = float(np.float32(TWO_PI - C1) .view(np.int32).__and__(-4096).view(np.float32))
    C3 = float(TWO_PI - C1 - C2)
    LN2_HI = 0.693359375
    LN2_LO = float(np.log(2.0) - LN2_HI)
    with ExitStack() as ctx:
        sb, ps, sem = sub_memory(nc, ctx, "ss_")
        small = {n: sb(n, [P, J]) for n in ("are", "aim", "cre", "cim", "ldt", "dt", "theta", "rho", "er", "ei",
                                            "t0", "t1", "t2", "dcr", "dci", "cos0", "sin0")}
        gates = sb("gates", [P, 8])
        bits = sb("bits", [P, J], I32)
        steps = sb("steps", [P, 2 * S])
        big = {n: sb(n, [P, J, S]) for n in ("qr", "qi", "w")}
        halves = [t[:, :, :].rearrange("p t d -> p (t d)")[:, h * J * S:(h + 1) * J * S]
                  for t in (c.XN, c.XT, c.ACC, X2) for h in range(2)]
        for n, part in zip(("phase_q", "turns", "mag_q", "pr", "pi", "u", "phase_p", "mag_p"), halves):
            big[n] = part.rearrange("p (j s) -> p j s", s=S)
        slot = sb("slot", [P, 2, 4, CH, S])
        d_skip = sb("d_skip", [1, DIM])
        k_sb = sb("k_sb", [S, S, DIM])
        k_rows = sb("k_rows", [P, TPB, DIM])
        fwd = sb("fwd", [P, TPB, 2 * SEQ])
        k_ps = [[ps(f"k{u}{h}", [S, CH, S]) for h in range(2)] for u in range(2)]
        f_banks = [ps(f"f{i}", [P, 2, DIM]) for i in range(2)]
        f_ps = [bank[:, h, :] for bank in f_banks for h in range(2)]
        loaded, asked, answered = sem("loaded"), sem("asked"), sem("answered")
        slot_ready, k_ready, k_free = sem("slot_ready"), sem("k_ready"), sem("k_free")
        k_stored, k_rows_loaded = sem("k_stored"), sem("k_rows_loaded")
        k_rows_dram = nc.dram_tensor("state_space_kernel", (SEQ, DIM), F32, kind="Internal").ap()
        fwd_loaded, inputs_loaded = sem("fwd_loaded"), sem("inputs_loaded")
        rho_ready, scaled = sem("rho_ready"), sem("scaled")
        k_whole, f_ready, begun = sem("k_whole"), sem("f_ready"), sem("begun")
        first = ExitStack()
        block = first.enter_context(nc.Block())

        @block.sync
        def _(sp):
            for n, k in (("are", "A_re"), ("aim", "A_im"), ("cre", "C_re"), ("cim", "C_im")):
                sp.dma_start(small[n][:, :], a["S_" + k]).then_inc(loaded, 16)
            for h in range(2):
                sp.dma_start(small["ldt"][h * N:(h + 1) * N, :],
                             a["L0_xattn_log_dt"][h * J:(h + 1) * J].partition_broadcast(N)).then_inc(loaded, 16)
            sp.dma_start(steps[:, :], a["steps"]).then_inc(loaded, 16)
            sp.dma_start(d_skip[:, :], row(a["L0_xattn_D_skip"])).then_inc(loaded, 16)
            sp.dma_start(fwd[:, :, :], a["fwd"].rearrange("(i p) f -> p i f", p=P)).then_inc(fwd_loaded, 16)
            load_inputs(c, a, sp, gates, inputs_loaded)

        @block.vector
        def _(dve):
            v = nc.vector

            def tt(*args):
                v.tensor_tensor(*args)
                dve.drain()

            def ts(*args):
                v.tensor_scalar(*args)
                dve.drain()

            def stt(*args):
                v.scalar_tensor_tensor(*args)
                dve.drain()

            def ask(n, done):
                dve.sem_inc(asked, 1)
                dve.wait_ge(answered, done)

            def reduce_angle(x, k):
                ts(k, x, 1.0 / TWO_PI, MAGIC, ALU.mult, ALU.add)
                ts(k, k, MAGIC, None, ALU.subtract)
                for part in (C1, C2, C3):
                    stt(x, k, -part, x, ALU.mult, ALU.add)
                ts(x, x, 3.1415925, -3.1415925, ALU.min, ALU.max)

            m = {n: t[:, :] for n, t in small.items()}
            dve.wait_ge(loaded, 8 * 16)
            ts(m["t0"], m["ldt"], float(1 / np.log(2.0)), MAGIC, ALU.mult, ALU.add)
            ts(m["t0"], m["t0"], MAGIC, -126.0, ALU.subtract, ALU.max)
            stt(m["t1"], m["t0"], -LN2_HI, m["ldt"], ALU.mult, ALU.add)
            stt(m["t1"], m["t0"], -LN2_LO, m["t1"], ALU.mult, ALU.add)
            coefs = [1.0 / 5040, 1.0 / 720, 1.0 / 120, 1.0 / 24, 1.0 / 6, 0.5, 1.0]
            ts(m["t2"], m["t1"], coefs[0], None, ALU.mult)
            for co in coefs[1:]:
                stt(m["t2"], m["t2"], co, m["t1"], ALU.add, ALU.mult)
            ts(bits[:, :], m["t0"], 127.0, 8388608.0, ALU.add, ALU.mult)
            stt(m["dt"], m["t2"], 1.0, bits[:, :].bitcast(F32), ALU.add, ALU.mult)
            tt(m["theta"], m["dt"], m["aim"], ALU.mult)
            tt(m["rho"], m["dt"], m["are"], ALU.mult)
            dve.sem_inc(rho_ready, 1)
            v.tensor_copy(m["t0"], m["theta"])
            dve.drain()
            reduce_angle(m["t0"], m["t1"])
            ask(1, 3)
            tt(m["cos0"], m["cos0"], m["cos0"], ALU.mult)
            ts(m["t1"], m["t0"], -1.0, 1.0, ALU.mult, ALU.add)
            v.reciprocal(m["t1"], m["t1"])
            dve.drain()
            stt(m["t0"], m["t0"], 2.0, m["t1"], ALU.mult, ALU.mult)
            ts(m["t1"], m["cos0"], -2.0, None, ALU.mult)
            stt(m["er"], m["t1"], 1.0, m["t0"], ALU.add, ALU.mult)
            tt(m["er"], m["er"], m["t1"], ALU.add)
            stt(m["ei"], m["t0"], 1.0, m["sin0"], ALU.add, ALU.mult)
            tt(m["t0"], m["cre"], m["er"], ALU.mult)
            tt(m["t1"], m["cim"], m["ei"], ALU.mult)
            tt(m["t0"], m["t0"], m["t1"], ALU.subtract)
            tt(m["t1"], m["cre"], m["ei"], ALU.mult)
            tt(m["t2"], m["cim"], m["er"], ALU.mult)
            tt(m["t1"], m["t1"], m["t2"], ALU.add)
            tt(m["er"], m["are"], m["are"], ALU.mult)
            tt(m["ei"], m["aim"], m["aim"], ALU.mult)
            tt(m["er"], m["er"], m["ei"], ALU.add)
            v.reciprocal(m["er"], m["er"])
            dve.drain()
            for out, x, y, op in (("dcr", "t0", "t1", ALU.add), ("dci", "t1", "t0", ALU.subtract)):
                tt(m[out], m[x], m["are"], ALU.mult)
                tt(m["t2"], m[y], m["aim"], ALU.mult)
                tt(m[out], m[out], m["t2"], op)
                stt(m[out], m[out], 2.0, m["er"], ALU.mult, ALU.mult)
            b = {n: t[:, :, :] for n, t in big.items()}
            wide = [P, J, S]
            for f, n in enumerate("qp"):
                at = steps[:, f * S:(f + 1) * S].unsqueeze(1).to_broadcast(wide)
                tt(b["phase_" + n], m["theta"].unsqueeze(2).to_broadcast(wide), at, ALU.mult)
                reduce_angle(b["phase_" + n], b["turns"])
                dve.sem_inc(asked, 1)
            dve.wait_ge(answered, 11)
            ts(b["pr"], b["pr"], -2.0, 1.0, ALU.mult, ALU.add)
            tt(b["pr"], b["pr"], b["mag_p"], ALU.mult)
            tt(b["pi"], b["pi"], b["mag_p"], ALU.mult)
            dcr, dci = (m[n].unsqueeze(2).to_broadcast(wide) for n in ("dcr", "dci"))
            tt(b["u"], b["pr"], dcr, ALU.mult)
            tt(b["w"], b["pi"], dci, ALU.mult)
            tt(b["u"], b["u"], b["w"], ALU.subtract)
            tt(b["pr"], b["pr"], dci, ALU.mult)
            tt(b["pi"], b["pi"], dcr, ALU.mult)
            stt(b["w"], b["pr"], -1.0, b["pi"], ALU.mult, ALU.subtract)
        @block.scalar
        def _(act):
            act.wait_ge(loaded, 8 * 16)
            act.wait_ge(asked, 1)
            s = {n: t[:, :] for n, t in small.items()}
            nc.scalar.activation(s["sin0"], s["t0"], ACT.Sin).then_inc(answered, 1)
            nc.scalar.activation(s["cos0"], s["t0"], ACT.Sin, scale=0.5).then_inc(answered, 1)
            act.wait_ge(answered, 2)
            nc.scalar.activation(s["t0"], s["rho"], ACT.Tanh, scale=0.5).then_inc(answered, 1)
            for f, n in enumerate("qp"):
                act.wait_ge(scaled, f + 1)
                mag, phase, re, im = (big[x][:, :, :] for x in ("mag_" + n, "phase_" + n, n + "r", n + "i"))
                nc.scalar.activation(mag, mag, ACT.Exp).then_inc(answered, 1)
                act.wait_ge(asked, 2 + f)
                nc.scalar.activation(im, phase, ACT.Sin).then_inc(answered, 1)
                nc.scalar.activation(re, phase, ACT.Sin, scale=0.5).then_inc(answered, 1)
                act.wait_ge(answered, 6 + 4 * f)
                nc.scalar.activation(re, re, ACT.Square).then_inc(answered, 1)
            act.wait_ge(inputs_loaded, 8 * 16)
            nc.scalar.activation(c.gate[:, :], gates[:, :], ACT.Tanh).then_inc(answered, 1)
            act.drain()

        @block.gpsimd
        def _(pool):
            def multiply(out, x, y):
                nc.gpsimd.tensor_tensor(out, x, y, ALU.mult)
                pool.drain()

            wide = [P, J, S]
            pool.wait_ge(loaded, 8 * 16)
            pool.wait_ge(rho_ready, 1)
            for f, n in enumerate("qp"):
                multiply(big["mag_" + n][:, :, :], small["rho"][:, :].unsqueeze(2).to_broadcast(wide),
                         steps[:, f * S:(f + 1) * S].unsqueeze(1).to_broadcast(wide))
                pool.sem_inc(scaled, 1)
            re, im, mag = (big[n][:, :, :] for n in ("qr", "qi", "mag_q"))
            pool.wait_ge(answered, 7)
            nc.gpsimd.tensor_scalar(re, re, -2.0, 1.0, ALU.mult, ALU.add)
            pool.drain()
            multiply(re, re, mag)
            multiply(im, im, mag)

        first.close()

        plain = Normalisation(nc, c, ctx, c.X, natural=c.XN)
        shaped = Normalisation(nc, c, ctx, c.XN, natural=X2, transposed=False, gain=a["L0_xattn_g_norm_in"],
                               shift=a["L0_xattn_b_norm_in"])
        block = ctx.enter_context(nc.Block())

        @block.sync
        def _(sp):
            shaped.load(sp)
            sp.wait_ge(k_whole, 1)
            sp.dma_start(k_rows_dram.rearrange("(a b) d -> b a d", b=S), k_sb[:, :, :]).then_inc(k_stored, 16)
            sp.wait_ge(k_stored, 16)
            sp.dma_start(k_rows[:, :, :], k_rows_dram.rearrange("(i p) d -> p i d", p=P)).then_inc(k_rows_loaded, 16)

        @block.gpsimd
        def _(pool):
            pool.sem_inc(k_ready, 2)
            plain.copy_first_tiles(pool)
            with pool.Fori(0, CHUNKS // 2) as g:
                for u in range(2):
                    pool.wait_ge(k_ready, g * 2 + u + 1)
                    for n, x in enumerate(("qr", "qi", "u", "w")):
                        last = nc.gpsimd.tensor_copy(slot[:, u, n, :, :],
                                                     big[x][:, pieces(g * (2 * CH) + u * CH, CH), :])
                    last.then_inc(slot_ready, 1)

        @block.vector
        def _(dve):
            v = nc.vector
            plain.statistics(dve)
            plain.apply(dve)
            plain.wait_natural(dve)
            shaped.statistics(dve)
            shaped.apply(dve)
            dve.wait_ge(k_free, CHUNKS + 2)
            v.tensor_tensor(k_sb[0:1, 0, :], k_sb[0:1, 0, :], d_skip[:, :], ALU.add).then_inc(k_whole, 1)
            dve.wait_ge(f_ready, 4)
            for h in range(2):
                v.tensor_copy(KA[:, h, :], f_ps[h])
                v.tensor_copy(KC[:, h, :], f_ps[h])
                v.tensor_copy(KB[:, h, :], f_ps[2 + h])
            dve.drain()
            v.tensor_copy(KC[0:1, 0, :], f_ps[2][0:1, :])
            v.memset(KB[0:1, 0, :], 0.0)
            dve.drain()

        @block.scalar
        def _(act):
            act.sem_inc(k_free, 2)
            plain.root(act)
            plain.copy(act)
            shaped.root(act)
            with act.Fori(0, CHUNKS // 2) as g:
                for u in range(2):
                    act.wait_ge(k_ready, g * 2 + u + 3)
                    for h in range(2):
                        last = nc.scalar.activation(k_sb[:, :, pieces(g * (2 * CH) + (u * CH + h * J), CH)],
                                                    k_ps[u][h][:, :, :].rearrange("b j a -> b a j"), ACT.Copy)
                    last.then_inc(k_free, 1)

        @block.tensor
        def _(pe):
            plain.turn(pe)
            with pe.Fori(0, CHUNKS // 2) as g:
                for u in range(2):
                    pe.wait_ge(slot_ready, g * 2 + u + 1)
                    pe.wait_ge(k_free, g * 2 + u + 1)
                    pe.sem_inc(begun, 1)
                    for j in range(CH):
                        for h in range(2):
                            r = slice(h * N, (h + 1) * N)
                            nc.tensor.matmul(k_ps[u][h][:, j, :], slot[r, u, 0, j, :], slot[r, u, 2, j, :],
                                             start=True, stop=False)
                            last = nc.tensor.matmul(k_ps[u][h][:, j, :], slot[r, u, 1, j, :], slot[r, u, 3, j, :],
                                                    start=False, stop=True)
                    last.then_inc(k_ready, 1)
            pe.wait_ge(k_rows_loaded, 16)
            pe.wait_ge(fwd_loaded, 16)
            for f in range(4):
                for i in range(TPB):
                    last = nc.tensor.matmul(f_ps[f], fwd[:, i, f * P:(f + 1) * P], k_rows[:, i, :],
                                            start=i == 0, stop=i == TPB - 1)
                last.then_inc(f_ready, 1)


def film_attention(nc, c, a, X2, FO, table):
    HEADS, DH, TOP = 4, 32, 32
    SCALE = float(1.0 / np.sqrt(np.float32(DH)))
    K_AT = SEQ
    V_AT = K_AT + KEYS
    with ExitStack() as ctx:
        sb, ps, sem = sub_memory(nc, ctx, "a0_")
        wq = sb("wq", [P, DK, P])
        wk = sb("wk", [CP, CK, P])
        wv = sb("wv", [CP, CK, DIM])
        wf = sb("wf", [P, 2, DK, 2 * DIM])
        bf = sb("bf", [1, 2, 2 * DIM])
        mod = sb("mod", [P, 1])
        context = sb("context", [CP, 2, CK, KEYS])
        mask8 = sb("mask8", [P, TILES], U8)
        share = sb("share", [P, TILES])
        key_mask8 = sb("key_mask8", [P, BATCH, KEYS], U8)
        key_fill = sb("key_fill", [P, BATCH, KEYS])
        q = sb("q", [P, SEQ])
        k = sb("k", [P, KEYS])
        v_t = sb("v_t", [P, DK, KEYS])
        k_wide = sb("k_wide", [P, HEADS, KEYS])
        vf = sb("vf", [KEYS + 1, BATCH, 4 * DIM])
        score = sb("score", [P, 2, TPB, HEADS, KEYS])
        rest = sb("rest", [P, 2, TPB, HEADS, KEYS])
        top = sb("top", [P, TPB, HEADS, 8])
        top_n = sb("top_n", [P, TPB, HEADS, 8])
        stat = sb("stat", [P, TPB, HEADS])
        mean = sb("mean", [P, 2, TPB, KEYS])
        mean_t = sb("mean_t", [KEYS + 1, SEQ])
        QKV = ps("qkv_ps", [P, 512])
        S = [ps(f"s{i}", [P, HEADS * KEYS]) for i in range(TPB)]
        T = ps("t", [KEYS, SEQ])
        V = ps("vf_ps", [KEYS, 2 * DIM])
        F_IN = [ps(f"f_in{i}", [P, 2 * DIM]) for i in range(TPB)]
        F_OUT = ps("f_out", [P, 2 * DIM])
        qkv_loaded = sem("qkv_loaded")
        w_loaded, rows_loaded = sem("w_loaded"), sem("rows_loaded")
        ctx_loaded = [sem(f"ctx_loaded{u}") for u in range(2)]
        setup_done = sem("setup_done")
        qkv_ready, qkv_done, k_wide_ready = sem("qkv_ready"), sem("qkv_done"), sem("k_wide_ready")
        vf_ready, vf_done = sem("vf_ready"), sem("vf_done")
        scores_ready, scores_read = sem("scores_ready"), sem("scores_read")
        shifted, exp_done = sem("shifted"), sem("exp_done")
        mean_ready, turned, turned_done = sem("mean_ready"), sem("turned"), sem("turned_done")
        film_in_ready, film_in_read = sem("film_in_ready"), sem("film_in_read")
        film_out_ready, film_out_read = sem("film_out_ready"), sem("film_out_read")
        zero_ready, zero_stored = sem("zero_ready"), c.transfers["zeros"]
        block = ctx.enter_context(nc.Block())
        LOADS = 16 * 7


        def steps(eng, body):
            body(0, 0)
            with eng.Fori(0, 2) as g:
                for u in (1, 0):
                    body(g * 2 + (2 - u), u, first=False)
            body(5, 1, first=False)
            body(6, 0, first=False, two_left=False)
            body(7, 1, first=False, two_left=False, one_left=False)

        @block.sync
        def _(sp):
            def load(b, u):
                sp.dma_start(context[:, u, :, :].unsqueeze(1),
                             a["context_T"][pieces(b), :, :].rearrange("b (k p) s -> p b k s", p=CP))\
                  .then_inc(ctx_loaded[u], 16)

            load(0, 0)
            load(1, 1)
            for dst, src, p in ((wq, "Wq", P), (wk, "Wk", CP), (wv, "Wv", CP)):
                sp.dma_start(dst[:, :, :], a["L0_xattn_" + src].rearrange("(k p) n -> p k n", p=p)).then_inc(qkv_loaded, 16)
            sp.dma_start(mod[:, :], spread(a["L0_xattn_mod_gate"])).then_inc(w_loaded, 16)
            sp.dma_start(mask8[:, :], a["mask_BxS_bf1"]).then_inc(w_loaded, 16)
            sp.dma_start(key_mask8[:, :, :], a["mask_BxS2_bf1"].partition_broadcast(P)).then_inc(w_loaded, 16)
            for n, way in enumerate(("in", "out")):
                sp.dma_start(wf[:, n, :, :], a["L0_xattn_W_film_" + way].rearrange("(k p) n -> p k n", p=P))\
                  .then_inc(w_loaded, 16)
                sp.dma_start(bf[:, n, :], row(a["L0_xattn_b_film_" + way])).then_inc(w_loaded, 16)
            sp.dma_start(mean_t[KEYS:KEYS + 1, :], row(a["ones"][0:2, :].rearrange("a b -> (a b)")))\
              .then_inc(rows_loaded, 16)
            sp.wait_ge(setup_done, 1)
            for b in range(BATCH):
                sp.dma_start(vf[KEYS:KEYS + 1, b, :], bf[:, :, :].rearrange("p w n -> p (w n)"))\
                  .then_inc(rows_loaded, 16)
            with sp.Fori(1, BATCH // 2) as g:
                for u in range(2):
                    sp.wait_ge(qkv_ready, g * 2 + (u - 1))
                    load(g * 2 + u, u)

        @block.gpsimd
        def _(pool):
            def widen(b):
                wide = [P, HEADS, KEYS]
                pool.wait_ge(qkv_done, b + 1)
                nc.gpsimd.tensor_tensor(k_wide[:, :, :], k[:, :].unsqueeze(1).to_broadcast(wide),
                                        c.headmask[:, 0:HEADS].unsqueeze(2).to_broadcast(wide), ALU.mult)\
                  .then_inc(k_wide_ready, 1)

            def body(b, u, first=True, two_left=True, one_left=True):
                if two_left:
                    widen(b + 2)

            widen(0)
            widen(1)
            nc.gpsimd.memset(c.ACC[:, 0:8, :], 0.0).then_inc(zero_ready, 1)
            pool.wait_ge(zero_ready, 1)
            pool.wait_ge(setup_done, 1)
            rows, step = table.shape[0], 8 * P
            for r in range(0, rows, step):
                n = min(step, rows - r) // P
                pool.dma_start(table[r:r + n * P, :].rearrange("(i p) d -> p i d", p=P), c.ACC[:, 0:n, :])\
                  .then_inc(zero_stored.sem, 16)
            steps(pool, body)
            pool.wait_ge(zero_stored.sem, zero_stored.expect(-(-rows // step)))

        @block.tensor
        def _(pe):
            def scores(b):
                pe.wait_ge(k_wide_ready, b + 1)
                pe.wait_ge(qkv_done, b + 1)
                pe.wait_ge(scores_read, b + 1)
                for i in range(TPB):
                    last = nc.tensor.matmul(S[i][:, :], q[:, i * P:(i + 1) * P],
                                            k_wide[:, :, :].rearrange("p h s -> p (h s)"), start=True, stop=True)
                last.then_inc(scores_ready, 1)

            def project(b, u):
                for kk in range(DK):
                    nc.tensor.matmul(QKV[:, 0:SEQ], wq[:, kk, :], c.XT[:, kk, pieces(b * SEQ, SEQ)], start=kk == 0,
                                     stop=kk == DK - 1)
                pe.wait_ge(ctx_loaded[u], b * 8 + (16 - 8 * u))
                for kk in range(CK):
                    nc.tensor.matmul(QKV[:, K_AT:V_AT], wk[:, kk, :], context[:, u, kk, :], start=kk == 0,
                                     stop=kk == CK - 1)
                for m in range(DK):
                    for kk in range(CK):
                        last = nc.tensor.matmul(QKV[:, V_AT + m * KEYS:V_AT + (m + 1) * KEYS],
                                                wv[:, kk, m * P:(m + 1) * P], context[:, u, kk, :],
                                                start=kk == 0, stop=kk == CK - 1)
                last.then_inc(qkv_ready, 1)

            def project_values(b):
                pe.wait_ge(qkv_done, b + 1)
                for way in range(2):
                    pe.wait_ge(vf_done, b * 2 + (way + 1))
                    for m in range(DK):
                        last = nc.tensor.matmul(V[:, :], v_t[:, m, :], wf[:, way, m, :], start=m == 0,
                                                stop=m == DK - 1)
                    last.then_inc(vf_ready, 1)

            def film(b, u):
                pe.wait_ge(mean_ready, b + 1)
                for i in range(TPB):
                    last = nc.tensor.transpose(T[:, i * P:(i + 1) * P], mean[:, u, i, :], c.ident[:, :])
                last.then_inc(turned, 1)
                pe.wait_ge(turned_done, b + 1)
                pe.wait_ge(vf_done, b * 2 + 3)
                for way in range(2):
                    if way == 0:
                        pe.wait_ge(film_in_read, b + 1)
                    for i in range(TPB):
                        if way == 1:
                            pe.wait_ge(film_out_read, b * TPB + (i + 1))
                        out = F_OUT if way else F_IN[i]
                        last = nc.tensor.matmul(out[:, :].unsqueeze(1), mean_t[:, i * P:(i + 1) * P],
                                                vf[:, pieces(b), way * 2 * DIM:(way + 1) * 2 * DIM],
                                                start=True, stop=True)
                        if way == 1:
                            last.then_inc(film_out_ready, 1)
                    if way == 0:
                        last.then_inc(film_in_ready, 1)

            def body(b, u, first=True, two_left=True, one_left=True):
                if one_left:
                    scores(b + 1)
                if two_left:
                    project(b + 2, u)
                if not first:
                    film(b - 1, 1 - u)
                if two_left:
                    project_values(b + 2)

            pe.wait_ge(qkv_loaded, 48)
            project(0, 0)
            scores(0)
            pe.wait_ge(setup_done, 1)
            project_values(0)
            project(1, 1)
            project_values(1)
            pe.wait_ge(rows_loaded, 9 * 16)
            steps(pe, body)
            film(BATCH - 1, 1)

        @block.scalar
        def _(act):
            act.sem_inc(vf_done, 1)
            act.sem_inc(film_out_read, 1)

            def copy_qkv(b):
                act.wait_ge(qkv_ready, b + 1)
                nc.scalar.activation(q[:, :], QKV[:, 0:SEQ], ACT.Copy)
                nc.scalar.activation(k[:, :], QKV[:, K_AT:V_AT], ACT.Copy)
                nc.scalar.activation(v_t[:, :, :].rearrange("p m s -> p (m s)"), QKV[:, V_AT:V_AT + DK * KEYS],
                                     ACT.Copy).then_inc(qkv_done, 1)

            def copy_values(b):
                for way in range(2):
                    act.wait_ge(vf_ready, b * 2 + (way + 1))
                    nc.scalar.activation(vf[0:KEYS, pieces(b), way * 2 * DIM:(way + 1) * 2 * DIM],
                                         V[:, :].unsqueeze(1), ACT.Copy).then_inc(vf_done, 1)

            def exp(b, u):
                act.wait_ge(shifted, b + 1)
                nc.scalar.activation(score[:, u, :, :, :], score[:, u, :, :, :], ACT.Exp).then_inc(exp_done, 1)

            def copy_film(b):
                act.wait_ge(turned, b + 1)
                nc.scalar.activation(mean_t[0:KEYS, :], T[:, :], ACT.Copy).then_inc(turned_done, 1)
                for i in range(TPB):
                    act.wait_ge(film_out_ready, b * TPB + (i + 1))
                    nc.scalar.activation(FO[:, pieces(b * TPB + i), :], F_OUT[:, :].unsqueeze(1), ACT.Copy)\
                      .then_inc(film_out_read, 1)

            def body(b, u, first=True, two_left=True, one_left=True):
                if two_left:
                    copy_qkv(b + 2)
                if not first:
                    copy_film(b - 1)
                if two_left:
                    copy_values(b + 2)
                if one_left:
                    exp(b + 1, 1 - u)

            for b in range(2):
                copy_qkv(b)
                copy_values(b)
            exp(0, 0)
            steps(act, body)
            copy_film(BATCH - 1)

        @block.vector
        def _(dve):
            vv = nc.vector
            dve.sem_inc(scores_read, 1)
            dve.sem_inc(film_in_read, 1)
            dve.wait_ge(w_loaded, LOADS)
            vv.tensor_scalar(wf[:, :, :, :].rearrange("p w k n -> p (w k n)"),
                             wf[:, :, :, :].rearrange("p w k n -> p (w k n)"), mod[:, 0:1], None, ALU.mult)
            vv.tensor_scalar(bf[:, :, :], bf[:, :, :], mod[0:1, 0:1], None, ALU.mult)
            vv.tensor_copy(share[:, :], mask8[:, :])
            vv.tensor_copy(key_fill[:, :, :], key_mask8[:, :, :])
            dve.drain()
            vv.tensor_scalar(bf[:, :, 0:DIM], bf[:, :, 0:DIM], 1.0, None, ALU.add)
            vv.tensor_scalar(share[:, :], share[:, :], 1.0 / HEADS, None, ALU.mult)
            vv.tensor_scalar(key_fill[:, :, :], key_fill[:, :, :], 1.0, 1.0e30, ALU.subtract, ALU.mult)
            dve.drain()
            dve.sem_inc(setup_done, 1)

            def largest(b, u):
                dve.drain()
                dve.wait_ge(scores_ready, b + 1)
                fill = key_fill[:, pieces(b), :].to_broadcast([P, HEADS, KEYS])
                for i in range(TPB):
                    last = vv.scalar_tensor_tensor(score[:, u, i, :, :],
                                                   S[i][:, :].rearrange("p (h s) -> p h s", s=KEYS),
                                                   SCALE, fill, ALU.mult, ALU.add)
                last.then_inc(scores_read, 1)
                dve.drain()
                for r in range(TOP // 8):
                    src, t8 = (score, top) if r == 0 else (rest, top_n)
                    for i in range(TPB):
                        for h in range(HEADS):
                            vv.max(t8[:, i, h, :], src[:, u, i, h, :])
                    dve.drain()
                    for i in range(TPB):
                        for h in range(HEADS):
                            vv.match_replace(rest[:, u, i, h, :], t8[:, i, h, :], src[:, u, i, h, :], NEG)
                    dve.drain()
                s3 = score[:, u, :, :, :].rearrange("p i h s -> p (i h) s")
                vv.tensor_tensor(s3, s3, top[:, :, :, 0].rearrange("p i h -> p (i h)").unsqueeze(2)
                                 .to_broadcast([P, TPB * HEADS, KEYS]), ALU.subtract).then_inc(shifted, 1)

            def average(b, u):
                s3 = score[:, u, :, :, :].rearrange("p i h s -> p (i h) s")
                s1 = score[:, u, :, :, :].rearrange("p i h s -> p (i h s)")
                st = stat[:, :, :].rearrange("p i h -> p (i h)")
                dve.wait_ge(exp_done, b + 1)
                vv.scalar_tensor_tensor(s1, rest[:, u, :, :, :].rearrange("p i h s -> p (i h s)"), NEG, s1,
                                        ALU.is_equal, ALU.mult)
                dve.drain()
                vv.tensor_reduce(st, s3, AX.X, ALU.add)
                dve.drain()
                vv.reciprocal(st, st)
                dve.drain()
                for i in range(TPB):
                    vv.tensor_scalar(stat[:, i, :], stat[:, i, :], share[:, pieces(b * TPB + i)], None, ALU.mult)
                dve.drain()
                vv.tensor_tensor(s3, s3, st.unsqueeze(2).to_broadcast([P, TPB * HEADS, KEYS]), ALU.mult)
                dve.drain()
                for i in range(TPB):
                    last = vv.tensor_reduce(mean[:, u, i, :], score[:, u, i, :, :].rearrange("p h s -> p s h"),
                                            AX.X, ALU.add)
                last.then_inc(mean_ready, 1)

            def scale_and_shift(b):
                dve.wait_ge(film_in_ready, b + 1)
                for n, op in ((0, ALU.mult), (1, ALU.add)):
                    for i in range(TPB):
                        x = X2[:, pieces(b * TPB + i), :]
                        last = vv.tensor_tensor(x, x, F_IN[i][:, n * DIM:(n + 1) * DIM].unsqueeze(1), op)
                    if n == 0:
                        dve.drain()
                last.then_inc(film_in_read, 1)

            def body(b, u, first=True, two_left=True, one_left=True):
                if one_left:
                    largest(b + 1, 1 - u)
                average(b, u)
                if not first:
                    scale_and_shift(b - 1)

            largest(0, 0)
            steps(dve, body)
            scale_and_shift(BATCH - 1)
            dve.drain()


def convolve(nc, c, a, X2, stats, FO, KA, KB, KC):
    PAIRS = BATCH // 2
    TPP = 2 * TPB
    with ExitStack() as ctx:
        sb, ps, sem = sub_memory(nc, ctx, "cv_")
        fwd = sb("fwd", [P, TPB, 2 * SEQ])
        back = sb("back", [P, 4, SEQ])
        prod = sb("prod", [P, 2, 4, 2 * DIM])
        spec = sb("spec", [P, 2, 2, 2 * DIM])
        y = sb("y", [P, TPP, DIM])
        f_ps = [[ps(f"f{part}{h}", [P, 2, DIM]) for h in range(2)] for part in range(2)]
        y_ps = [ps(f"y{i}", [P, 2, DIM]) for i in range(TPB)]
        loaded, f_ready, f_done = sem("loaded"), sem("f_ready"), sem("f_done")
        prod_free, spec_ready = sem("prod_free"), sem("spec_ready")
        y_ready, y_done = sem("y_ready"), sem("y_done")
        block = ctx.enter_context(nc.Block())

        @block.sync
        def _(sp):
            sp.dma_start(fwd[:, :, :], a["fwd"].rearrange("(i p) f -> p i f", p=P)).then_inc(loaded, 16)
            sp.dma_start(back[:, :, :], a["back"].rearrange("(i p) l -> p i l", p=P)).then_inc(loaded, 16)

        def pairs(eng, body):
            with eng.Fori(0, PAIRS - 1) as g:
                body(g, False)
            body(PAIRS - 1, True)

        @block.tensor
        def _(pe):
            def forward(g):
                for h in range(2):
                    pe.wait_ge(f_done, g * 2 + h + 1)
                    for part in range(2):
                        for i in range(TPB):
                            col = part * SEQ + h * P
                            last = nc.tensor.matmul(f_ps[part][h][:, :, :], fwd[:, i, col:col + P],
                                                    X2[:, bass.ds(g * TPP + i, 2, TPB), :],
                                                    start=i == 0, stop=i == TPB - 1)
                    last.then_inc(f_ready, 1)

            def body(g, final):
                if not final:
                    forward(g + 1)
                pe.wait_ge(spec_ready, g * 2 + 2)
                for i in range(TPB):
                    pe.wait_ge(y_done, g * TPB + (i + 1))
                    for n in range(4):
                        last = nc.tensor.matmul(y_ps[i][:, :, :].rearrange("p b d -> p (b d)"),
                                                back[:, n, i * P:(i + 1) * P], spec[:, n // 2, n % 2, :],
                                                start=n == 0, stop=n == 3)
                    last.then_inc(y_ready, 1)

            pe.wait_ge(loaded, 32)
            forward(0)
            pairs(pe, body)

        @block.vector
        def _(dve):
            v = nc.vector
            dve.sem_inc(f_done, 2)
            dve.sem_inc(y_done, 2)
            dve.sem_inc(prod_free, 2)

            def multiply(g):
                for h in range(2):
                    dve.wait_ge(f_ready, g * 2 + h + 1)
                    dve.wait_ge(prod_free, g * 2 + h + 1)
                    for n, (part, kern) in enumerate(((0, KA), (1, KB), (0, KB), (1, KC))):
                        last = v.tensor_tensor(prod[:, h, n, :].rearrange("p (b d) -> p b d", b=2), f_ps[part][h][:, :, :],
                                               kern[:, h, :].unsqueeze(1).to_broadcast([P, 2, DIM]), ALU.mult)
                    last.then_inc(f_done, 1)

            def body(g, final):
                if not final:
                    multiply(g + 1)
                for i in range(TPB):
                    dve.wait_ge(y_ready, g * TPB + i + 1)
                    for b in range(2):
                        t = g * TPP + (b * TPB + i)
                        last = v.tensor_tensor(y[:, b * TPB + i, :].unsqueeze(1), y_ps[i][:, b, :].unsqueeze(1),
                                               FO[:, pieces(t), 0:DIM], ALU.mult)
                    last.then_inc(y_done, 1)
                dve.drain()
                tiles = pieces(g * TPP, TPP)
                v.tensor_tensor(y[:, :, :], y[:, :, :], FO[:, tiles, DIM:2 * DIM], ALU.add)
                dve.drain()
                v.tensor_tensor(X2[:, tiles, :], y[:, :, :], c.XN[:, tiles, :], ALU.add)
                dve.drain()
                for i in range(TPP):
                    t = pieces(g * TPP + i)
                    v.bn_stats(stats[:, t, :].rearrange("p a s -> p (a s)"), X2[:, t, :].rearrange("p a s -> p (a s)"))

            multiply(0)
            pairs(dve, body)
            dve.drain()

        @block.gpsimd
        def _(pool):
            def body(g, final):
                for h in range(2):
                    pool.wait_ge(f_done, g * 2 + h + 3)
                    pool.wait_ge(y_done, g * 2 + 2)
                    nc.gpsimd.tensor_tensor(spec[:, 0, h, :], prod[:, h, 0, :], prod[:, h, 1, :], ALU.subtract)
                    nc.gpsimd.tensor_tensor(spec[:, 1, h, :], prod[:, h, 2, :], prod[:, h, 3, :], ALU.add)\
                      .then_inc(spec_ready, 1)
                    pool.wait_ge(spec_ready, g * 2 + h + 1)
                    pool.sem_inc(prod_free, 1)

            pairs(pool, body)


def layer0_attention(nc, c, a, S):
    pre = "L0_xattn_"
    with ExitStack() as ctx:
        sb, ps, sem = sub_memory(nc, ctx, "l0i_")
        KA, KB, KC = (sb(f"kernel{n}", [P, 2, DIM]) for n in range(3))
        X2 = sb("x2", [P, TILES, DIM])
        X2_stats = sb("x2_stats", [P, TILES, 6])
        state_space_kernel(nc, c, a, KA, KB, KC, X2)
        with ExitStack() as inner:
            FO = inner.enter_context(nc.sbuf_tensor("film_out", [P, TILES, 2 * DIM], F32))
            film_attention(nc, c, a, X2, FO, S.table)
            convolve(nc, c, a, X2, X2_stats, FO, KA, KB, KC)
        dense_layer(nc, c, "l0x", 1024, a[pre + "W1"], a[pre + "W2"], func=ACT.Gelu, up_bias=a["L0_b1"],
                    down_bias=a[pre + "b2"], into=X2, stats=X2_stats,
                    normalised={"source": X2, "gain": a[pre + "g_ffn"], "shift": a[pre + "b_ffn"],
                                "stats": X2_stats})
        normalise(nc, c, X2, transposed=False, gain=a[pre + "g_norm_out"], shift=a[pre + "b_norm_out"], residual=0,
                  stats=X2_stats)


def build(nc, a, out):
    with ExitStack() as ctx:
        sb, ps, sem = sub_memory(nc, ctx)
        c = Core()
        c.transfers = {n: Transfers(nc, ctx, n) for n in ["zeros", "sent", "stored"] + [f"arrived{i}" for i in range(8)]}
        c.X = sb("residual", [P, TILES, DIM])
        c.XN = sb("normal", [P, TILES, DIM])
        c.XT = sb("normal_turned", [P, DK, TOKENS])
        c.ACC = sb("branch", [P, TILES, DIM])
        c.ident = sb("identity", [P, P])
        c.gate = sb("tanh_gates", [P, 8])
        c.headmask = sb("head_masks", [P, 16])
        c.above = sb("above", [P, P])
        c.ones = sb("ones", [P, P])
        c.stats = sb("row_stats", [P, TILES, 6])
        c.iota = sb("iota", [P, 40])
        c.chosen = sb("chosen", [P, 16, KT])
        c.share = sb("choice_share", [P, KT])
        S = Core()
        S.slot = sb("choice_slot", [P, KT], U32)
        S.owner = sb("tile_owner", [P, 32], I32)
        rows = slot_tiles(16) * SLOT_TILE
        S.table = nc.dram_tensor("slot_tokens", (rows, DIM), F32, kind="Internal").ap()
        S.results = nc.dram_tensor("slot_results", (rows, DIM), F32, kind="Internal").ap()
        layer0_attention(nc, c, a, S)
        normalise(nc, c, natural=c.XN, transposed=False)
        hash_router(nc, c)
        plan_slots(nc, c, 8, S)
        routed_experts(nc, c, "l0", 8, 1024, S, a["L0_ffn_W1"], a["L0_ffn_W2"], up_bias=a["L0_ffn_b1"],
                       down_bias=a["L0_ffn_b2"], send=True)
        collect(nc, c, 8, S, 4)
        layer1_attention(nc, c, a)
        normalise(nc, c, natural=c.XN)
        softmax_router(nc, c, "l1_router", a["L1_gate_T"], 8, eps=1e-5, gain=a["L1_gain"], shift=a["L1_shift"])
        plan_slots(nc, c, 8, S)
        shared = {"up": a["L1_ffn_sWu"], "down": a["L1_ffn_sWd"], "gate": a["L1_ffn_sWg"]}
        dense_layer(nc, c, "l1s", 512, **shared, blocks=range(0, 2), send=S)
        routed_experts(nc, c, "l1", 8, 512, S, a["L1_ffn_Wu"], a["L1_ffn_Wd"], gate=a["L1_ffn_Wg"])
        dense_layer(nc, c, "l1s", 512, **shared, blocks=range(2, 4), collected=(8, S, 5))
        narrow_attention(nc, c, a, 2)
        adapter_layer(nc, c, a)
        narrow_attention(nc, c, a, 3)
        normalise(nc, c, natural=c.XN)
        softmax_router(nc, c, "l3_router", a["L3_ffn_Wr"], 16)
        plan_slots(nc, c, 16, S)
        shared = {"up": a["L3_ffn_Su"], "down": a["L3_ffn_Sd"], "gate": a["L3_ffn_Sg"]}
        dense_layer(nc, c, "l3s", 256, **shared, blocks=range(0, 2), send=S)
        routed_experts(nc, c, "l3", 16, 128, S, a["L3_ffn_Wu"], a["L3_ffn_Wd"], gate=a["L3_ffn_Wg"])
        dense_layer(nc, c, "l3s", 256, **shared, blocks=range(2, 4), collected=(16, S, 7), out=out)


def constants():
    ident = np.eye(P, dtype=np.float32)
    p = np.arange(P)
    headmask = np.zeros((P, 16), np.float32)
    for h in range(4):
        headmask[:, h] = p // 32 == h
    for h in range(8):
        headmask[:, 4 + h] = p // 16 == h
    iota = np.tile(np.concatenate([np.arange(32), (np.arange(8) - 1) % 8]).astype(np.float32), (P, 1))
    above = np.triu(np.ones((P, P), np.float32), 1)
    ones = np.ones((P, P), np.float32)
    N = 2 * SEQ
    l = np.arange(SEQ)[:, None]
    k = np.arange(SEQ)[None, :]
    turn = 2 * np.pi * ((l * k) % N) / N
    re, im = np.cos(turn), -np.sin(turn)
    im[:, 0] = (-1.0) ** np.arange(SEQ)
    fwd = np.concatenate([re, im], 1)
    scale = np.full(SEQ, 2.0 / N)
    scale[0] = 1.0 / N
    back = np.concatenate([re * scale, im * scale], 1).T
    fwd, back = fwd.astype(np.float32), np.ascontiguousarray(back.astype(np.float32))
    steps = np.tile(np.concatenate([np.arange(16), 16 * np.arange(16)]).astype(np.float32), (P, 1))
    return {"ident": ident, "headmask": headmask, "iota": iota, "above": above, "ones": ones, "fwd": fwd, "back": back, "steps": steps}


def layout(inputs):
    a = {k: np.asarray(v) for k, v in inputs.items()}
    d = {k: np.ascontiguousarray(v) for k, v in a.items()}
    d["L0_xattn_mod_gate"] = d["L0_xattn_mod_gate"].reshape(1)
    d["context_T"] = np.ascontiguousarray(a["ctx_768"].transpose(0, 2, 1))
    d["L1_gate_T"] = np.ascontiguousarray(a["L1_ffn_gate_w"].T)
    d["L1_gain"] = np.ascontiguousarray(a["L1_ffn_ln_scale"].reshape(DK, P).T)
    d["L1_shift"] = np.ascontiguousarray(a["L1_ffn_ln_bias"].reshape(DK, P).T)
    for k in ("L1_ffn_ln_scale", "L1_ffn_ln_bias"):
        del d[k]
    d["L0_ffn_b1"] = np.ascontiguousarray(a["L0_ffn_b1"].reshape(8, 8, P).transpose(0, 2, 1))
    d["L0_b1"] = np.ascontiguousarray(a["L0_xattn_b1"].reshape(8, P).T)
    del d["L0_xattn_b1"]
    for n in ("bq", "bk"):
        d["L2_" + n] = np.ascontiguousarray(a["L2_xattn_" + n].reshape(DK, P).T)
        del d["L2_xattn_" + n]
    for n in ("bd1", "ba_down"):
        d["L2_" + n] = np.ascontiguousarray(a["L2_ffn_" + n].reshape(4, P).T)
        del d["L2_ffn_" + n]
    d["L2_bd2"] = np.ascontiguousarray(a["L2_ffn_bd2"].reshape(8, DK, P).transpose(2, 0, 1))
    del d["L2_ffn_bd2"]
    d["mask_BxS_bk0"] = np.ascontiguousarray(d["mask_BxS_bk0"].reshape(TILES, P).T)
    d["mask_BxS_bf1"] = np.ascontiguousarray(d["mask_BxS_bf1"].reshape(TILES, P).T)
    d["L3_Wq_T"] = np.ascontiguousarray(a["L3_xattn_Wq"].T)
    d["L3_Wkv_T"] = np.ascontiguousarray(a["L3_xattn_Wkv"].T)
    for k in ("A_re", "A_im", "C_re", "C_im"):
        v = a["L0_xattn_" + k]
        d["S_" + k] = np.ascontiguousarray(v.reshape(2, 128, 64).transpose(0, 2, 1).reshape(128, 128))
        del d["L0_xattn_" + k]
    for k in ("ctx_768", "L1_ffn_gate_w", "L3_xattn_Wq", "L3_xattn_Wkv"):
        del d[k]
    d.update(constants())
    return d


def kernel(**inputs):
    import concourse.bacc as bacc
    from concourse.bass_utils import run_bass_kernel_spmd

    nc = bacc.Bacc("TRN2", target_bir_lowering=False, num_devices=1)
    arrays = layout(inputs)
    args = {k: nc.dram_tensor("in_" + k, v.shape, mybir.dt.from_np(v.dtype), kind="ExternalInput").ap()
            for k, v in arrays.items()}
    out = nc.dram_tensor("out_0", (BATCH, SEQ, DIM), F32, kind="ExternalOutput").ap()
    build(nc, args, out)
    r = run_bass_kernel_spmd(nc, [{"in_" + k: v for k, v in arrays.items()}], core_ids=[0])
    return r.results[0]["out_0"]
```
